# Optimizing a Trainium2 kernel written in Bass

```python
import numpy as np
import jax
import jax.numpy as jnp

def _softmax(x, axis=-1):
    return jax.nn.softmax(x, axis=axis)

def _gelu(x):
    return jax.nn.gelu(x, approximate=True)

def _silu(x):
    return jax.nn.silu(x)

def _sigmoid(x):
    return jax.nn.sigmoid(x)

def _layernorm(x, axis=-1, eps=1e-05):
    m = jnp.mean(x, axis=axis, keepdims=True)
    v = jnp.var(x, axis=axis, keepdims=True)
    return (x - m) / jnp.sqrt(v + eps)

def _scatter_add(tgt, idx, src, axis=0):
    return tgt.at[idx].add(src)

def _segment_sum(src, seg, n):
    return jax.ops.segment_sum(src, seg, n)
kernel_name = 'mk_gnn_resnorm_d4_gnn_r32_697284'

def setup_inputs(seed: int=0):
    np.random.seed(seed)
    _w = jnp.asarray

    def _rec_inputs():
        import jax
        import jax.numpy as jnp
        _gk = jax.random.key(seed)
        x = -0.0003713 + 1 * jax.random.normal(jax.random.fold_in(_gk, 1), (3125, 128), jnp.float32)
        _s = jax.random.randint(jax.random.fold_in(_gk, 2), (50000,), 0, 3125, jnp.int32)
        _d = jax.random.randint(jax.random.fold_in(_gk, 3), (50000,), 0, 3125, jnp.int32)
        _loop = jnp.arange(3125, dtype=jnp.int32)
        src = jnp.concatenate([_s, _d, _loop])
        dst = jnp.concatenate([_d, _s, _loop])
        _o = jnp.argsort(dst, stable=True)
        src = src[_o]
        dst = dst[_o]
        edge_attr_4 = jax.random.uniform(jax.random.fold_in(_gk, 12), (103125, 4), jnp.float32, 0.0, 1)
        edge_weight = jax.random.uniform(jax.random.fold_in(_gk, 14), (103125,), jnp.float32, 0.0, 1)
        return (x, src, dst, edge_attr_4, edge_weight)
    x, src, dst, edge_attr_4, edge_weight = _rec_inputs()

    def _L0_gnn_setup():
        import jax, jax.numpy as jnp
        import numpy as np
        NEG_SLOPE = 0.2

        def gat_conv(x, src, dst, n, W, att_src, att_dst, bias, concat):
            H, C = att_src.shape
            xp = (x @ W).reshape(n, H, C)
            a_src = jnp.einsum('nhc,hc->nh', xp, att_src)
            a_dst = jnp.einsum('nhc,hc->nh', xp, att_dst)
            e = jax.nn.leaky_relu(a_src[src] + a_dst[dst], NEG_SLOPE)
            m = jax.ops.segment_max(e, dst, num_segments=n)
            ex = jnp.exp(e - m[dst])
            s = jax.ops.segment_sum(ex, dst, num_segments=n)
            alpha = ex / s[dst]
            out = jax.ops.segment_sum(xp[src] * alpha[:, :, None], dst, num_segments=n)
            out = out.reshape(n, H * C) if concat else out.mean(axis=1)
            return out + bias
        key = jax.random.key(seed)
        ks = jax.random.split(key, 16)
        N, E, D, H = (3125, 50000, 128, 4)
        HID, OUT = (128, 128)
        C = HID // H
        x = jax.random.normal(ks[0], (N, D), dtype=jnp.float32)
        edge_index = jax.random.randint(ks[1], (2, E), 0, N, dtype=jnp.int32)
        g = lambda k, shp: jax.random.normal(k, shp, dtype=jnp.float32) * 0.1
        return {'x': x, 'edge_index': edge_index, 'W1': g(ks[2], (D, H * C)), 'as1': g(ks[3], (H, C)), 'ad1': g(ks[4], (H, C)), 'b1': jnp.zeros((H * C,), jnp.float32), 'W2': g(ks[5], (HID, H * C)), 'as2': g(ks[6], (H, C)), 'ad2': g(ks[7], (H, C)), 'b2': jnp.zeros((H * C,), jnp.float32), 'W3': g(ks[8], (HID, H * OUT)), 'as3': g(ks[9], (H, OUT)), 'ad3': g(ks[10], (H, OUT)), 'b3': jnp.zeros((OUT,), jnp.float32)}
    _L0_gnn_all = _L0_gnn_setup()
    _L0_gnn_in = {k: v for k, v in _L0_gnn_all.items() if k in ('W1', 'as1', 'ad1', 'b1', 'W2', 'as2', 'ad2', 'b2', 'W3', 'as3', 'ad3', 'b3')}
    del _L0_gnn_all

    def _L1_gnn_setup():
        import jax, jax.numpy as jnp
        import numpy as np
        N_NODES = 3125
        N_EDGES = 25000
        HIDDEN = 128
        LN_EPS = 1e-05
        key = jax.random.key(seed)
        ks = jax.random.split(key, 8)
        h = jax.random.normal(ks[0], (N_NODES, HIDDEN), dtype=jnp.float32)
        src = jax.random.randint(ks[1], (N_EDGES,), 0, N_NODES, dtype=jnp.int64)
        dst = jax.random.randint(ks[2], (N_EDGES,), 0, N_NODES, dtype=jnp.int64)
        w1 = jax.random.normal(ks[3], (HIDDEN, 4 * HIDDEN), dtype=jnp.float32) * (1.0 / np.sqrt(HIDDEN))
        b1 = jnp.zeros((4 * HIDDEN,), dtype=jnp.float32)
        w2 = jax.random.normal(ks[4], (4 * HIDDEN, HIDDEN), dtype=jnp.float32) * (1.0 / np.sqrt(4 * HIDDEN))
        b2 = jnp.zeros((HIDDEN,), dtype=jnp.float32)
        gamma = jnp.ones((HIDDEN,), dtype=jnp.float32)
        beta = jnp.zeros((HIDDEN,), dtype=jnp.float32)
        return {'h': h, 'src': src, 'dst': dst, 'w1': w1, 'b1': b1, 'w2': w2, 'b2': b2, 'gamma': gamma, 'beta': beta}
    _L1_gnn_all = _L1_gnn_setup()
    _L1_gnn_in = {k: v for k, v in _L1_gnn_all.items() if k in ('w1', 'b1', 'w2', 'b2', 'gamma', 'beta')}
    del _L1_gnn_all

    def _L2_gnn_setup():
        import jax, jax.numpy as jnp
        import numpy as np
        N_NODES = 3125
        N_EDGES = 100000
        IN_FEAT = 128
        OUT_CH = 128
        K = 6
        key = jax.random.key(seed)
        k1, k2, k3, k4, k5, k6, k7 = jax.random.split(key, 7)
        nodes = jax.random.normal(k1, (N_NODES, IN_FEAT), dtype=jnp.float32)
        edges = jax.random.uniform(k2, (N_EDGES,), dtype=jnp.float32)
        senders = jax.random.randint(k3, (N_EDGES,), 0, N_NODES, dtype=jnp.int32)
        receivers = jax.random.randint(k4, (N_EDGES,), 0, N_NODES, dtype=jnp.int32)
        Wk = jax.random.normal(k5, (K, IN_FEAT, OUT_CH), dtype=jnp.float32) / jnp.sqrt(IN_FEAT)
        bk = jax.random.normal(k6, (K, OUT_CH), dtype=jnp.float32) * 0.01
        bias = jax.random.normal(k7, (OUT_CH,), dtype=jnp.float32) * 0.01
        return {'nodes': nodes, 'edges': edges, 'senders': senders, 'receivers': receivers, 'Wk': Wk, 'bk': bk, 'bias': bias}
    _L2_gnn_all = _L2_gnn_setup()
    _L2_gnn_in = {k: v for k, v in _L2_gnn_all.items() if k in ('Wk', 'bk', 'bias')}
    del _L2_gnn_all

    def _L3_gnn_setup():
        import jax, jax.numpy as jnp
        import numpy as np
        N_NODES = 3125
        N_EDGES = 50000
        HIDDEN = 128
        N_ETYPES = 4
        N_STEPS = 4

        def _gru_cell(x, h, W_ih, W_hh, b_ih, b_hh):
            gi = x @ W_ih.T + b_ih
            gh = h @ W_hh.T + b_hh
            ir, iz, inn = jnp.split(gi, 3, axis=1)
            hr, hz, hn = jnp.split(gh, 3, axis=1)
            r = jax.nn.sigmoid(ir + hr)
            z = jax.nn.sigmoid(iz + hz)
            n = jnp.tanh(inn + r * hn)
            return (1.0 - z) * n + z * h
        key = jax.random.key(seed)
        ks = jax.random.split(key, 10)
        s = 1.0 / np.sqrt(HIDDEN)
        node_feat = jax.random.normal(ks[0], (N_NODES, HIDDEN), dtype=jnp.float32)
        edge_index = jax.random.randint(ks[1], (2, N_EDGES), 0, N_NODES)
        edge_feat = jax.random.uniform(ks[2], (N_EDGES, N_ETYPES), dtype=jnp.float32)
        W_edge = jax.random.uniform(ks[3], (N_ETYPES, HIDDEN, HIDDEN), minval=-s, maxval=s, dtype=jnp.float32)
        b_edge = jax.random.uniform(ks[4], (N_ETYPES, HIDDEN), minval=-s, maxval=s, dtype=jnp.float32)
        W_ih = jax.random.uniform(ks[5], (3 * HIDDEN, HIDDEN), minval=-s, maxval=s, dtype=jnp.float32)
        W_hh = jax.random.uniform(ks[6], (3 * HIDDEN, HIDDEN), minval=-s, maxval=s, dtype=jnp.float32)
        b_ih = jax.random.uniform(ks[7], (3 * HIDDEN,), minval=-s, maxval=s, dtype=jnp.float32)
        b_hh = jax.random.uniform(ks[8], (3 * HIDDEN,), minval=-s, maxval=s, dtype=jnp.float32)
        return {'node_feat': node_feat, 'edge_index': edge_index, 'edge_feat': edge_feat, 'W_edge': W_edge, 'b_edge': b_edge, 'W_ih': W_ih, 'W_hh': W_hh, 'b_ih': b_ih, 'b_hh': b_hh}
    _L3_gnn_all = _L3_gnn_setup()
    _L3_gnn_in = {k: v for k, v in _L3_gnn_all.items() if k in ('W_edge', 'b_edge', 'W_ih', 'W_hh', 'b_ih', 'b_hh')}
    del _L3_gnn_all
    return {'x': x, 'src': src, 'dst': dst, 'edge_attr_4': edge_attr_4, 'edge_weight': edge_weight, 'L0_gnn_W1': _L0_gnn_in['W1'], 'L0_gnn_as1': _L0_gnn_in['as1'], 'L0_gnn_ad1': _L0_gnn_in['ad1'], 'L0_gnn_b1': _L0_gnn_in['b1'], 'L0_gnn_W2': _L0_gnn_in['W2'], 'L0_gnn_as2': _L0_gnn_in['as2'], 'L0_gnn_ad2': _L0_gnn_in['ad2'], 'L0_gnn_b2': _L0_gnn_in['b2'], 'L0_gnn_W3': _L0_gnn_in['W3'], 'L0_gnn_as3': _L0_gnn_in['as3'], 'L0_gnn_ad3': _L0_gnn_in['ad3'], 'L0_gnn_b3': _L0_gnn_in['b3'], 'L1_gnn_w1': _L1_gnn_in['w1'], 'L1_gnn_b1': _L1_gnn_in['b1'], 'L1_gnn_w2': _L1_gnn_in['w2'], 'L1_gnn_b2': _L1_gnn_in['b2'], 'L1_gnn_gamma': _L1_gnn_in['gamma'], 'L1_gnn_beta': _L1_gnn_in['beta'], 'L2_gnn_Wk': _L2_gnn_in['Wk'], 'L2_gnn_bk': _L2_gnn_in['bk'], 'L2_gnn_bias': _L2_gnn_in['bias'], 'L3_gnn_W_edge': _L3_gnn_in['W_edge'], 'L3_gnn_b_edge': _L3_gnn_in['b_edge'], 'L3_gnn_W_ih': _L3_gnn_in['W_ih'], 'L3_gnn_W_hh': _L3_gnn_in['W_hh'], 'L3_gnn_b_ih': _L3_gnn_in['b_ih'], 'L3_gnn_b_hh': _L3_gnn_in['b_hh']}

def reference(x, src, dst, edge_attr_4, edge_weight, L0_gnn_W1, L0_gnn_as1, L0_gnn_ad1, L0_gnn_b1, L0_gnn_W2, L0_gnn_as2, L0_gnn_ad2, L0_gnn_b2, L0_gnn_W3, L0_gnn_as3, L0_gnn_ad3, L0_gnn_b3, L1_gnn_w1, L1_gnn_b1, L1_gnn_w2, L1_gnn_b2, L1_gnn_gamma, L1_gnn_beta, L2_gnn_Wk, L2_gnn_bk, L2_gnn_bias, L3_gnn_W_edge, L3_gnn_b_edge, L3_gnn_W_ih, L3_gnn_W_hh, L3_gnn_b_ih, L3_gnn_b_hh):
    import jax
    import jax.numpy as jnp

    def _L0_gnn_ref(x, edge_index, W1, as1, ad1, b1, W2, as2, ad2, b2, W3, as3, ad3, b3):
        import jax, jax.numpy as jnp
        import numpy as np
        NEG_SLOPE = 0.2

        def gat_conv(x, src, dst, n, W, att_src, att_dst, bias, concat):
            H, C = att_src.shape
            xp = (x @ W).reshape(n, H, C)
            a_src = jnp.einsum('nhc,hc->nh', xp, att_src)
            a_dst = jnp.einsum('nhc,hc->nh', xp, att_dst)
            e = jax.nn.leaky_relu(a_src[src] + a_dst[dst], NEG_SLOPE)
            m = jax.ops.segment_max(e, dst, num_segments=n)
            ex = jnp.exp(e - m[dst])
            s = jax.ops.segment_sum(ex, dst, num_segments=n)
            alpha = ex / s[dst]
            out = jax.ops.segment_sum(xp[src] * alpha[:, :, None], dst, num_segments=n)
            out = out.reshape(n, H * C) if concat else out.mean(axis=1)
            return out + bias
        n = x.shape[0]
        loops = jnp.arange(n, dtype=edge_index.dtype)
        src = jnp.concatenate([edge_index[0], loops])
        dst = jnp.concatenate([edge_index[1], loops])
        h = jax.nn.relu(gat_conv(x, src, dst, n, W1, as1, ad1, b1, True))
        h = jax.nn.relu(gat_conv(h, src, dst, n, W2, as2, ad2, b2, True))
        return gat_conv(h, src, dst, n, W3, as3, ad3, b3, False)

    def _L1_gnn_ref(h, src, dst, w1, b1, w2, b2, gamma, beta):
        import jax, jax.numpy as jnp
        import numpy as np
        N_NODES = 3125
        N_EDGES = 25000
        HIDDEN = 128
        LN_EPS = 1e-05
        n = h.shape[0]
        u = jax.ops.segment_sum(h[src], dst, num_segments=n)
        hidden = jax.nn.relu(u @ w1 + b1)
        m = hidden @ w2 + b2 + h
        mean = jnp.mean(m, axis=-1, keepdims=True)
        var = jnp.mean(jnp.square(m - mean), axis=-1, keepdims=True)
        out = (m - mean) * jax.lax.rsqrt(var + LN_EPS) * gamma + beta
        return out

    def _L2_gnn_ref(nodes, edges, senders, receivers, Wk, bk, bias):
        import jax, jax.numpy as jnp
        import numpy as np
        N_NODES = 3125
        N_EDGES = 100000
        IN_FEAT = 128
        OUT_CH = 128
        K = 6
        N = nodes.shape[0]
        K_ = Wk.shape[0]
        deg = jax.ops.segment_sum(edges, senders, num_segments=N)
        lap_w = jnp.concatenate([-edges, deg])
        lap_recv = jnp.concatenate([receivers, jnp.arange(N, dtype=receivers.dtype)])
        lambda_max = 2.0 * lap_w.max()
        norm = 2.0 * lap_w / lambda_max
        scale = jax.ops.segment_sum(norm, lap_recv, num_segments=N)
        Tx0 = nodes
        out = Tx0 @ Wk[0] + bk[0]
        Tx1 = scale[:, None] * nodes
        out = out + Tx1 @ Wk[1] + bk[1]
        for k in range(2, K_):
            Tx2 = 2.0 * Tx1 - Tx0
            out = out + Tx2 @ Wk[k] + bk[k]
            Tx0, Tx1 = (Tx1, Tx2)
        return out + bias

    def _L3_gnn_ref(node_feat, edge_index, edge_feat, W_edge, b_edge, W_ih, W_hh, b_ih, b_hh):
        import jax, jax.numpy as jnp
        import numpy as np
        N_NODES = 3125
        N_EDGES = 50000
        HIDDEN = 128
        N_ETYPES = 4
        N_STEPS = 4

        def _gru_cell(x, h, W_ih, W_hh, b_ih, b_hh):
            gi = x @ W_ih.T + b_ih
            gh = h @ W_hh.T + b_hh
            ir, iz, inn = jnp.split(gi, 3, axis=1)
            hr, hz, hn = jnp.split(gh, 3, axis=1)
            r = jax.nn.sigmoid(ir + hr)
            z = jax.nn.sigmoid(iz + hz)
            n = jnp.tanh(inn + r * hn)
            return (1.0 - z) * n + z * h
        etypes = jnp.argmax(edge_feat, axis=1)
        src, dst = (edge_index[0], edge_index[1])
        N = node_feat.shape[0]
        h = node_feat
        for _ in range(N_STEPS):
            trans = jnp.einsum('nd,tod->tno', h, W_edge) + b_edge[:, None, :]
            msg = trans[etypes, src]
            a = jax.ops.segment_sum(msg, dst, num_segments=N)
            h = _gru_cell(a, h, W_ih, W_hh, b_ih, b_hh)
        return h
    edge_index = jnp.stack([src, dst])
    x = _layernorm(x + _L0_gnn_ref(x, edge_index, L0_gnn_W1, L0_gnn_as1, L0_gnn_ad1, L0_gnn_b1, L0_gnn_W2, L0_gnn_as2, L0_gnn_ad2, L0_gnn_b2, L0_gnn_W3, L0_gnn_as3, L0_gnn_ad3, L0_gnn_b3), axis=-1)
    x = _layernorm(x + _L1_gnn_ref(x, src, dst, L1_gnn_w1, L1_gnn_b1, L1_gnn_w2, L1_gnn_b2, L1_gnn_gamma, L1_gnn_beta), axis=-1)
    x = _layernorm(x + _L2_gnn_ref(x, edge_weight, src, dst, L2_gnn_Wk, L2_gnn_bk, L2_gnn_bias), axis=-1)
    x = _layernorm(x + _L3_gnn_ref(x, edge_index, edge_attr_4, L3_gnn_W_edge, L3_gnn_b_edge, L3_gnn_W_ih, L3_gnn_W_hh, L3_gnn_b_ih, L3_gnn_b_hh), axis=-1)
    return x

_drawn_inputs = setup_inputs


def setup_inputs(seed=0):
    import zlib

    import numpy as np

    out = dict(_drawn_inputs(seed))
    spreads = {'L0_gnn_b1': (0.0, 0.1),
     'L0_gnn_b2': (0.0, 0.1),
     'L0_gnn_b3': (0.0, 0.1),
     'L1_gnn_b1': (0.0, 0.38),
     'L1_gnn_b2': (0.0, 0.1),
     'L1_gnn_gamma': (1.0, 0.2),
     'L1_gnn_beta': (0.0, 0.1)}
    factors = {'L0_gnn_ad1': 200.0,
     'L0_gnn_as2': 8.0,
     'L0_gnn_ad2': 97.146,
     'L0_gnn_as3': 64.0,
     'L0_gnn_ad3': 200.0,
     'L2_gnn_bk': 5.074,
     'L2_gnn_bias': 8.0}
    for name, (base, spread) in spreads.items():
        noise = np.random.default_rng([zlib.crc32(name.encode()), seed]).standard_normal(out[name].shape)
        drawn = base * np.exp(spread * noise) if base else spread * noise
        out[name] = jnp.asarray(drawn.astype(out[name].dtype))
    for name, factor in factors.items():
        out[name] = (out[name] * factor).astype(out[name].dtype)
    return out
```

```python
from contextlib import ExitStack

import concourse.bass as bass
from concourse import mybir
from concourse.alu_op_type import AluOpType as ALU

F32 = mybir.dt.float32
F16 = mybir.dt.float16
BF16 = mybir.dt.bfloat16
I32 = mybir.dt.int32
ACT = mybir.ActivationFunctionType
AX = mybir.AxisListType.X

N = 3125
NB = 25
NP = NB * 128
E = 103125
EC = 808
EP = EC * 128
SLACK = 384
D = 128
H = 4
NT = 7
BIG = -3.0e38
SC = 4096.0
GR = 4
NXT = 49
GEN = [128, 128, 128, 128, 128, 128, 32]
LNEPS = 1e-5


def tile_w(j):
    return min(512, NP - 512 * j)


class Queues:

    def __init__(self, nc, ctx):
        self.nc, self.ctx = nc, ctx
        self.q = {e: [] for e in ("pe", "dve", "act", "pool", "sp")}
        self.n = {}
        self.sem = {}
        self.branch = False
        self.flag = {}
        for e in self.q:
            self._sem(e)

    def _sem(self, name):
        if name not in self.sem:
            self.sem[name] = self.ctx.enter_context(self.nc.semaphore(f"s_{name}"))
            self.n[name] = 0
        return self.sem[name]

    def wait(self, e, *tokens):
        for t in tokens:
            if t is None:
                continue
            if isinstance(t, list):
                self.wait(e, *t)
                continue
            s, v = self.sem[t[0]], t[1]
            self.q[e].append(lambda eng, s=s, v=v: eng.wait_ge(s, v))

    def op(self, e, fn, *tokens):
        self.wait(e, *tokens)
        name = "g_" + e if self.branch else e
        s = self._sem(name)
        self.n[name] += 1
        self.q[e].append(lambda eng: fn(eng).then_inc(s, 1))
        return (name, self.n[name])

    def raw(self, e, fn, *tokens):
        self.wait(e, *tokens)
        self.q[e].append(fn)

    def dma(self, e, sem, out, in_, *tokens):
        sem = "g_" + sem if self.branch else sem
        s = self._sem(sem)
        self.wait(e, *tokens)
        self.n[sem] += 16
        self.q[e].append(lambda eng: eng.dma_start(out, in_).then_inc(s, 16))
        return (sem, self.n[sem])

    def last(self, e):
        return (e, self.n[e])

    def barrier(self):
        now = [(k, v) for k, v in self.n.items() if v and k.startswith("g_") == self.branch]
        for e in self.q:
            self.wait(e, now)

    def general(self, build):
        now = [(k, v) for k, v in self.n.items() if v and not k.startswith("g_")]
        outer, self.q = self.q, {e: [] for e in self.q}
        for e in self.q:
            self.wait(e, now)
        self.branch = True
        build()
        self.barrier()
        self.branch = False
        inner, self.q = self.q, outer

        def branch(e):
            def emit(eng):
                with eng.If(self.flag[e] != 0):
                    for fn in inner[e]:
                        fn(eng)
            return emit

        for e in self.q:
            self.q[e].append(branch(e))

    def emit(self, e, eng):
        for fn in self.q[e]:
            fn(eng)


def gnn_kernel(nc, x, src, dst, bnd, attr, ew,
               W1, as1, ad1, b1, W2, as2, ad2, b2, W3, as3, ad3, b3,
               mw1, mb1, mw2, mb2, gamma, beta, Wk, bk, cbias,
               We, be, Wih, Whh, bih, bhh, out, dbg=None):
    ctx = ExitStack()
    P = Queues(nc, ctx)
    pe = lambda fn, *w: P.op("pe", fn, *w)
    dve = lambda fn, *w: P.op("dve", fn, *w)
    act = lambda fn, *w: P.op("act", fn, *w)
    pool = lambda fn, *w: P.op("pool", fn, *w)
    sp = lambda sem, o, i, *w: P.dma("sp", sem, o, i, *w)

    def sb(name, shape, dt=F32, c=ctx):
        return c.enter_context(nc.sbuf_tensor(name, shape, dt))

    def dram(name, shape, dt):
        return nc.dram_tensor(name, shape, dt).ap()

    AT = [dram(f"AT{j}", (128, 4 * NB, tile_w(j)), F16) for j in range(NT)]
    AC = dram("AC", (NB, 128, NP), F16)
    AT2 = [dram(f"ATL{j}", (128, 4 * NB, tile_w(j)), F16) for j in range(NT)]
    AC2 = dram("ACL", (NB, 128, NP), F16)
    MT = dram("MT", (NB, 128, NP), BF16)
    KT_D = dram("KTAB", (EP + SLACK, 3), F32)
    ROWS = dram("ROWS", (4, NP), F32)
    RROW = dram("RROW", (8, NP), F32)

    PS = ctx.enter_context(nc.psum_tensor("PS", [128, 8, 512], F32))

    ident = sb("ident", [128, 128])
    identh = sb("identh", [128, 128], F16)
    ones = sb("ones", [128, 128])
    io_i = sb("io_i", [128, 400], I32)
    ioh = sb("ioh", [128, 400], F16)
    iof = sb("iof", [128, 128])
    thr_i = sb("thr_i", [128, 8], I32)
    thr = sb("thr", [128, 8])
    thr100 = sb("thr100", [128, 8])
    thr400 = sb("thr400", [128, 8])
    epst = sb("epst", [128, 1])
    xr = sb("xr", [128, NB, D])
    net = sb("net", [128, 2 * NB])
    wmin = sb("wmin", [128, 4])
    flag = sb("flag", [128, 4])
    flag_i = sb("flag_i", [128, 1], I32)

    c0 = pool(lambda g: g.memset(ident[:], 1.0))
    t_id = pool(lambda g: g.affine_select(out=ident[:], in_=ident[:], compare_op=ALU.is_equal, fill=0.0,
                                          base=0, pattern=[[-1, 128]], channel_multiplier=1), c0)
    t_io = pool(lambda g: g.iota(io_i[:], pattern=[[1, 400]], base=0, channel_multiplier=0))
    t_th = pool(lambda g: g.iota(thr_i[:], pattern=[[512, 8]], base=0, channel_multiplier=4))
    t_on = dve(lambda v: v.memset(ones[:], 1.0))
    t_ep = dve(lambda v: v.memset(epst[:], LNEPS))
    t_idh = dve(lambda v: v.tensor_copy(identh[:], ident[:]), t_id)
    t_ioh = dve(lambda v: v.tensor_copy(ioh[:], io_i[:]), t_io)
    t_iof = dve(lambda v: v.tensor_copy(iof[:], io_i[:, 0:128]), t_io)
    t_thr = dve(lambda v: v.tensor_copy(thr[:], thr_i[:]), t_th)
    t_100 = dve(lambda v: v.tensor_scalar(thr100[:], thr[:], 25.0, None, ALU.mult), t_thr)
    t_400 = dve(lambda v: v.tensor_scalar(thr400[:], thr[:], 100.0, None, ALU.mult), t_thr)
    t_xz = dve(lambda v: v.memset(xr[:, NB - 1, :], 0.0))
    sp("x", xr[:, 0:NB - 1, :], x[0:128 * (NB - 1), :].rearrange("(b p) d -> p b d", p=128))
    t_x = sp("x", xr[0:N - 128 * (NB - 1), NB - 1, :], x[128 * (NB - 1):N, :], t_xz)

    pa = ExitStack()
    ewt = sb("ewt", [128, EC], F32, pa)
    hi_f = sb("hi_f", [128, EC], F32, pa)
    lo_f = sb("lo_f", [128, EC], F32, pa)
    dh_f = sb("dh_f", [128, EC], F32, pa)
    dl_f = sb("dl_f", [128, EC], F32, pa)
    KW = sb("KW", [128, NT, 2, 3, 128], F32, pa)
    pb = ExitStack()
    dst_i = sb("dst_i", [128, EC], I32, pb)
    src_i = sb("src_i", [128, EC], I32, pb)
    dsn_i = sb("dsn_i", [128, EC], I32, pb)
    att = sb("att", [128, EC, 4], F32, pb)
    mx = sb("mx", [128, EC], F32, pb)
    ne = sb("ne", [128, EC, 3], F32, pb)
    tt = sb("tt", [128, EC], F32, pb)
    di = sb("di", [128, EC], I32, pb)
    df = sb("df", [128, EC], F32, pb)
    k3 = sb("k3", [128, EC, 3], F32, pb)
    tail = sb("tail", [128, 3, 3], F32, pb)
    bb_i = sb("bb_i", [128, EC], I32, pb)
    bb = sb("bb", [128, EC], F32, pb)
    scr = sb("scr", [128, EC], F32, pb)
    nbt = sb("nbt", [128, 8], F32, pb)
    c0f = sb("c0f", [128, 8], F32, pb)
    c0i = sb("c0i", [128, 8], I32, pb)
    drow = sb("drow", [128, NT, 128], I32, pb)
    drf = sb("drf", [128, NT, 128], F32, pb)
    sf = sb("sf", [128, 8], F32, pb)
    si = sb("si", [128, 8], I32, pb)
    win = sb("win", [128, NT, 256, 3], F32, pb)
    win2 = sb("win2", [128, NT, 3, 256], F32, pb)

    t_bb = sp("bb", bb_i[:], bnd.partition_broadcast(128))
    t_d = sp("dst", dst_i[:], dst[0:EP].rearrange("(p i) -> p i", p=128))
    t_dn = sp("dsn", dsn_i[:], dst[1:EP + 1].rearrange("(p i) -> p i", p=128))
    t_s = sp("src", src_i[:], src.rearrange("(p i) -> p i", p=128))
    t_a = sp("att", att[:], attr.rearrange("(p i) t -> p i t", p=128))
    t_w = sp("ew", ewt[:], ew.rearrange("(p i) -> p i", p=128))

    t = dve(lambda v: v.tensor_copy(bb[:], bb_i[:]), t_bb)
    for k in range(NT):
        t = dve(lambda v, k=k: v.tensor_scalar(scr[:], bb[:], thr[:, k:k + 1], 0.0, ALU.is_lt, ALU.add,
                                               accum_out=nbt[:, k:k + 1]), t, t_thr)
    t = dve(lambda v: v.tensor_scalar(c0f[:, 0:NT], nbt[:, 0:NT], 1.0, 0.0, ALU.subtract, ALU.max), t)
    t_c0 = dve(lambda v: v.tensor_copy(c0i[:, 0:NT], c0f[:, 0:NT]), t)
    dst_r = dst[0:EP].rearrange("(c e) -> c e", e=128)

    def gather(sem, o, tab, ix, *w):
        s = P._sem(sem)
        P.wait("pool", *w)
        P.n[sem] += 16
        P.q["pool"].append(lambda g: g.indirect_dma_start(
            out=o, out_offset=None, in_=tab,
            in_offset=bass.IndirectOffsetOnAxis(ap=ix, axis=0)).then_inc(s, 16))
        return (sem, P.n[sem])

    for k in range(NT):
        t_g = gather("g0", drow[:, k, :], dst_r, c0i[:, k:k + 1], t_c0)

    t = dve(lambda v: v.tensor_scalar(di[:], src_i[:], 7, None, ALU.logical_shift_right), t_s)
    t_hi = dve(lambda v: v.tensor_copy(hi_f[:], di[:]), t)
    t = dve(lambda v: v.tensor_scalar(di[:], src_i[:], 127, None, ALU.bitwise_and), t_hi)
    t_lo = dve(lambda v: v.tensor_copy(lo_f[:], di[:]), t)
    t = dve(lambda v: v.tensor_scalar(di[:], dst_i[:], 7, None, ALU.logical_shift_right), t_d, t_lo)
    t_dh = dve(lambda v: v.tensor_copy(dh_f[:], di[:]), t)
    t = dve(lambda v: v.tensor_scalar(di[:], dst_i[:], 127, None, ALU.bitwise_and), t_dh)
    t_dl = dve(lambda v: v.tensor_copy(dl_f[:], di[:]), t)
    t_df = dve(lambda v: v.tensor_copy(df[:], dst_i[:]))
    t = dve(lambda v: v.tensor_reduce(mx[:], att[:], AX, ALU.max), t_a)
    for c in range(3):
        t_ne = dve(lambda v, c=c: v.tensor_tensor(ne[:, :, c], att[:, :, c], mx[:], ALU.not_equal), t)
    t = dve(lambda v: v.scalar_tensor_tensor(out=tt[:], in0=ne[:, :, 2], scalar=1.0, in1=ne[:, :, 1],
                                             op0=ALU.add, op1=ALU.mult), t_ne)
    t = dve(lambda v: v.scalar_tensor_tensor(out=tt[:], in0=tt[:], scalar=1.0, in1=ne[:, :, 0],
                                             op0=ALU.add, op1=ALU.mult), t)
    t = dve(lambda v: v.scalar_tensor_tensor(out=tt[:], in0=tt[:], scalar=25.0, in1=hi_f[:],
                                             op0=ALU.mult, op1=ALU.add), t, t_hi)
    t = dve(lambda v: v.scalar_tensor_tensor(out=k3[:, :, 0], in0=df[:], scalar=100.0, in1=tt[:],
                                             op0=ALU.mult, op1=ALU.add), t, t_df)
    dve(lambda v: v.scalar_tensor_tensor(out=k3[:, :, 1], in0=df[:], scalar=25.0, in1=hi_f[:],
                                         op0=ALU.mult, op1=ALU.add), t_df)
    t_k3 = dve(lambda v: v.tensor_copy(k3[:, :, 2], lo_f[:]), t_lo)
    t_tl = dve(lambda v: v.memset(tail[:], 1.0e6))
    sp("ktab", KT_D[0:EP, :].rearrange("(p i) c -> p (i c)", p=128), k3.rearrange("p i c -> p (i c)"), t_k3)
    t_kt = sp("ktab", KT_D[EP:EP + SLACK, :].rearrange("(p i) c -> p (i c)", p=128),
              tail.rearrange("p i c -> p (i c)"), t_tl)
    t_wm = dve(lambda v: v.tensor_reduce(wmin[:, 0:1], ewt[:], AX, ALU.min), t_w)

    t = dve(lambda v: v.tensor_copy(drf[:], drow[:]), t_g)
    for k in range(NT):
        t = dve(lambda v, k=k: v.tensor_scalar(scr[:, 0:128], drf[:, k, :], thr[:, k:k + 1], 0.0, ALU.is_lt,
                                               ALU.add, accum_out=nbt[:, k:k + 1]), t)
    t = dve(lambda v: v.scalar_tensor_tensor(out=sf[:, 0:NT], in0=c0f[:, 0:NT], scalar=128.0, in1=nbt[:, 0:NT],
                                             op0=ALU.mult, op1=ALU.add), t)
    t_si = dve(lambda v: v.tensor_copy(si[:, 0:NT], sf[:, 0:NT]), t)
    for k in range(NT):
        t_win = gather("g1", win[:, k].rearrange("p e c -> p (e c)"), KT_D, si[:, k:k + 1], t_si, t_kt)
    t = t_win
    for k in range(NT):
        dve(lambda v, k=k: v.tensor_scalar(win2[:, k, 0, :], win[:, k, :, 0], thr400[:, k:k + 1], None,
                                           ALU.subtract), t, t_400)
        dve(lambda v, k=k: v.tensor_scalar(win2[:, k, 1, :], win[:, k, :, 1], thr100[:, k:k + 1], None,
                                           ALU.subtract), t_100)
        t2 = dve(lambda v, k=k: v.tensor_copy(win2[:, k, 2, :], win[:, k, :, 2]))
    t = dve(lambda v: v.tensor_tensor(scr[:], dst_i[:], dsn_i[:], ALU.is_gt), t_dn)
    t = dve(lambda v: v.tensor_reduce(flag[:, 0:1], scr[:], AX, ALU.max), t)
    t1 = dve(lambda v: v.tensor_scalar(nbt[:, 0:NT], win2[:, :, 0, 255], 400.0, None, ALU.is_lt), t2)
    t1 = dve(lambda v: v.tensor_reduce(flag[:, 1:2], nbt[:, 0:NT], AX, ALU.max), t1)
    t = dve(lambda v: v.tensor_tensor(flag[:, 2:3], flag[:, 0:1], flag[:, 1:2], ALU.max), t, t1)
    t = pool(lambda g: g.partition_all_reduce(flag[:, 3:4], flag[:, 2:3], 128, bass.bass_isa.ReduceOp.max), t)
    t = dve(lambda v: v.tensor_copy(flag_i[:], flag[:, 3:4]), t)

    def load_flag(e):
        def emit(eng):
            P.flag[e] = eng.value_load(flag_i[0:1, 0:1], min_val=0, max_val=1)
        return emit

    for eng_name in P.q:
        P.raw(eng_name, load_flag(eng_name), t)
    nev = {}
    for i, (k, h) in enumerate((k, h) for k in range(NT) for h in range(2)):
        b = i % 4
        for a in range(3):
            tp = pe(lambda p, k=k, h=h, a=a, b=b: p.transpose(
                PS[:, b, 128 * a:128 * a + 128], win2[:, k, a, 128 * h:128 * h + 128], ident[:]),
                t2, t_id, nev.get(i - 4) if a == 0 else None)
        nev[i] = act(lambda s, k=k, h=h, b=b: s.copy(
            KW[:, k, h].rearrange("p a g -> p (a g)"), PS[:, b, 0:384]), tp)
    P.barrier()
    pb.close()

    pc = ExitStack()
    ST = [sb(f"ST{i}", [128, 4 * NB, 256], F16, pc) for i in range(2)]
    SCt = [sb(f"SC{i}", [128, NB, 256], F16, pc) for i in range(2)]
    OM = [sb(f"OM{i}", [128, 500], F16, pc) for i in range(4)]
    OL = [sb(f"OL{i}", [128, 128], F16, pc) for i in range(4)]
    WS = [sb(f"WS{i}", [128, 2, 128], F32, pc) for i in range(4)]
    WH = [sb(f"WH{i}", [128, 2, NB], F32, pc) for i in range(4)]
    MK = [sb(f"MK{i}", [128, NP], BF16, pc) for i in range(2)]
    PST = PS[:, 4:8, :].bitcast(F16)

    n_ch = 0
    t_ch = {}
    t_pc = {}
    n_wc = 0
    t_wp = {}
    t_we = {}
    ev = {}
    st_dma = {}
    mk_n = 0
    mk_dma = {}
    mk_ev = None
    NG = NP // GR

    def deg_col(i):
        sl = i % 4
        w0 = t_we.get(i - 4)
        pool(lambda g: g.tensor_scalar(WS[sl][:, 0, :], iof[:], lo_f[:, i:i + 1], None, ALU.is_equal), w0)
        pool(lambda g: g.tensor_scalar(WS[sl][:, 1, :], iof[:], dl_f[:, i:i + 1], None, ALU.is_equal))
        pool(lambda g: g.tensor_scalar(WH[sl][:, 0, :], iof[:, 0:NB], hi_f[:, i:i + 1], ewt[:, i:i + 1],
                                       ALU.is_equal, ALU.mult))
        t = pool(lambda g: g.tensor_scalar(WH[sl][:, 1, :], iof[:, 0:NB], dh_f[:, i:i + 1], ewt[:, i:i + 1],
                                           ALU.is_equal, ALU.mult))
        pe(lambda p: p.matmul(PS[:, 3, 0:NB], WS[sl][:, 0, :], WH[sl][:, 0, :], start=(i == 0), stop=False,
                              skip_group_check=True), t)
        t_we[i] = pe(lambda p: p.matmul(PS[:, 3, NB:2 * NB], WS[sl][:, 1, :], WH[sl][:, 1, :], start=False,
                                        stop=(i == EC - 1), skip_group_check=True))

    for g in range(NG):
        k, gl = divmod(g, 128)
        hf = g // 64
        s2 = hf % 2
        b = g % 3
        for h in range(2):
            sl = n_ch % 4
            wfree = t_pc.get(n_ch - 4)
            dve(lambda v, sl=sl, k=k, h=h, gl=gl: v.tensor_scalar(
                OM[sl][:, 0:400], ioh[:, 0:400], KW[:, k, h, 0, gl:gl + 1], None, ALU.is_equal), wfree)
            dve(lambda v, sl=sl, k=k, h=h, gl=gl: v.tensor_scalar(
                OM[sl][:, 400:500], ioh[:, 0:100], KW[:, k, h, 1, gl:gl + 1], None, ALU.is_equal))
            t = dve(lambda v, sl=sl, k=k, h=h, gl=gl: v.tensor_scalar(
                OL[sl][:], ioh[:, 0:128], KW[:, k, h, 2, gl:gl + 1], None, ALU.is_equal))
            t_pc[n_ch] = pe(lambda p, sl=sl, b=b, h=h: p.matmul(
                PS[:, b, 0:500], OL[sl][:], OM[sl][:], start=(h == 0), stop=(h == 1)),
                t, ev.get(g - 3) if h == 0 else None)
            n_ch += 1
        col = 4 * (g % 64)
        w = [t_pc[n_ch - 1]]
        if g % 64 == 0:
            w.append(st_dma.get(hf - 2))
        act(lambda s, s2=s2, b=b, col=col: s.copy(
            ST[s2][:, :, col:col + 4], PS[:, b, 0:400].rearrange("p (d c) -> p c d", d=4)), *w)
        ev[g] = act(lambda s, s2=s2, b=b, col=col: s.copy(
            SCt[s2][:, :, col:col + 4], PS[:, b, 400:500].rearrange("p (d c) -> p c d", d=4)))
        deg_col(g)
        if g == NG - 1:
            for i in range(NG, EC):
                deg_col(i)
        if g % 64 == 63 or g == NG - 1:
            wd = 256 if g % 64 == 63 else 128
            n0 = 256 * hf
            tA = sp(f"st{s2}", AT[n0 // 512][:, :, n0 % 512:n0 % 512 + wd], ST[s2][:, :, 0:wd], ev[g])
            td = None
            for db in range(wd // 128):
                blk = 2 * hf + db
                c = slice(128 * db, 128 * db + 128)
                td = dve(lambda v, s2=s2, blk=blk, c=c: v.tensor_tensor(
                    SCt[s2][:, blk, c], SCt[s2][:, blk, c], identh[:], ALU.add), ev[g])
            tC = sp(f"sc{s2}", AC[:, :, n0:n0 + wd].rearrange("h l d -> l h d"), SCt[s2][:, :, 0:wd], td)
            tq = None
            for db in range(wd // 128):
                blk = 2 * hf + db
                for c in range(NB):
                    tq = pe(lambda p, c=c, db=db, s2=s2: p.transpose(
                        PST[:, c // 8, 128 * (c % 8):128 * (c % 8) + 128],
                        SCt[s2][:, c, 128 * db:128 * db + 128], identh[:]), td, mk_ev)
                mk_ev = dve(lambda v, m=mk_n % 2: v.tensor_scalar(
                    MK[m][:], PST.rearrange("p b c -> p (b c)")[:, 0:NP], 0.0, BIG, ALU.is_equal, ALU.mult),
                    tq, mk_dma.get(mk_n - 2))
                mk_dma[mk_n] = sp(f"mk{mk_n % 2}", MT[blk], MK[mk_n % 2][:], mk_ev)
                mk_n += 1
            st_dma[hf] = [tA, tC, tq]
    t_net = dve(lambda v: v.tensor_copy(net[:], PS[:, 3, 0:2 * NB]), t_we[EC - 1])
    P.barrier()
    pc.close()
    pa.close()

    def general_build():
        q = ExitStack()
        nx = EC + NB
        kall = sb("kall", [128, nx, 3], F32, q)
        kxi = sb("kxi", [128, 2, NB], I32, q)
        gbk = sb("gbk", [128, 3], F32, q)
        gst = sb("gst", [128, 3], F32, q)
        KD = sb("KD", [128, NXT, 3], F32, q)
        OG = sb("OG", [128, NXT, 628], F16, q)
        tot = sb("tot", [128, 500], F32, q)
        part = sb("part", [128, 2, 500], F16, q)
        SG = sb("SG", [128, NB, 128], F16, q)
        MG = sb("MG", [128, NP], BF16, q)
        t = sp("kall", kall[:, 0:EC, :].rearrange("p i c -> p (i c)"), KT_D[0:EP, :].rearrange("(p i) c -> p (i c)", p=128))
        pool(lambda g: g.iota(kxi[:, 0, :], pattern=[[128 * 25 + 1, NB]], base=0, channel_multiplier=25))
        t1 = pool(lambda g: g.iota(kxi[:, 1, :], pattern=[[0, NB]], base=0, channel_multiplier=1))
        dve(lambda v: v.memset(kall[:, EC:nx, 0], 1.0e6))
        dve(lambda v: v.tensor_copy(kall[:, EC:nx, 1], kxi[:, 0, :]), t1)
        dve(lambda v: v.tensor_copy(kall[:, EC:nx, 2], kxi[:, 1, :]))
        dve(lambda v: v.memset(gst[:], 0.0))
        dve(lambda v: v.memset(gbk[:], 0.0))
        P.barrier()
        dve(lambda v: v.memset(gst[:, 0:1], 400.0))
        dve(lambda v: v.memset(gst[:, 1:2], 100.0))
        P.barrier()
        dc = lambda a: a.rearrange("p (c d) -> p d c", d=GR)
        for j in range(NT):
            if not GEN[j]:
                continue
            s_ohm, s_mm, s_cut, s_st = (P._sem(f"g_{n}{j}") for n in ("ohm", "mm", "cut", "st"))
            dve(lambda v, j=j: v.memset(gbk[:, 0:1], 400.0 * 128 * j))
            dve(lambda v, j=j: v.memset(gbk[:, 1:2], 100.0 * 128 * j))

            def hot(v, j=j, s_ohm=s_ohm, s_mm=s_mm, s_cut=s_cut, s_st=s_st):
                with v.Fori(0, GEN[j]) as g:
                    v.memset(tot[:], 0.0)
                    with v.Fori(0, nx // NXT) as b:
                        v.drain()
                        v.tensor_tensor(KD[:], kall[:, bass.ds(b * NXT, NXT), :],
                                        gbk[:].unsqueeze(1).broadcast_to([128, NXT, 3]), ALU.subtract)
                        v.drain()
                        for c in range(NXT):
                            v.tensor_scalar(OG[:, c, 0:400], ioh[:, 0:400], KD[:, c, 0:1], None, ALU.is_equal)
                            v.tensor_scalar(OG[:, c, 400:500], ioh[:, 0:100], KD[:, c, 1:2], None, ALU.is_equal)
                            v.tensor_scalar(OG[:, c, 500:628], ioh[:, 0:128], KD[:, c, 2:3], None, ALU.is_equal)
                        v.drain()
                        v.sem_inc(s_ohm, 1)
                        v.wait_ge(s_mm, g * (nx // NXT) + b + 1)
                        v.tensor_tensor(tot[:], tot[:], PS[:, 0, 0:500], ALU.add)
                    v.drain()
                    v.wait_ge(s_st, g * 64)
                    v.tensor_copy(dc(part[:, 0, 0:400]), tot[:, 0:400].rearrange("p (d c) -> p d c", d=GR))
                    v.tensor_copy(dc(part[:, 0, 400:500]), tot[:, 400:500].rearrange("p (d c) -> p d c", d=GR))
                    v.drain()
                    for a, b in ((0, 400), (400, 500)):
                        v.tensor_tensor(dc(part[:, 1, a:b]), tot[:, a:b].rearrange("p (d c) -> p d c", d=GR),
                                        dc(part[:, 0, a:b]), ALU.subtract)
                    v.tensor_tensor(gbk[:], gbk[:], gst[:], ALU.add)
                    v.drain()
                    v.sem_inc(s_cut, 1)

            def count(p, j=j, s_ohm=s_ohm, s_mm=s_mm):
                with p.Fori(0, GEN[j]) as g:
                    with p.Fori(0, nx // NXT) as b:
                        p.wait_ge(s_ohm, g * (nx // NXT) + b + 1)
                        for c in range(NXT):
                            mm = p.matmul(PS[:, 0, 0:500], OG[:, c, 500:628], OG[:, c, 0:500],
                                          start=(c == 0), stop=(c == NXT - 1))
                        mm.then_inc(s_mm, 1)

            def store(a, j=j, s_cut=s_cut, s_st=s_st):
                with a.Fori(0, GEN[j]) as g:
                    a.wait_ge(s_cut, g + 1)
                    for i, (ta, tc) in enumerate(((AT[j], AC), (AT2[j], AC2))):
                        a.dma_start(ta[:, :, bass.ds(g * GR, GR)],
                                    part[:, i, 0:400].rearrange("p (c d) -> p c d", d=GR)).then_inc(s_st, 16)
                        a.dma_start(tc[:, :, bass.ds(g * GR + 512 * j, GR)].rearrange("h l d -> l h d"),
                                    part[:, i, 400:500].rearrange("p (c d) -> p c d", d=GR)).then_inc(s_st, 16)
                    a.wait_ge(s_st, g * 64 + 64)

            P.barrier()
            P.raw("dve", hot)
            P.raw("pe", count)
            P.raw("act", store)
            s_j = P._sem(f"g_end{j}")
            P.n[f"g_end{j}"] += 1
            P.raw("act", lambda a, s_j=s_j: a.sem_inc(s_j, 1))
            P.barrier()
        t3 = t4 = None
        for blk in range(NB):
            t = sp("sg", SG[:], AC[:, :, 128 * blk:128 * blk + 128].rearrange("h l d -> l h d"), t3)
            for c in range(NB):
                t2 = pe(lambda p, c=c: p.transpose(
                    PST[:, c // 8, 128 * (c % 8):128 * (c % 8) + 128], SG[:, c, :], identh[:]), t, t3)
            t3 = dve(lambda v: v.tensor_scalar(MG[:], PST.rearrange("p b c -> p (b c)")[:, 0:NP], 0.0, BIG,
                                               ALU.is_equal, ALU.mult), t2, t4)
            t4 = sp("mg", MT[blk], MG[:], t3)
        q.close()

    P.general(general_build)
    hT = sb("hT", [128, NP])

    def to_cols(rows, dst_T, *w):
        last = {}
        for j in range(NT):
            for q in range(tile_w(j) // 128):
                t = pe(lambda p, j=j, q=q: p.transpose(PS[:, j % 4, 128 * q:128 * q + 128],
                                                       rows[:, 4 * j + q, :], ident[:]),
                       *w, last.get(j - 4))
            last[j] = act(lambda s, j=j: s.copy(dst_T[:, 512 * j:512 * j + tile_w(j)],
                                                PS[:, j % 4, 0:tile_w(j)]), t)
        return last[NT - 1]

    def layernorm(rows, t1, t2, *w):
        m, r = t2[:, 0, :], t2[:, 1, :]
        bc = lambda a: a.unsqueeze(2).broadcast_to([128, NB, D])
        t = dve(lambda v: v.tensor_reduce(m, rows[:], AX, ALU.add), *w)
        t = dve(lambda v: v.tensor_scalar(m, m, 1.0 / D, None, ALU.mult), t)
        t = dve(lambda v: v.tensor_tensor(rows[:], rows[:], bc(m), ALU.subtract), t)
        t = act(lambda s: s.square(t1[:], rows[:]), t)
        t = dve(lambda v: v.tensor_reduce(r, t1[:], AX, ALU.add), t)
        t = act(lambda s: s.activation(r, r, ACT.Sqrt, bias=epst[:], scale=1.0 / D), t)
        t = dve(lambda v: v.reciprocal(r, r), t)
        return dve(lambda v: v.tensor_tensor(rows[:], rows[:], bc(r), ALU.mult), t)

    to_cols(xr, hT)
    P.barrier()
    HALF = [(0, 1536), (1536, 1664)]

    def gat(l, W, a_s, a_d, bias):
        last = l == 3
        C = 128 if last else 32
        F = H * C
        g = ExitStack()
        Wt = sb(f"W{l}", [128, F], F32, g)
        ab = sb(f"ab{l}", [128, 2, F], F32, g)
        tmp = sb(f"tmp{l}", [128, F], F32, g)
        wa = sb(f"wa{l}", [128, 8], F32, g)
        bcol = sb(f"bc{l}", [128, 1], F32, g)
        acol = sb(f"ac{l}", [128, NB, 8], F32, g)
        a2 = sb(f"a2{l}", [128, NB, 8], F32, g)
        xp = sb(f"xp{l}", [128, NB, 4, 128 if last else 33], F32, g)
        amax = sb(f"am{l}", [128, NB, 4], F32, g)
        Rc = sb(f"Rc{l}", [128, NB, 8], F32, g)
        rrow = sb(f"rr{l}", [8, NP], F32, g)

        sp("gw", Wt[:], W)
        sp("gw", bcol[:], bias.rearrange("(p o) -> p o", o=1))
        sp("gw", ab[:, 0, :], a_s.rearrange("h c -> (h c)").partition_broadcast(128))
        t = sp("gw", ab[:, 1, :], a_d.rearrange("h c -> (h c)").partition_broadcast(128))
        for s in range(2):
            t1 = dve(lambda v, s=s: v.tensor_tensor(tmp[:], Wt[:], ab[:, s, :], ALU.mult), t)
            t = dve(lambda v, s=s: v.tensor_reduce(wa[:, 4 * s:4 * s + 4],
                                                   tmp.rearrange("p (h c) -> p h c", h=H), AX, ALU.add), t1)
        t_wa = t
        e = {}
        for j in range(NT):
            wd = tile_w(j)
            t = pe(lambda p, j=j, wd=wd: p.matmul(PS[0:4, j % 2, 0:wd], wa[:, 0:4], hT[:, 512 * j:512 * j + wd],
                                                  start=True, stop=True), t_wa, e.get(j - 2))
            e[j] = act(lambda s, j=j, wd=wd: s.copy(rrow[0:4, 512 * j:512 * j + wd], PS[0:4, j % 2, 0:wd]), t)
        t_rows = sp("rows", ROWS, rrow[0:4, :], e[NT - 1])
        for k in range(NB):
            t = pe(lambda p, k=k: p.matmul(PS[:, 2, 8 * k:8 * k + 8], hT[:, 128 * k:128 * k + 128], wa[:],
                                           start=True, stop=True), t_wa)
        t_ac = act(lambda s: s.copy(acol.rearrange("p k h -> p (k h)"), PS[:, 2, 0:8 * NB]), t)
        t_a2 = dve(lambda v: v.tensor_scalar(a2[:], acol[:], 0.2, None, ALU.mult), t_ac)
        e = {}
        if not last:
            t_one = pool(lambda q: q.memset(xp[:, :, :, 32:33], 1.0))
            for j in range(NT):
                nb = tile_w(j) // 128
                for q in range(nb):
                    t = pe(lambda p, j=j, q=q: p.matmul(
                        PS[:, 3 + j % 2, 128 * q:128 * q + 128],
                        hT[:, 512 * j + 128 * q:512 * j + 128 * q + 128], Wt[:], start=True, stop=True),
                        t_wa, e.get(j - 2))
                e[j] = act(lambda s, j=j, nb=nb: s.copy(
                    xp[:, 4 * j:4 * j + nb, :, 0:32],
                    PS[:, 3 + j % 2, 0:128 * nb].rearrange("p (k h c) -> p k h c", k=nb, h=4)), t)
        else:
            for k in range(NB):
                t = pe(lambda p, k=k: p.matmul(PS[:, 3 + k % 2, :], hT[:, 128 * k:128 * k + 128], Wt[:],
                                               start=True, stop=True), t_wa, e.get(k - 2))
                e[k] = act(lambda s, k=k: s.copy(xp[:, k].rearrange("p h c -> p (h c)"), PS[:, 3 + k % 2, :]), t)
        m = ExitStack()
        arow = sb(f"ar{l}", [128, 4, NP], F32, m)
        MKb = [sb(f"mb{l}{i}", [128, NP], BF16, m) for i in range(3)]
        junk = sb(f"jk{l}", [128, NP], F32, m)
        for h in range(H):
            t_ar = sp("arow", arow[:, h, :], ROWS[h].partition_broadcast(128), t_rows)
        free = {}
        for k in range(NB):
            t_m = sp(f"mkl{k % 3}", MKb[k % 3][:], MT[k], free.get(k - 3))
            for h in range(H):
                t = dve(lambda v, k=k, h=h: v.tensor_tensor_reduce(
                    junk[:], MKb[k % 3][:], arow[:, h, :], 1.0, BIG, ALU.add, ALU.max,
                    amax[:, k, h:h + 1]), t_m, t_ar, t if h or k else None)
            free[k] = t
        t_am = t
        bd = acol[:, :, 4:8]
        t = dve(lambda v: v.tensor_tensor(amax[:], amax[:], bd, ALU.add), t_am, t_ac)
        t = dve(lambda v: v.scalar_tensor_tensor(out=amax[:], in0=amax[:], scalar=0.2, in1=amax[:],
                                                 op0=ALU.mult, op1=ALU.max), t)
        dve(lambda v: v.tensor_tensor(Rc[:, :, 0:4], bd, amax[:], ALU.subtract), t)
        t_rc = dve(lambda v: v.tensor_tensor(Rc[:, :, 4:8], a2[:, :, 4:8], amax[:], ALU.subtract), t)
        e = {}
        for j in range(NT):
            wd = tile_w(j)
            for q in range(wd // 128):
                t = pe(lambda p, j=j, q=q: p.transpose(PS[0:8, j % 2, 128 * q:128 * q + 128], Rc[:, 4 * j + q, :],
                                                       ident[:]), t_rc, e.get(j - 2))
            e[j] = act(lambda s, j=j, wd=wd: s.copy(rrow[:, 512 * j:512 * j + wd], PS[0:8, j % 2, 0:wd]),
                       t, t_rows)
        t_rr = sp("rrow", RROW, rrow[:], e[NT - 1])
        P.barrier()
        m.close()

        Rb = [sb(f"Rb{l}{i}", [128, 2, 1664], F32, g) for i in range(2)]
        E1 = [sb(f"E1{l}{i}", [128, 1664], F32, g) for i in range(3)]
        E2 = [sb(f"E2{l}{i}", [128, 1664], F32, g) for i in range(2)]
        Cb = [sb(f"Cb{l}{i}", [128, 1664], F16, g) for i in range(3)]
        if last:
            acc = sb("acc", [128, 1664], F32, g)
            rec = sb("rec", [128, 512], F32, g)
            tm2 = sb("tm2", [128, 512], F32, g)
            oT = sb("oT", [128, NP], F32, g)
        else:
            nsb = sb(f"ns{l}", [33, 1664], F32, g)
            rc = sb(f"rc{l}", [128, 13], F32, g)
            hr = sb(f"hr{l}", [128, NB, 4, 32], F32, g)
        n = 0
        t_p = {}
        t_mx = {}
        t_c = {}
        ps_free = [None, None]
        rb_free = [None, None]
        acc_free = None
        ns_free = None
        rc_free = None
        rec_free = None
        for h in range(H):
            for half, (o, wd) in enumerate(HALF):
                pb0 = 3 * half
                it = 2 * h + half
                rb = Rb[it % 2]
                sp(f"rb{it % 2}", rb[:, 0, 0:wd], RROW[h, o:o + wd].partition_broadcast(128), t_rr, rb_free[it % 2])
                t_rb = sp(f"rb{it % 2}", rb[:, 1, 0:wd], RROW[4 + h, o:o + wd].partition_broadcast(128))
                for k in range(NB):
                    e1, e2, cb = E1[n % 3], E2[n % 2], Cb[n % 3]
                    t_c[n] = sp(f"cb{n % 3}", cb[:, 0:wd], AC[k, :, o:o + wd],
                                t_mx.get((n - 3, "p")))
                    ta = act(lambda s, e1=e1, rb=rb, k=k, h=h, wd=wd: s.activation(
                        e1[:, 0:wd], rb[:, 0, 0:wd], ACT.Exp, bias=acol[:, k, h:h + 1]),
                        t_rb, t_p.get(n - 3))
                    tb = act(lambda s, e2=e2, rb=rb, k=k, h=h, wd=wd: s.activation(
                        e2[:, 0:wd], rb[:, 1, 0:wd], ACT.Exp, bias=a2[:, k, h:h + 1]),
                        t_mx.get((n - 2, "m")), t_a2)
                    tm = dve(lambda v, e1=e1, e2=e2, wd=wd: v.tensor_tensor(
                        e1[:, 0:wd], e1[:, 0:wd], e2[:, 0:wd], ALU.max), tb)
                    t_mx[(n, "m")] = tm
                    tq = dve(lambda v, e1=e1, cb=cb, wd=wd: v.scalar_tensor_tensor(
                        out=e1[:, 0:wd], in0=e1[:, 0:wd], scalar=1.0, in1=cb[:, 0:wd],
                        op0=ALU.min, op1=ALU.mult), tm, t_c[n])
                    t_mx[(n, "p")] = tq
                    M = 128 if last else 33
                    for c in range(0, wd, 512):
                        cw = min(512, wd - c)
                        tz = pe(lambda p, e1=e1, k=k, h=h, c=c, cw=cw, M=M, pb0=pb0: p.matmul(
                            PS[0:M, pb0 + c // 512, 0:cw], xp[:, k, h, :], e1[:, c:c + cw],
                            start=(k == 0), stop=(k == NB - 1)), tq, ps_free[half] if k == 0 else None)
                    if last:
                        if k == 0:
                            ty = pool(lambda q, e1=e1, wd=wd: q.tensor_copy(acc[:, 0:wd], e1[:, 0:wd]),
                                      tq, acc_free)
                        else:
                            ty = pool(lambda q, e1=e1, wd=wd: q.tensor_tensor(
                                acc[:, 0:wd], acc[:, 0:wd], e1[:, 0:wd], ALU.add), tq, ty)
                        t_p[n] = [tz, ty]
                    else:
                        t_p[n] = tz
                    n += 1

                def rest(h=h, o=o, wd=wd, rb=rb, pb0=pb0, M=M):
                    e1, e2, cb = E1[0], E2[0], Cb[0]
                    td = None
                    for k in range(NB):
                        tc = sp("cb", cb[:, 0:wd], AC2[k, :, o:o + wd], td)
                        act(lambda s, k=k: s.activation(e1[:, 0:wd], rb[:, 0, 0:wd], ACT.Exp,
                                                        bias=acol[:, k, h:h + 1]), td)
                        tb = act(lambda s, k=k: s.activation(e2[:, 0:wd], rb[:, 1, 0:wd], ACT.Exp,
                                                             bias=a2[:, k, h:h + 1]))
                        tm = dve(lambda v: v.tensor_tensor(e1[:, 0:wd], e1[:, 0:wd], e2[:, 0:wd], ALU.max), tb)
                        tq = dve(lambda v: v.scalar_tensor_tensor(
                            out=e1[:, 0:wd], in0=e1[:, 0:wd], scalar=1.0, in1=cb[:, 0:wd],
                            op0=ALU.min, op1=ALU.mult), tm, tc)
                        for c in range(0, wd, 512):
                            cw = min(512, wd - c)
                            tz = pe(lambda p, k=k, c=c, cw=cw: p.matmul(
                                PS[0:M, pb0 + c // 512, 0:cw], xp[:, k, h, :], e1[:, c:c + cw],
                                start=False, stop=True, skip_group_check=True), tq)
                        td = [tz]
                        if last:
                            td.append(pool(lambda q: q.tensor_tensor(acc[:, 0:wd], acc[:, 0:wd], e1[:, 0:wd],
                                                                     ALU.add), tq))

                P.general(rest)
                rb_free[it % 2] = tb
                if not last:
                    nb = wd // 128
                    tn = None
                    for c in range(0, wd, 512):
                        cw = min(512, wd - c)
                        tn = act(lambda s, c=c, cw=cw, pb0=pb0: s.copy(
                            nsb[:, c:c + cw], PS[0:33, pb0 + c // 512, 0:cw]), tz, ns_free)
                    ps_free[half] = tn
                    for q in range(nb):
                        tq2 = pe(lambda p, q=q: p.transpose(
                            PS[:, 7, 33 * q:33 * q + 33], nsb[0:33, 128 * q:128 * q + 128], ident[0:33, 0:33]),
                            tn, rc_free)
                    ns_free = tq2
                    psv = PS[:, 7, 0:33 * nb].rearrange("p (k c) -> p k c", c=33)
                    t1 = dve(lambda v, nb=nb, psv=psv: v.reciprocal(rc[:, 0:nb], psv[:, :, 32]), tq2)
                    rc_free = dve(lambda v, nb=nb, psv=psv, o=o, h=h: v.tensor_tensor(
                        hr[:, o // 128:o // 128 + nb, h, :], psv[:, :, 0:32],
                        rc[:, 0:nb].unsqueeze(2).broadcast_to([128, nb, 32]), ALU.mult), t1)
                else:
                    for c in range(0, wd, 512):
                        cw = min(512, wd - c)
                        td = pe(lambda p, c=c, cw=cw: p.matmul(PS[:, 7, 0:cw], ones[:], acc[:, c:c + cw],
                                                               start=True, stop=True), ty, rec_free)
                        t1 = dve(lambda v, cw=cw: v.reciprocal(rec[:, 0:cw], PS[:, 7, 0:cw]), td, rec_free)
                        oc = slice(o + c, o + c + cw)
                        if h == 0:
                            t2 = dve(lambda v, c=c, cw=cw, oc=oc, pb0=pb0: v.tensor_tensor(
                                oT[:, oc], PS[:, pb0 + c // 512, 0:cw], rec[:, 0:cw], ALU.mult), t1, tz)
                        else:
                            t2 = dve(lambda v, c=c, cw=cw, pb0=pb0: v.tensor_tensor(
                                tm2[:, 0:cw], PS[:, pb0 + c // 512, 0:cw], rec[:, 0:cw], ALU.mult), t1, tz)
                            t2 = dve(lambda v, cw=cw, oc=oc: v.tensor_tensor(
                                oT[:, oc], oT[:, oc], tm2[:, 0:cw], ALU.add), t2)
                        rec_free = t2
                    ps_free[half] = t2
                    acc_free = td
        P.barrier()
        if not last:
            lastj = {}
            for j in range(NT):
                for q in range(tile_w(j) // 128):
                    t = pe(lambda p, j=j, q=q: p.transpose(
                        PS[:, j % 4, 128 * q:128 * q + 128],
                        hr[:, 4 * j + q].rearrange("p h c -> p (h c)"), ident[:]), lastj.get(j - 4))
                lastj[j] = act(lambda s, j=j: s.activation(
                    hT[:, 512 * j:512 * j + tile_w(j)], PS[:, j % 4, 0:tile_w(j)], ACT.Relu, bias=bcol[:]), t)
        else:
            t = act(lambda s: s.activation(oT[:], oT[:], ACT.Identity, bias=bcol[:], scale=0.25))
            lastj = {}
            for j in range(NT):
                nb = tile_w(j) // 128
                for q in range(nb):
                    t1 = pe(lambda p, j=j, q=q: p.transpose(
                        PS[:, j % 4, 128 * q:128 * q + 128],
                        oT[:, 512 * j + 128 * q:512 * j + 128 * q + 128], ident[:]), t, lastj.get(j - 4))
                lastj[j] = dve(lambda v, j=j, nb=nb: v.tensor_tensor(
                    xr[:, 4 * j:4 * j + nb, :], xr[:, 4 * j:4 * j + nb, :],
                    PS[:, j % 4, 0:128 * nb].rearrange("p (k c) -> p k c", c=128), ALU.add), t1)
        P.barrier()
        g.close()

    gat(1, W1, as1, ad1, b1)
    gat(2, W2, as2, ad2, b2)
    gat(3, W3, as3, ad3, b3)

    pd = ExitStack()
    ln1 = sb("ln1", [128, NB, D], F32, pd)
    ln2 = sb("ln2", [128, 2, NB], F32, pd)
    mr = sb("mr", [128, NB, D], F32, pd)

    def split(rows, hi, lo, *w):
        t = act(lambda s: s.mul(hi[:], rows[:], SC), *w)
        return dve(lambda v: v.scalar_tensor_tensor(out=lo[:], in0=rows[:], scalar=SC, in1=hi[:],
                                                    op0=ALU.mult, op1=ALU.subtract), t)

    q = ExitStack()
    hh = [sb(f"hh{i}", [128, NB, D], F16, pd) for i in range(2)]
    hl = [sb(f"hl{i}", [128, NB, D], F16, pd) for i in range(2)]
    w1t = sb("w1t", [128, 512], F32, q)
    w2t = sb("w2t", [128, 4, 128], F32, q)
    b1c = sb("b1c", [128, 4], F32, q)
    rowb = sb("rowb", [128, 3, 128], F32, q)
    uT = sb("uT", [128, NP], F32, q)
    Cf = [sb(f"Cf{i}", [128, NP], F16, q) for i in range(4)]
    hid = [sb(f"hid{i}", [128, 4, 512], F32, q) for i in range(2)]
    sp("l1w", w1t[:], mw1)
    sp("l1w", w2t[:], mw2.rearrange("(c p) d -> p c d", p=128))
    sp("l1w", b1c[:], mb1)
    for i, a in enumerate((mb2, gamma, beta)):
        t_l1 = sp("l1w", rowb[:, i, :], a.partition_broadcast(128))
    t = layernorm(xr, ln1, ln2)
    t_x1 = t
    t_sp = split(xr, hh[0], hl[0], t)
    t_xT = to_cols(xr, hT, t_x1)
    free = {}
    first = t_xT
    for k in range(NB):
        tc = sp(f"cf{k % 4}", Cf[k % 4][:], AC[k], free.get(k - 4))
        for a, part in enumerate((hh[0], hl[0])):
            for j in range(NT):
                wd = tile_w(j)
                t = pe(lambda p, k=k, j=j, wd=wd, part=part, a=a: p.matmul(
                    PS[:, j, 0:wd], part[:, k, :], Cf[k % 4][:, 512 * j:512 * j + wd],
                    start=(k == 0 and a == 0), stop=(k == NB - 1 and a == 1)), tc, t_sp, first)
        free[k] = t

    def rest1():
        t = None
        for k in range(NB):
            tc = sp("cf", Cf[0][:], AC2[k], t)
            for part in (hh[0], hl[0]):
                for j in range(NT):
                    t = pe(lambda p, k=k, j=j, part=part: p.matmul(
                        PS[:, j, 0:tile_w(j)], part[:, k, :], Cf[0][:, 512 * j:512 * j + tile_w(j)],
                        start=False, stop=True, skip_group_check=True), tc)

    P.general(rest1)
    t_u = {}
    for j in range(NT):
        wd = tile_w(j)
        t_u[j] = dve(lambda v, j=j, wd=wd: v.scalar_tensor_tensor(
            out=uT[:, 512 * j:512 * j + wd], in0=PS[:, j, 0:wd], scalar=1.0 / SC, in1=hT[:, 512 * j:512 * j + wd],
            op0=ALU.mult, op1=ALU.subtract), t)
    e = {}
    eh = {}
    eo = {}
    n = 0
    for j in range(NT):
        wd = tile_w(j)
        nb = wd // 128
        for c in range(4):
            t = pe(lambda p, j=j, c=c, wd=wd, b=n % 4: p.matmul(
                PS[:, b, 0:wd], w1t[:, 128 * c:128 * c + 128], uT[:, 512 * j:512 * j + wd],
                start=True, stop=True), t_u[NT - 1], t_l1, e.get(n - 4))
            e[n] = act(lambda s, j=j, c=c, wd=wd, b=n % 4: s.activation(
                hid[j % 2][:, c, 0:wd], PS[:, b, 0:wd], ACT.Relu, bias=b1c[:, c:c + 1]), t, eh.get(j - 2))
            n += 1
        for qq in range(nb):
            for c in range(4):
                t = pe(lambda p, j=j, qq=qq, c=c: p.matmul(
                    PS[:, 4 + j % 2, 128 * qq:128 * qq + 128], hid[j % 2][:, c, 128 * qq:128 * qq + 128],
                    w2t[:, c, :], start=(c == 0), stop=(c == 3)), e[n - 1], eo.get(j - 2))
        eh[j] = t
        t = dve(lambda v, j=j, nb=nb: v.tensor_tensor(
            mr[:, 4 * j:4 * j + nb, :], PS[:, 4 + j % 2, 0:wd].rearrange("p (k c) -> p k c", c=128)
            if False else PS[:, 4 + j % 2, 0:128 * nb].rearrange("p (k c) -> p k c", c=128),
            xr[:, 4 * j:4 * j + nb, :], ALU.add), t)
        eo[j] = t
    rb3 = lambda i: rowb[:, i, :].unsqueeze(1).broadcast_to([128, NB, D])
    t = dve(lambda v: v.tensor_tensor(mr[:], mr[:], rb3(0), ALU.add), t)
    t = layernorm(mr, ln1, ln2, t)
    t = dve(lambda v: v.tensor_tensor(mr[:], mr[:], rb3(1), ALU.mult), t)
    t = dve(lambda v: v.tensor_tensor(mr[:], mr[:], rb3(2), ALU.add), t)
    t = dve(lambda v: v.tensor_tensor(xr[:], xr[:], mr[:], ALU.add), t)
    t_x2 = layernorm(xr, ln1, ln2, t)
    P.barrier()
    q.close()

    q = ExitStack()
    wkt = sb("wkt", [128, 6, 128], F32, q)
    wab = sb("wab", [128, 2, 128], F32, q)
    bkb = sb("bkb", [128, 7, 128], F32, q)
    bsum = sb("bsum", [128, 128], F32, q)
    lam = sb("lam", [128, 4], F32, q)
    scl = sb("scl", [128, NB], F32, q)
    t2x = sb("t2x", [128, NB, D], F32, q)
    sp("l2w", wkt[:], Wk.rearrange("k d o -> d k o"))
    sp("l2w", bkb[:, 0:6, :].rearrange("p k o -> p (k o)"), bk.rearrange("k o -> (k o)").partition_broadcast(128))
    t_l2 = sp("l2w", bkb[:, 6, :], cbias.partition_broadcast(128))
    t = dve(lambda v: v.tensor_reduce(bsum[:], bkb.rearrange("p k o -> p o k"), AX, ALU.add), t_l2)
    t = dve(lambda v: v.tensor_tensor(wab[:, 0, :], wkt[:, 0, :], wkt[:, 2, :], ALU.subtract), t)
    for c in (3, 4, 5):
        t = dve(lambda v, c=c: v.scalar_tensor_tensor(out=wab[:, 0, :], in0=wkt[:, c, :], scalar=-float(c - 1),
                                                      in1=wab[:, 0, :], op0=ALU.mult, op1=ALU.add), t)
    t = dve(lambda v: v.scalar_tensor_tensor(out=wab[:, 1, :], in0=wkt[:, 2, :], scalar=2.0,
                                             in1=wkt[:, 1, :], op0=ALU.mult, op1=ALU.add), t)
    for c in (3, 4, 5):
        t = dve(lambda v, c=c: v.scalar_tensor_tensor(out=wab[:, 1, :], in0=wkt[:, c, :], scalar=float(c),
                                                      in1=wab[:, 1, :], op0=ALU.mult, op1=ALU.add), t)
    t_wab = t
    dve(lambda v: v.tensor_reduce(lam[:, 0:1], net[:, 0:NB], AX, ALU.max))
    t = dve(lambda v: v.tensor_scalar(lam[:, 1:2], wmin[:, 0:1], -1.0, None, ALU.mult))
    t = dve(lambda v: v.tensor_tensor(lam[:, 2:3], lam[:, 0:1], lam[:, 1:2], ALU.max), t)
    t = pool(lambda g: g.partition_all_reduce(lam[:, 3:4], lam[:, 2:3], 128, bass.bass_isa.ReduceOp.max), t)
    t = dve(lambda v: v.reciprocal(lam[:, 0:1], lam[:, 3:4]), t)
    t1 = dve(lambda v: v.tensor_tensor(scl[:], net[:, 0:NB], net[:, NB:2 * NB], ALU.subtract))
    t_sc = dve(lambda v: v.tensor_scalar(scl[:], scl[:], lam[:, 0:1], None, ALU.mult), t, t1)
    t_xT = to_cols(xr, hT)
    e = {}
    for j in range(13):
        nb = min(2, NB - 2 * j)
        for qq in range(nb):
            k = 2 * j + qq
            t = pe(lambda p, k=k, qq=qq, j=j: p.matmul(
                PS[:, 4 + j % 4, 256 * qq:256 * qq + 256], hT[:, 128 * k:128 * k + 128],
                wab.rearrange("p a o -> p (a o)"), start=True, stop=True), t_xT, t_wab, e.get(j - 4))
        psv = PS[:, 4 + j % 4, 0:256 * nb].rearrange("p (k a o) -> p k a o", a=2, o=128)
        ks = slice(2 * j, 2 * j + nb)
        t2 = dve(lambda v, psv=psv, ks=ks, nb=nb: v.tensor_tensor(
            t2x[:, ks, :], psv[:, :, 1, :], scl[:, ks].unsqueeze(2).broadcast_to([128, nb, 128]), ALU.mult),
            t, t_sc)
        e[j] = dve(lambda v, psv=psv, ks=ks: v.tensor_tensor(t2x[:, ks, :], t2x[:, ks, :], psv[:, :, 0, :],
                                                             ALU.add), t2)
    t = dve(lambda v: v.tensor_tensor(t2x[:], t2x[:], bsum[:].unsqueeze(1).broadcast_to([128, NB, D]), ALU.add),
            e[12])
    t = dve(lambda v: v.tensor_tensor(xr[:], xr[:], t2x[:], ALU.add), t)
    t = layernorm(xr, ln1, ln2, t)
    P.barrier()
    q.close()

    q = ExitStack()
    wer = sb("wer", [128, 4, 128], F32, q)
    weT = sb("weT", [128, 4, 128], F32, q)
    wir = sb("wir", [128, 2, 3, 128], F32, q)
    wgT = sb("wgT", [128, 2, 3, 128], F32, q)
    bet = sb("bet", [4, 128], F32, q)
    bi = sb("bi", [128, 2, 3], F32, q)
    brz = sb("brz", [128, 2], F32, q)
    sel = sb("sel", [128, 4, 4], F16, q)
    cnt = sb("cnt", [4, NP], F32, q)
    hN = [hT, sb("hN", [128, NP], F32, q)]
    Ab = [sb(f"Ab{i}", [128, NB, 512], F16, q) for i in range(3)]
    ub = [sb(f"ub{i}", [128, 512], F32, q) for i in range(2)]
    aT = sb("aT", [128, 512], F32, q)
    rg = sb("rg", [128, 512], F32, q)
    zg = sb("zg", [128, 512], F32, q)
    hnb = sb("hnb", [128, 512], F32, q)
    ng = sb("ng", [128, 512], F32, q)
    dd = sb("dd", [128, 512], F32, q)

    sp("l3w", wer[:], We.rearrange("t o d -> o t d"))
    sp("l3w", wir[:, 0], Wih.rearrange("(g o) d -> o g d", o=128))
    sp("l3w", wir[:, 1], Whh.rearrange("(g o) d -> o g d", o=128))
    sp("l3w", bet[:], be)
    sp("l3w", bi[:, 0, :], bih)
    t_l3 = sp("l3w", bi[:, 1, :], bhh)
    for i in range(4):
        t = pe(lambda p, i=i: p.transpose(PS[:, 0, 128 * i:128 * i + 128], wer[:, i, :], ident[:]), t_l3)
    act(lambda s: s.copy(weT.rearrange("p t o -> p (t o)"), PS[:, 0, :]), t)
    for a in range(2):
        for i in range(3):
            t = pe(lambda p, a=a, i=i: p.transpose(PS[:, 1 + a, 128 * i:128 * i + 128], wir[:, a, i, :], ident[:]),
                   t_l3)
        t_wg = act(lambda s, a=a: s.copy(wgT[:, a].rearrange("p g o -> p (g o)"), PS[:, 1 + a, 0:384]), t)
    t_brz = dve(lambda v: v.tensor_tensor(brz[:], bi[:, 0, 0:2], bi[:, 1, 0:2], ALU.add), t_l3)
    t = dve(lambda v: v.memset(sel[:], 0.0))
    for i in range(4):
        t_sel = dve(lambda v, i=i: v.memset(sel[:, i, i:i + 1], 1.0), t)
    P.barrier()
    split(xr, hh[0], hl[0])
    to_cols(xr, hT)
    P.barrier()

    n = 0
    a_free = {}
    u_ev = {}
    nu = 0
    t_h = None
    for step in range(4):
        cur, nxt = hN[step % 2], hN[1 - step % 2]
        sh, sl = hh[step % 2], hl[step % 2]
        nh, nl = hh[1 - step % 2], hl[1 - step % 2]
        for j in range(NT):
            wd = tile_w(j)
            cs = slice(512 * j, 512 * j + wd)
            if step == 0:
                pass
            for ty in range(4):
                ab = Ab[n % 3]
                ta = sp(f"ab{n % 3}", ab[:, :, 0:wd], AT[j][:, NB * ty:NB * ty + NB, :], a_free.get(n - 3))
                ubank = nu % 2
                for k in range(NB):
                    for a, part in enumerate((sh, sl)):
                        t = pe(lambda p, ab=ab, k=k, part=part, wd=wd, ubank=ubank, a=a: p.matmul(
                            PS[:, ubank, 0:wd], part[:, k, :], ab[:, k, 0:wd],
                            start=(k == 0 and a == 0), stop=(k == NB - 1 and a == 1)),
                            ta if k == 0 and a == 0 else None, t_h if k == 0 and a == 0 else None,
                            u_ev.get(nu - 2) if k == 0 and a == 0 else None)
                tu = t
                if step == 0:
                    for k in range(NB):
                        t = pe(lambda p, ab=ab, k=k, ty=ty, wd=wd: p.matmul(
                            PS[0:4, 7, 0:wd], sel[:, ty, :], ab[:, k, 0:wd],
                            start=(k == 0 and ty == 0), stop=(k == NB - 1 and ty == 3)),
                            t_sel, u_ev.get("cnt"))
                a_free[n] = t

                def rest3(step=step, j=j, ty=ty, wd=wd, ubank=ubank, sh=sh, sl=sl, ab=Ab[(n + 1) % 3]):
                    ta = sp("ab", ab[:, :, 0:wd], AT2[j][:, NB * ty:NB * ty + NB, :])
                    for k in range(NB):
                        for part in (sh, sl):
                            pe(lambda p, k=k, part=part: p.matmul(
                                PS[:, ubank, 0:wd], part[:, k, :], ab[:, k, 0:wd],
                                start=False, stop=True, skip_group_check=True), ta)
                        if step == 0:
                            pe(lambda p, k=k: p.matmul(
                                PS[0:4, 7, 0:wd], sel[:, ty, :], ab[:, k, 0:wd],
                                start=False, stop=True, skip_group_check=True), ta)

                P.general(rest3)
                n += 1
                u_ev[nu] = act(lambda s, nu=nu, ubank=ubank, wd=wd: s.mul(
                    ub[nu % 2][:, 0:wd], PS[:, ubank, 0:wd], 1.0 / SC), tu, u_ev.get(("w", nu - 2)))
                if step == 0 and ty == 3:
                    u_ev["cnt"] = act(lambda s, cs=cs, wd=wd: s.copy(cnt[:, cs], PS[0:4, 7, 0:wd]), t)
                u_ev[("w", nu)] = pe(lambda p, nu=nu, ty=ty, wd=wd: p.matmul(
                    PS[:, 2, 0:wd], weT[:, ty, :], ub[nu % 2][:, 0:wd], start=(ty == 0), stop=False),
                    u_ev[nu], u_ev.get("a") if ty == 0 else None)
                nu += 1
            t = pe(lambda p, cs=cs, wd=wd: p.matmul(PS[:, 2, 0:wd], bet[:], cnt[:, cs], start=False, stop=True),
                   u_ev.get("cnt"))
            t_a = act(lambda s, wd=wd: s.copy(aT[:, 0:wd], PS[:, 2, 0:wd]), t, u_ev.get("gi"))
            u_ev["a"] = t_a
            gw = u_ev.get("g")
            for i in range(2):
                pe(lambda p, i=i, wd=wd: p.matmul(PS[:, 3 + i, 0:wd], wgT[:, 0, i, :], aT[:, 0:wd],
                                                  start=True, stop=False), t_a, gw)
                t = pe(lambda p, i=i, wd=wd, cur=cur, cs=cs: p.matmul(
                    PS[:, 3 + i, 0:wd], wgT[:, 1, i, :], cur[:, cs], start=False, stop=True))
                if i == 0:
                    t_r = t
                else:
                    t_z = t
            t_in = pe(lambda p, wd=wd: p.matmul(PS[:, 5, 0:wd], wgT[:, 0, 2, :], aT[:, 0:wd],
                                                start=True, stop=True))
            t_hn = pe(lambda p, wd=wd, cur=cur, cs=cs: p.matmul(PS[:, 6, 0:wd], wgT[:, 1, 2, :], cur[:, cs],
                                                                start=True, stop=True))
            u_ev["gi"] = t_hn
            t_r = act(lambda s, wd=wd: s.activation(rg[:, 0:wd], PS[:, 3, 0:wd], ACT.Sigmoid, bias=brz[:, 0:1]), t_r)
            t_z = act(lambda s, wd=wd: s.activation(zg[:, 0:wd], PS[:, 4, 0:wd], ACT.Sigmoid, bias=brz[:, 1:2]),
                      t_z, u_ev.get("h"))
            t = dve(lambda v, wd=wd: v.scalar_tensor_tensor(
                out=hnb[:, 0:wd], in0=PS[:, 6, 0:wd], scalar=bi[:, 1, 2:3], in1=rg[:, 0:wd],
                op0=ALU.add, op1=ALU.mult), t_hn, t_r)
            t = dve(lambda v, wd=wd: v.tensor_tensor(hnb[:, 0:wd], PS[:, 5, 0:wd], hnb[:, 0:wd], ALU.add), t)
            u_ev["g"] = [t, t_z]
            t_n = act(lambda s, wd=wd: s.activation(ng[:, 0:wd], hnb[:, 0:wd], ACT.Tanh, bias=bi[:, 0, 2:3]),
                      t, u_ev.get("h"))
            t = dve(lambda v, wd=wd, cur=cur, cs=cs: v.tensor_tensor(dd[:, 0:wd], cur[:, cs], ng[:, 0:wd],
                                                                     ALU.subtract), t_n)
            t = dve(lambda v, wd=wd: v.tensor_tensor(dd[:, 0:wd], dd[:, 0:wd], zg[:, 0:wd], ALU.mult), t, t_z)
            t = dve(lambda v, wd=wd, nxt=nxt, cs=cs: v.tensor_tensor(nxt[:, cs], dd[:, 0:wd], ng[:, 0:wd],
                                                                     ALU.add), t)
            u_ev["h"] = t
            nb = wd // 128
            for qq in range(nb):
                t1 = pe(lambda p, qq=qq, nxt=nxt, j=j: p.transpose(
                    PS[:, 7, 128 * qq:128 * qq + 128],
                    nxt[:, 512 * j + 128 * qq:512 * j + 128 * qq + 128], ident[:]), t, u_ev.get("tr"),
                    u_ev.get("cnt"))
            psv = PS[:, 7, 0:wd].rearrange("p (k c) -> p k c", c=128)
            if step < 3:
                t2 = act(lambda s, nh=nh, j=j, nb=nb, psv=psv: s.mul(nh[:, 4 * j:4 * j + nb, :], psv, SC), t1)
                t3 = dve(lambda v, nh=nh, nl=nl, j=j, nb=nb, psv=psv: v.scalar_tensor_tensor(
                    out=nl[:, 4 * j:4 * j + nb, :], in0=psv, scalar=SC, in1=nh[:, 4 * j:4 * j + nb, :],
                    op0=ALU.mult, op1=ALU.subtract), t2)
            else:
                t3 = dve(lambda v, j=j, nb=nb, psv=psv: v.tensor_tensor(
                    xr[:, 4 * j:4 * j + nb, :], xr[:, 4 * j:4 * j + nb, :], psv, ALU.add), t1)
            u_ev["tr"] = t3
            u_ev["cnt"] = t3 if step == 0 else u_ev.get("cnt")
        t_h = t3
    t = layernorm(xr, ln1, ln2, t3)
    sp("out", out[0:128 * (NB - 1), :].rearrange("(b p) d -> p b d", p=128), xr[:, 0:NB - 1, :], t)
    t = sp("out", out[128 * (NB - 1):N, :], xr[0:N - 128 * (NB - 1), NB - 1, :])
    P.wait("sp", t)
    q.close()
    pd.close()

    block = ctx.enter_context(nc.Block())

    @block.sync
    def _(eng):
        P.emit("sp", eng)

    @block.gpsimd
    def _(eng):
        P.emit("pool", eng)

    @block.scalar
    def _(eng):
        P.emit("act", eng)

    @block.vector
    def _(eng):
        P.emit("dve", eng)

    @block.tensor
    def _(eng):
        P.emit("pe", eng)

    ctx.close()


_INS = ["x", "src", "dst", "bnd", "edge_attr_4", "edge_weight",
        "L0_gnn_W1", "L0_gnn_as1", "L0_gnn_ad1", "L0_gnn_b1", "L0_gnn_W2", "L0_gnn_as2", "L0_gnn_ad2", "L0_gnn_b2",
        "L0_gnn_W3", "L0_gnn_as3", "L0_gnn_ad3", "L0_gnn_b3",
        "L1_gnn_w1", "L1_gnn_b1", "L1_gnn_w2", "L1_gnn_b2", "L1_gnn_gamma", "L1_gnn_beta",
        "L2_gnn_Wk", "L2_gnn_bk", "L2_gnn_bias",
        "L3_gnn_W_edge", "L3_gnn_b_edge", "L3_gnn_W_ih", "L3_gnn_W_hh", "L3_gnn_b_ih", "L3_gnn_b_hh"]


def lay_out(inputs):
    import numpy as np

    a = {k: np.ascontiguousarray(v) for k, v in inputs.items()}

    def pad(v, fill):
        o = np.full((EP,) + v.shape[1:], fill, v.dtype)
        o[:E] = v
        return o

    a["src"] = pad(a["src"], 0)
    a["dst"] = pad(a["dst"], 4000)
    a["edge_attr_4"] = pad(a["edge_attr_4"], 0)
    a["edge_weight"] = pad(a["edge_weight"], 0)
    for name in ("L1_gnn_b1", "L3_gnn_b_ih", "L3_gnn_b_hh"):
        a[name] = np.ascontiguousarray(a[name].reshape(-1, 128).T)
    a["bnd"] = np.ascontiguousarray(a["dst"][::128])
    a["dst"] = np.concatenate([a["dst"], np.full(128, 4000, a["dst"].dtype)])
    return a


def kernel(**inputs):
    import concourse.bacc as _bacc
    from concourse.bass_utils import run_bass_kernel_spmd as _run

    nc = _bacc.Bacc("TRN2", target_bir_lowering=False, num_devices=1)
    a = lay_out(inputs)
    arrays, args = {}, []
    for name in _INS:
        arrays[f"in_{name}"] = a[name]
        args.append(nc.dram_tensor(f"in_{name}", a[name].shape, mybir.dt.from_np(a[name].dtype),
                                   kind="ExternalInput").ap())
    args.append(nc.dram_tensor("out_0", (N, D), F32, kind="ExternalOutput").ap())
    gnn_kernel(nc, *args)
    r = _run(nc, [arrays], core_ids=[0])
    return r.results[0]["out_0"]
```

```python
from contextlib import ExitStack

import concourse.bass as bass
from concourse import mybir
from concourse.alu_op_type import AluOpType as ALU

F32 = mybir.dt.float32
F16 = mybir.dt.float16
BF16 = mybir.dt.bfloat16
I32 = mybir.dt.int32
ACT = mybir.ActivationFunctionType
AX = mybir.AxisListType.X

N = 3125
NB = 25
NP = NB * 128
E = 103125
EC = 808
EP = EC * 128
SLACK = 384
D = 128
H = 4
NT = 7
BIG = -3.0e38
SC = 4096.0
GR = 2
GRG = 4
NW = 13
NXT = 49
GEN = [128, 128, 128, 128, 128, 128, 32]
LNEPS = 1e-5


def tile_w(j):
    return min(512, NP - 512 * j)


class Queues:

    def __init__(self, nc, ctx):
        self.nc, self.ctx = nc, ctx
        self.q = {e: [] for e in ("pe", "dve", "act", "pool", "sp")}
        self.n = {}
        self.sem = {}
        self.own = {}
        self.pre = ""
        self.flag = {}
        self.per = {}
        self.it = None

    def _sem(self, name):
        if name not in self.sem:
            self.sem[name] = self.ctx.enter_context(self.nc.semaphore(f"s_{name}"))
            self.n[name] = 0
            self.own[name] = self.pre
        return self.sem[name]

    def wait(self, e, *tokens):
        most = {}
        flat = list(tokens)
        while flat:
            t = flat.pop(0)
            if isinstance(t, list):
                flat = t + flat
            elif t is not None:
                most[t[0]] = max(t[1], most.get(t[0], 0))
        for name, v in most.items():
            self.q[e].append(lambda eng, name=name, v=v: eng.wait_ge(
                self.sem[name], self.it * self.per[name] + v if name in self.per else v))

    def op(self, e, fn, *tokens):
        self.wait(e, *tokens)
        name = self.pre + e
        s = self._sem(name)
        self.n[name] += 1
        self.q[e].append(lambda eng: fn(eng).then_inc(s, 1))
        return (name, self.n[name])

    def raw(self, e, fn, *tokens):
        self.wait(e, *tokens)
        self.q[e].append(fn)

    def dma(self, e, sem, out, in_, *tokens):
        sem = self.pre + sem
        s = self._sem(sem)
        self.wait(e, *tokens)
        self.n[sem] += 16
        get = lambda a: a() if callable(a) else a
        self.q[e].append(lambda eng: eng.dma_start(get(out), get(in_)).then_inc(s, 16))
        return (sem, self.n[sem])

    def now(self):
        return [(k, v) for k, v in self.n.items() if v and self.own[k] == self.pre]

    def barrier(self, engines=None):
        now = self.now()
        for e in engines or self.q:
            self.wait(e, now)

    def general(self, build, pre="g_", flag="edges"):
        now = self.now()
        outer, self.q = self.q, {e: [] for e in self.q}
        for e in self.q:
            self.wait(e, now)
        was, self.pre = self.pre, pre
        build()
        self.barrier()
        self.pre = was
        inner, self.q = self.q, outer

        def branch(e):
            def emit(eng):
                with eng.If(self.flag[flag, e] != 0):
                    for fn in inner[e]:
                        fn(eng)
            return emit

        for e in self.q:
            self.q[e].append(branch(e))

    def loop(self, count, pre, engines, build):
        now = self.now()
        outer, self.q = self.q, {e: [] for e in self.q}
        was, self.pre = self.pre, pre
        build()
        self.barrier(engines)
        turn = {k: v for k, v in self.now()}
        self.pre = was
        inner, self.q = self.q, outer

        def run(e):
            def emit(eng):
                self.per = turn
                with eng.Fori(0, count) as it:
                    self.it = it
                    for fn in inner[e]:
                        fn(eng)
                self.per = {}
            return emit

        def after(name, v):
            return lambda eng: eng.wait_ge(self.sem[name], v)

        for e in self.q:
            if e in engines:
                self.wait(e, now)
                self.q[e].append(run(e))
            else:
                for k, v in turn.items():
                    self.q[e].append(after(k, v * count))

    def emit(self, e, eng):
        for fn in self.q[e]:
            fn(eng)


def gnn_kernel(nc, x, src, dst, bnd, attr, ew,
               W1, as1, ad1, b1, W2, as2, ad2, b2, W3, as3, ad3, b3,
               mw1, mb1, mw2, mb2, gamma, beta, Wk, bk, cbias,
               We, be, Wih, Whh, bih, bhh, out):
    ctx = ExitStack()
    P = Queues(nc, ctx)
    pe = lambda fn, *w: P.op("pe", fn, *w)
    dve = lambda fn, *w: P.op("dve", fn, *w)
    act = lambda fn, *w: P.op("act", fn, *w)
    pool = lambda fn, *w: P.op("pool", fn, *w)
    sp = lambda sem, o, i, *w: P.dma("sp", sem, o, i, *w)

    def sb(name, shape, dt=F32, c=ctx):
        return c.enter_context(nc.sbuf_tensor(name, shape, dt))

    def dram(name, shape, dt):
        return nc.dram_tensor(name, shape, dt).ap()

    AT = [dram(f"AT{j}", (128, 4 * NB, tile_w(j)), F16) for j in range(NT)]
    AC = dram("AC", (NB, 128, NP), F16)
    AT2 = [dram(f"ATL{j}", (128, 4 * NB, tile_w(j)), F16) for j in range(NT)]
    AC2 = dram("ACL", (NB, 128, NP), F16)
    KT_D = dram("KTAB", (EP + SLACK, 4), F32)
    WS_D = dram("WSUM", (NW * 256,), F32)

    PS = ctx.enter_context(nc.psum_tensor("PS", [128, 8, 512], F32))
    PST = PS[:, 4:8, :].bitcast(F16)

    ident = sb("ident", [128, 128])
    identh = sb("identh", [128, 128], F16)
    io_i = sb("io_i", [128, 400], I32)
    ioh = sb("ioh", [128, 400], F16)
    iof = sb("iof", [128, 128])
    thr_i = sb("thr_i", [128, NW], I32)
    thr = sb("thr", [128, NW])
    thr25 = sb("thr25", [128, NW])
    thr100 = sb("thr100", [128, NW])
    epst = sb("epst", [128, 1])
    xr = sb("xr", [128, NB, D])
    net = sb("net", [128, 2 * NB])
    wmin = sb("wmin", [128, 4])
    flag = sb("flag", [128, 5])
    flag_i = sb("flag_i", [128, 2], I32)
    range_i = sb("range_i", [128, 3], I32)

    c0 = pool(lambda g: g.memset(ident[:], 1.0))
    t_id = pool(lambda g: g.affine_select(out=ident[:], in_=ident[:], compare_op=ALU.is_equal, fill=0.0,
                                          base=0, pattern=[[-1, 128]], channel_multiplier=1), c0)
    t_io = pool(lambda g: g.iota(io_i[:], pattern=[[1, 400]], base=0, channel_multiplier=0))
    t_th = pool(lambda g: g.iota(thr_i[:], pattern=[[256, NW]], base=0, channel_multiplier=GR))
    t_ep = dve(lambda v: v.memset(epst[:], LNEPS))
    t_idh = dve(lambda v: v.tensor_copy(identh[:], ident[:]), t_id)
    t_ioh = dve(lambda v: v.tensor_copy(ioh[:], io_i[:]), t_io)
    t_iof = dve(lambda v: v.tensor_copy(iof[:], io_i[:, 0:128]), t_io)
    t_thr = dve(lambda v: v.tensor_copy(thr[:], thr_i[:]), t_th)
    t_25 = dve(lambda v: v.tensor_scalar(thr25[:], thr[:], 25.0, None, ALU.mult), t_thr)
    t_100 = dve(lambda v: v.tensor_scalar(thr100[:], thr[:], 100.0, None, ALU.mult), t_thr)
    t_xz = dve(lambda v: v.memset(xr[:, NB - 1, :], 0.0))

    pa = ExitStack()
    lo_f = sb("lo_f", [128, EC], F32, pa)
    hi_f = sb("hi_f", [128, EC], F32, pa)
    w3 = sb("w3", [128, EC, 3], BF16, pa)
    KW = sb("KW", [128, NW, 3, 128], F32, pa)
    pb = ExitStack()
    ewt = sb("ewt", [128, EC], F32, pb)
    dst_i = sb("dst_i", [128, EC], I32, pb)
    src_i = sb("src_i", [128, EC], I32, pb)
    dsn_i = sb("dsn_i", [128, EC], I32, pb)
    att = sb("att", [128, EC, 4], F32, pb)
    mx = sb("mx", [128, EC], F32, pb)
    ne = sb("ne", [128, EC, 3], F32, pb)
    tt = sb("tt", [128, EC], F32, pb)
    di = sb("di", [128, EC], I32, pb)
    df = sb("df", [128, EC], F32, pb)
    k4 = sb("k4", [128, EC, 4], F32, pb)
    tail = sb("tail", [128, 3, 4], F32, pb)
    bb_i = sb("bb_i", [128, EC], I32, pb)
    bb = sb("bb", [128, EC], F32, pb)
    scr = sb("scr", [128, EC], F32, pb)
    nbt = sb("nbt", [128, NW], F32, pb)
    c0f = sb("c0f", [128, NW], F32, pb)
    c0i = sb("c0i", [128, NW], I32, pb)
    drow = sb("drow", [128, NW, 128], I32, pb)
    drf = sb("drf", [128, NW, 128], F32, pb)
    sf = sb("sf", [128, NW], F32, pb)
    si = sb("si", [128, NW], I32, pb)
    win = sb("win", [128, NW, 128, 4], F32, pb)
    win2 = sb("win2", [128, NW, 3, 128], F32, pb)
    wmk = sb("wmk", [128, NW, 128], F32, pb)
    wst = sb("wst", [NB, 128], F32, pb)
    wsx = sb("wsx", [128, NW, GR], F32, pb)

    t_bb = sp("bb", bb_i[:], bnd.partition_broadcast(128))
    t_s = sp("src", src_i[:], src.rearrange("(p i) -> p i", p=128))
    t_d = sp("dst", dst_i[:], dst[0:EP].rearrange("(p i) -> p i", p=128))
    t_a = sp("att", att[:], attr.rearrange("(p i) t -> p i t", p=128))
    t_w = sp("ew", ewt[:], ew.rearrange("(p i) -> p i", p=128))
    t_dn = sp("dsn", dsn_i[:], dst[1:EP + 1].rearrange("(p i) -> p i", p=128))
    sp("x", xr[:, 0:NB - 1, :], x[0:128 * (NB - 1), :].rearrange("(b p) d -> p b d", p=128))
    t_x = sp("x", xr[0:N - 128 * (NB - 1), NB - 1, :], x[128 * (NB - 1):N, :], t_xz)

    t = dve(lambda v: v.tensor_copy(bb[:], bb_i[:]), t_bb)
    for k in range(NW):
        t = dve(lambda v, k=k: v.tensor_scalar(scr[:], bb[:], thr[:, k:k + 1], 0.0, ALU.is_lt, ALU.add,
                                               accum_out=nbt[:, k:k + 1]), t, t_thr)
    t = dve(lambda v: v.tensor_scalar(c0f[:], nbt[:], 1.0, 0.0, ALU.subtract, ALU.max), t)
    t_c0 = dve(lambda v: v.tensor_copy(c0i[:], c0f[:]), t)
    dst_r = dst[0:EP].rearrange("(c e) -> c e", e=128)

    def gather(sem, o, tab, ix, *w):
        s = P._sem(sem)
        P.wait("pool", *w)
        P.n[sem] += 16
        P.q["pool"].append(lambda g: g.indirect_dma_start(
            out=o, out_offset=None, in_=tab,
            in_offset=bass.IndirectOffsetOnAxis(ap=ix, axis=0)).then_inc(s, 16))
        return (sem, P.n[sem])

    for k in range(NW):
        t_g = gather("g0", drow[:, k, :], dst_r, c0i[:, k:k + 1], t_c0)

    t = dve(lambda v: v.tensor_scalar(di[:], src_i[:], 7, None, ALU.logical_shift_right), t_s)
    t_hi = dve(lambda v: v.tensor_copy(hi_f[:], di[:]), t)
    t = dve(lambda v: v.tensor_scalar(di[:], src_i[:], 127, None, ALU.bitwise_and), t_hi)
    t_lo = dve(lambda v: v.tensor_copy(lo_f[:], di[:]), t)
    t_df = dve(lambda v: v.tensor_copy(df[:], dst_i[:]), t_d)
    t = dve(lambda v: v.tensor_reduce(mx[:], att[:], AX, ALU.max), t_a)
    for c in range(3):
        t_ne = dve(lambda v, c=c: v.tensor_tensor(ne[:, :, c], att[:, :, c], mx[:], ALU.not_equal), t)
    t = dve(lambda v: v.scalar_tensor_tensor(out=tt[:], in0=ne[:, :, 2], scalar=1.0, in1=ne[:, :, 1],
                                             op0=ALU.add, op1=ALU.mult), t_ne)
    t = dve(lambda v: v.scalar_tensor_tensor(out=tt[:], in0=tt[:], scalar=1.0, in1=ne[:, :, 0],
                                             op0=ALU.add, op1=ALU.mult), t)
    t = dve(lambda v: v.scalar_tensor_tensor(out=tt[:], in0=tt[:], scalar=25.0, in1=hi_f[:],
                                             op0=ALU.mult, op1=ALU.add), t, t_hi)
    t_k0 = dve(lambda v: v.scalar_tensor_tensor(out=k4[:, :, 0], in0=df[:], scalar=100.0, in1=tt[:],
                                                op0=ALU.mult, op1=ALU.add), t, t_df)
    t_k1 = dve(lambda v: v.scalar_tensor_tensor(out=k4[:, :, 1], in0=df[:], scalar=25.0, in1=hi_f[:],
                                                op0=ALU.mult, op1=ALU.add), t_df)
    t_k2 = act(lambda s: s.copy(k4[:, :, 2], lo_f[:]), t_lo)
    t_k3 = act(lambda s: s.copy(k4[:, :, 3], ewt[:]), t_w)
    t_tl = dve(lambda v: v.memset(tail[:], 1.0e6))
    sp("ktab", KT_D[0:EP, :].rearrange("(p i) c -> p (i c)", p=128), k4.rearrange("p i c -> p (i c)"),
       t_k1, t_k3)
    t_kt = sp("ktab", KT_D[EP:EP + SLACK, :].rearrange("(p i) c -> p (i c)", p=128),
              tail.rearrange("p i c -> p (i c)"), t_tl)
    t_wm = dve(lambda v: v.tensor_reduce(wmin[:, 0:1], ewt[:], AX, ALU.min), t_w)
    t = dve(lambda v: v.tensor_copy(w3[:, :, 0], ewt[:]), t_w)
    t = dve(lambda v: v.tensor_tensor(tt[:], ewt[:], w3[:, :, 0], ALU.subtract), t, t_k0)
    t = dve(lambda v: v.tensor_copy(w3[:, :, 1], tt[:]), t)
    t_w3 = dve(lambda v: v.tensor_tensor(w3[:, :, 2], tt[:], w3[:, :, 1], ALU.subtract), t)

    t = dve(lambda v: v.tensor_copy(drf[:], drow[:]), t_g)
    for k in range(NW):
        t = dve(lambda v, k=k: v.tensor_scalar(scr[:, 0:128], drf[:, k, :], thr[:, k:k + 1], 0.0, ALU.is_lt,
                                               ALU.add, accum_out=nbt[:, k:k + 1]), t)
    t = dve(lambda v: v.scalar_tensor_tensor(out=sf[:], in0=c0f[:], scalar=128.0, in1=nbt[:],
                                             op0=ALU.mult, op1=ALU.add), t)
    t_si = dve(lambda v: v.tensor_copy(si[:], sf[:]), t)
    for k in range(NW):
        t_win = gather("g1", win[:, k].rearrange("p e c -> p (e c)"), KT_D, si[:, k:k + 1], t_si, t_kt)
    bcw = lambda a: a[:].unsqueeze(2).broadcast_to([128, NW, 128])
    t2 = []
    t2.append(dve(lambda v: v.tensor_tensor(win2[:, :, 0, :], win[:, :, :, 0], bcw(thr100), ALU.subtract),
                  t_win, t_100))
    t_w1 = dve(lambda v: v.tensor_tensor(win2[:, :, 1, :], win[:, :, :, 1], bcw(thr25), ALU.subtract), t_25)
    t2.append(t_w1)
    t2.append(act(lambda s: s.copy(win2[:, :, 2, :], win[:, :, :, 2]), t_win))
    t = dve(lambda v: v.tensor_tensor(scr[:], dst_i[:], dsn_i[:], ALU.is_gt), t_dn)
    t = dve(lambda v: v.tensor_reduce(flag[:, 0:1], scr[:], AX, ALU.max), t)
    t1 = dve(lambda v: v.tensor_scalar(nbt[:], win2[:, :, 0, 127], 100.0 * GR, None, ALU.is_lt), t2)
    t1 = dve(lambda v: v.tensor_reduce(flag[:, 1:2], nbt[:], AX, ALU.max), t1)
    t = dve(lambda v: v.tensor_tensor(flag[:, 2:3], flag[:, 0:1], flag[:, 1:2], ALU.max), t, t1)
    t = pool(lambda g: g.partition_all_reduce(flag[:, 3:4], flag[:, 2:3], 128, bass.bass_isa.ReduceOp.max), t)
    t = dve(lambda v: v.tensor_scalar(flag[:, 4:5], flag[:, 3:4], -1.0, 1.0, ALU.mult, ALU.add), t)
    t = dve(lambda v: v.tensor_copy(flag_i[:], flag[:, 3:5]), t)

    def load_flag(name, tile, col, *w):
        def emit_on(e):
            def emit(eng):
                P.flag[name, e] = eng.value_load(tile[0:1, col:col + 1], min_val=0, max_val=1)
            return emit

        for e in P.q:
            P.raw(e, emit_on(e), *w)

    load_flag("edges", flag_i, 0, t)
    load_flag("plain", flag_i, 1)
    for d in range(GR):
        t = dve(lambda v, d=d: v.scalar_tensor_tensor(out=wmk[:], in0=win2[:, :, 1, :], scalar=25.0 * d,
                                                      in1=win[:, :, :, 3], op0=ALU.is_ge, op1=ALU.mult), t_w1)
        t = dve(lambda v, d=d: v.scalar_tensor_tensor(out=wmk[:], in0=win2[:, :, 1, :], scalar=25.0 * d + 25.0,
                                                      in1=wmk[:], op0=ALU.is_lt, op1=ALU.mult), t)
        t = t_w1 = dve(lambda v, d=d: v.tensor_reduce(wsx[:, :, d], wmk[:], AX, ALU.add), t)
    t = sp("wsum", WS_D.rearrange("(k p d) -> p k d", p=128, d=GR), wsx[:], t)
    t_wst = sp("wsum", wst[:], WS_D[0:NP].rearrange("(b p) -> b p", p=128), t)
    t = pe(lambda p: p.transpose(PS[:, 4, 0:NB], wst[:], ident[0:NB, 0:NB]), t_wst, t_id)
    dve(lambda v: v.tensor_copy(net[:, NB:2 * NB], PS[:, 4, 0:NB]), t)
    nev = {}
    for k in range(NW):
        b = k % 4
        for a in range(3):
            tp = pe(lambda p, k=k, a=a, b=b: p.transpose(
                PS[:, b, 128 * a:128 * a + 128], win2[:, k, a, :], ident[:]),
                t2, t_id, nev.get(k - 4) if a == 0 else None)
        nev[k] = act(lambda s, k=k, b=b: s.copy(
            KW[:, k].rearrange("p a g -> p (a g)"), PS[:, b, 0:384]), tp)
    P.barrier()
    pb.close()

    pc = ExitStack()
    ST = [sb(f"ST{i}", [128, 5 * NB, 256], F16, pc) for i in range(2)]
    OM = [sb(f"OM{i}", [128, GR, 5 * NB], F16, pc) for i in range(6)]
    OL = [sb(f"OL{i}", [128, 128], F16, pc) for i in range(6)]
    WS = [sb(f"WS{i}", [128, 128], BF16, pc) for i in range(16)]
    HT = [sb(f"HT{i}", [128, 8, NB], BF16, pc) for i in range(2)]
    WH = [sb(f"WH{i}", [128, 8, 3, NB], BF16, pc) for i in range(3)]
    NG = NP // GR
    NBT = EC // 8
    t_ws = {}
    t_we = {}

    def deg_hot(i):
        c8 = slice(8 * i, 8 * i + 8)
        t = dve(lambda v: v.tensor_tensor(HT[i % 2][:], iof[:, 0:NB].unsqueeze(1).broadcast_to([128, 8, NB]),
                                          hi_f[:, c8].unsqueeze(2).broadcast_to([128, 8, NB]), ALU.is_equal),
                t_ws.get((i - 2, "w")))
        for a in range(3):
            t_ws[i, "w"] = pool(lambda g, a=a: g.tensor_tensor(
                WH[i % 3][:, :, a, :], HT[i % 2][:], w3[:, c8, a].unsqueeze(2).broadcast_to([128, 8, NB]),
                ALU.mult), t, t_we.get(i - 3))
        for c in range(8):
            t_ws[i, c] = pool(lambda g, c=c: g.tensor_scalar(
                WS[8 * (i % 2) + c][:], iof[:], lo_f[:, 8 * i + c:8 * i + c + 1], None, ALU.is_equal),
                t_we.get(i - 2))

    def deg_sum(i):
        for c in range(8):
            t_we[i] = pe(lambda p, c=c: p.matmul(
                PS[:, 3, 0:3 * NB], WS[8 * (i % 2) + c][:], WH[i % 3][:, c].rearrange("p a h -> p (a h)"),
                start=(i == 0 and c == 0), stop=(i == NBT - 1 and c == 7)), t_ws[i, c], t_ws[i, "w"])

    t_pc = {}
    ev = {}
    st_dma = {}
    pair = lambda a, w: a[:, 0:GR * w].rearrange("p (d c) -> p d c", d=GR)
    for g in range(NG):
        k, gl = divmod(g, 128)
        s2 = k % 2
        b = (g // 2) % 3
        sl = g % 6
        if g % 15 == 0 and g // 15 <= NBT:
            if g // 15 < NBT:
                deg_hot(g // 15)
            if g:
                deg_sum(g // 15 - 1)
        dve(lambda v, sl=sl, k=k, gl=gl: v.tensor_scalar(
            OM[sl][:, :, 0:4 * NB], pair(ioh, 4 * NB), KW[:, k, 0, gl:gl + 1], None, ALU.is_equal),
            t_pc.get(g - 6))
        dve(lambda v, sl=sl, k=k, gl=gl: v.tensor_scalar(
            OM[sl][:, :, 4 * NB:5 * NB], pair(ioh, NB), KW[:, k, 1, gl:gl + 1], None, ALU.is_equal))
        t = dve(lambda v, sl=sl, k=k, gl=gl: v.tensor_scalar(
            OL[sl][:], ioh[:, 0:128], KW[:, k, 2, gl:gl + 1], None, ALU.is_equal))
        t_pc[g] = pe(lambda p, sl=sl, b=b, g=g: p.matmul(
            PS[:, b, 250 * (g % 2):250 * (g % 2) + 250], OL[sl][:], OM[sl].rearrange("p d c -> p (d c)"),
            start=True, stop=True), t, ev.get(g // 2 - 3) if g % 2 == 0 else None)
        if g % 2:
            col = GR * (gl - 1)
            ev[g // 2] = act(lambda s, s2=s2, b=b, col=col: s.copy(
                ST[s2][:, :, col:col + 2 * GR], PS[:, b, 0:500].rearrange("p (d c) -> p c d", d=2 * GR)),
                t_pc[g], st_dma.get(k - 2) if col == 0 else None)
        if gl == 127 or g == NG - 1:
            wd = GR * (gl + 1)
            n0 = 256 * k
            tA = sp(f"st{s2}", AT[n0 // 512][:, :, n0 % 512:n0 % 512 + wd], ST[s2][:, 0:4 * NB, 0:wd], ev[g // 2])
            for db in range(wd // 128):
                c = slice(128 * db, 128 * db + 128)
                td = pool(lambda q, s2=s2, r=4 * NB + 2 * k + db, c=c: q.tensor_tensor(
                    ST[s2][:, r, c], ST[s2][:, r, c], identh[:], ALU.add), ev[g // 2])
            tC = sp(f"sc{s2}", AC[:, :, n0:n0 + wd].rearrange("h l d -> l h d"), ST[s2][:, 4 * NB:5 * NB, 0:wd], td)
            st_dma[k] = [tA, tC]
    t = dve(lambda v: v.tensor_reduce(net[:, 0:NB], PS[:, 3, 0:3 * NB].rearrange("p (a h) -> p h a", a=3), AX,
                                      ALU.add), t_we[NBT - 1])
    P.barrier()
    pc.close()
    pa.close()

    def general_build():
        q = ExitStack()
        nx = EC + NB
        kall = sb("kall", [128, nx, 4], F32, q)
        kxi = sb("kxi", [128, 2, NB], I32, q)
        gbk = sb("gbk", [128, 3], F32, q)
        gst = sb("gst", [128, 3], F32, q)
        KD = sb("KD", [128, NXT, 3], F32, q)
        OG = sb("OG", [128, NXT, 628], F16, q)
        tot = sb("tot", [128, 500], F32, q)
        part = sb("part", [128, 2, 500], F16, q)
        wsd = sb("wsd", [128, 8, 128], F32, q)
        wsh = sb("wsh", [128, 8, NB], F32, q)
        dpl = sb("dpl", [128, 2, EC], F32, q)
        dpi = sb("dpi", [128, 2, EC], I32, q)
        t = sp("kall", kall[:, 0:EC, :].rearrange("p i c -> p (i c)"), KT_D[0:EP, :].rearrange("(p i) c -> p (i c)", p=128))
        pool(lambda g: g.iota(kxi[:, 0, :], pattern=[[128 * 25 + 1, NB]], base=0, channel_multiplier=25))
        t1 = pool(lambda g: g.iota(kxi[:, 1, :], pattern=[[0, NB]], base=0, channel_multiplier=1))
        dve(lambda v: v.memset(kall[:, EC:nx, 0], 1.0e6))
        dve(lambda v: v.tensor_copy(kall[:, EC:nx, 1], kxi[:, 0, :]), t1)
        dve(lambda v: v.tensor_copy(kall[:, EC:nx, 2], kxi[:, 1, :]))
        dve(lambda v: v.memset(gst[:], 0.0))
        dve(lambda v: v.memset(gbk[:], 0.0))
        P.barrier()
        dve(lambda v: v.memset(gst[:, 0:1], 400.0))
        dve(lambda v: v.memset(gst[:, 1:2], 100.0))
        P.barrier()
        dc = lambda a: a.rearrange("p (c d) -> p d c", d=GRG)
        for j in range(NT):
            if not GEN[j]:
                continue
            s_ohm, s_mm, s_cut, s_st = (P._sem(f"g_{n}{j}") for n in ("ohm", "mm", "cut", "st"))
            dve(lambda v, j=j: v.memset(gbk[:, 0:1], 400.0 * 128 * j))
            dve(lambda v, j=j: v.memset(gbk[:, 1:2], 100.0 * 128 * j))

            def hot(v, j=j, s_ohm=s_ohm, s_mm=s_mm, s_cut=s_cut, s_st=s_st):
                with v.Fori(0, GEN[j]) as g:
                    v.memset(tot[:], 0.0)
                    with v.Fori(0, nx // NXT) as b:
                        v.drain()
                        v.tensor_tensor(KD[:], kall[:, bass.ds(b * NXT, NXT), 0:3],
                                        gbk[:].unsqueeze(1).broadcast_to([128, NXT, 3]), ALU.subtract)
                        v.drain()
                        for c in range(NXT):
                            v.tensor_scalar(OG[:, c, 0:400], ioh[:, 0:400], KD[:, c, 0:1], None, ALU.is_equal)
                            v.tensor_scalar(OG[:, c, 400:500], ioh[:, 0:100], KD[:, c, 1:2], None, ALU.is_equal)
                            v.tensor_scalar(OG[:, c, 500:628], ioh[:, 0:128], KD[:, c, 2:3], None, ALU.is_equal)
                        v.drain()
                        v.sem_inc(s_ohm, 1)
                        v.wait_ge(s_mm, g * (nx // NXT) + b + 1)
                        v.tensor_tensor(tot[:], tot[:], PS[:, 0, 0:500], ALU.add)
                    v.drain()
                    v.wait_ge(s_st, g * 64 + 1)
                    v.tensor_copy(dc(part[:, 0, 0:400]), tot[:, 0:400].rearrange("p (d c) -> p d c", d=GRG))
                    v.tensor_copy(dc(part[:, 0, 400:500]), tot[:, 400:500].rearrange("p (d c) -> p d c", d=GRG))
                    v.drain()
                    for a, b in ((0, 400), (400, 500)):
                        v.tensor_tensor(dc(part[:, 1, a:b]), tot[:, a:b].rearrange("p (d c) -> p d c", d=GRG),
                                        dc(part[:, 0, a:b]), ALU.subtract)
                    v.tensor_tensor(gbk[:], gbk[:], gst[:], ALU.add)
                    v.drain()
                    v.sem_inc(s_cut, 1)

            def count(p, j=j, s_ohm=s_ohm, s_mm=s_mm):
                with p.Fori(0, GEN[j]) as g:
                    with p.Fori(0, nx // NXT) as b:
                        p.wait_ge(s_ohm, g * (nx // NXT) + b + 1)
                        for c in range(NXT):
                            mm = p.matmul(PS[:, 0, 0:500], OG[:, c, 500:628], OG[:, c, 0:500],
                                          start=(c == 0), stop=(c == NXT - 1))
                        mm.then_inc(s_mm, 1)

            def store(a, j=j, s_cut=s_cut, s_st=s_st):
                a.sem_inc(s_st, 1)
                with a.Fori(0, GEN[j]) as g:
                    a.wait_ge(s_cut, g + 1)
                    for i, (ta, tc) in enumerate(((AT[j], AC), (AT2[j], AC2))):
                        a.dma_start(ta[:, :, bass.ds(g * GRG, GRG)],
                                    part[:, i, 0:400].rearrange("p (c d) -> p c d", d=GRG)).then_inc(s_st, 16)
                        a.dma_start(tc[:, :, bass.ds(g * GRG + 512 * j, GRG)].rearrange("h l d -> l h d"),
                                    part[:, i, 400:500].rearrange("p (c d) -> p c d", d=GRG)).then_inc(s_st, 16)
                    a.wait_ge(s_st, g * 64 + 65)

            P.barrier()
            P.raw("dve", hot)
            P.raw("pe", count)
            P.raw("act", store)
            s_j = P._sem(f"g_end{j}")
            P.n[f"g_end{j}"] += 1
            P.raw("act", lambda a, s_j=s_j: a.sem_inc(s_j, 1))
            P.barrier()
        t = sp("kall", dpi[:, 0, :], dst[0:EP].rearrange("(p i) -> p i", p=128))
        t1 = dve(lambda v: v.tensor_scalar(dpi[:, 1, :], dpi[:, 0, :], 7, None, ALU.logical_shift_right), t)
        t1 = dve(lambda v: v.tensor_copy(dpl[:, 1, :], dpi[:, 1, :]), t1)
        t1 = dve(lambda v: v.tensor_scalar(dpi[:, 0, :], dpi[:, 0, :], 127, None, ALU.bitwise_and), t1)
        dve(lambda v: v.tensor_copy(dpl[:, 0, :], dpi[:, 0, :]), t1)
        dve(lambda v: v.memset(net[:, NB:2 * NB], 0.0))

        def into():
            for c in range(8):
                col = lambda a, c=c: a[:, bass.ds(P.it * 8 + c, 1)]
                dve(lambda v, c=c, col=col: v.tensor_tensor(
                    wsd[:, c, :], iof[:], col(dpl[:, 0, :]).broadcast_to([128, 128]), ALU.is_equal))
                t = dve(lambda v, c=c, col=col: v.tensor_tensor(
                    wsh[:, c, :], iof[:, 0:NB], col(dpl[:, 1, :]).broadcast_to([128, NB]), ALU.is_equal))
                t = dve(lambda v, c=c, col=col: v.tensor_tensor(
                    wsh[:, c, :], wsh[:, c, :], col(kall[:, 0:EC, 3]).broadcast_to([128, NB]), ALU.mult), t)
                tm = pe(lambda p, c=c: p.matmul(PS[:, 0, 0:NB], wsd[:, c, :], wsh[:, c, :],
                                                start=(c == 0), stop=(c == 7)), t)
            dve(lambda v: v.tensor_tensor(net[:, NB:2 * NB], net[:, NB:2 * NB], PS[:, 0, 0:NB], ALU.add), tm)

        P.loop(EC // 8, "gw_", ("pe", "dve"), into)
        q.close()


    hT = sb("hT", [128, NP])

    P.general(general_build)
    hA = sb("hA", [128, NP])
    hB = sb("hB", [128, NP])

    def to_cols(rows, dst_T, *w):
        last = {}
        for j in range(NT):
            for q in range(tile_w(j) // 128):
                t = pe(lambda p, j=j, q=q: p.transpose(PS[:, j % 4, 128 * q:128 * q + 128],
                                                       rows[:, 4 * j + q, :], ident[:]),
                       *w, last.get(j - 4))
            last[j] = act(lambda s, j=j: s.copy(dst_T[:, 512 * j:512 * j + tile_w(j)],
                                                PS[:, j % 4, 0:tile_w(j)]), t)
        return last[NT - 1]

    def layernorm(rows, t1, t2, *w):
        m, r = t2[:, 0, :], t2[:, 1, :]
        bc = lambda a: a.unsqueeze(2).broadcast_to([128, NB, D])
        t = dve(lambda v: v.tensor_reduce(m, rows[:], AX, ALU.add), *w)
        t = dve(lambda v: v.tensor_scalar(m, m, 1.0 / D, None, ALU.mult), t)
        t = dve(lambda v: v.tensor_tensor(rows[:], rows[:], bc(m), ALU.subtract), t)
        t = act(lambda s: s.square(t1[:], rows[:]), t)
        t = dve(lambda v: v.tensor_reduce(r, t1[:], AX, ALU.add), t)
        t = act(lambda s: s.activation(r, r, ACT.Sqrt, bias=epst[:], scale=1.0 / D), t)
        t = dve(lambda v: v.reciprocal(r, r), t)
        return dve(lambda v: v.tensor_tensor(rows[:], rows[:], bc(r), ALU.mult), t)

    to_cols(xr, hA)
    P.barrier()
    SMAX = 16384.0
    STEP = 2.0 ** 60

    def gat(l, hin, hout, W, a_s, a_d, bias):
        last = l == 3
        C = 128 if last else 32
        C1 = C + 1
        F = H * C
        g = ExitStack()
        Wt = sb(f"W{l}", [128, F + 8], F32, g)
        bcol = sb(f"bc{l}", [128, 128 if last else 1], F32, g)
        acol = sb(f"ac{l}", [128, NB, 8], F32, g)
        rows = sb(f"ro{l}", [128, NB, 128], F32, g)
        red = sb(f"re{l}", [128, 16], F32, g)
        G = sb(f"G{l}", [128, 16], F32, g)
        rng = sb(f"rn{l}", [128, 8], F32, g)
        rng_i = range_i[:, l - 1:l]
        m = ExitStack()
        if last:
            y = sb("y3", [128, NB, H, C1], F32, m)
        else:
            Y = sb(f"Y{l}", [128, NB, H, 4 * C1], F16, m)
            Cy = sb(f"Cy{l}", [128, NB, 2, H, C1], F16, m)
            nega = sb(f"na{l}", [128, NB, 4], F32, m)
            a60 = sb(f"a6{l}", [128, NB, 4], F32, m)
            qd = sb(f"qd{l}", [128, NB, 4], F32, m)
        brow = sb(f"br{l}", [128, H, NP], F32, m)
        w1 = sb(f"w1{l}", [128, NB, 4], F32, m)
        w0 = sb(f"w0{l}", [128, NB, 4], F32, m)
        u = ExitStack()
        ab = sb(f"ab{l}", [128, 2, F], F32, u)
        tmp = sb(f"tmp{l}", [128, F], F32, u)
        wrep = sb(f"wr{l}", [128, H, 128], F32, u)
        dif = sb(f"df{l}", [128, NB, 4], F32, u)
        if not last:
            xp = sb(f"xp{l}", [128, NB, H, C], F32, u)
            xk = sb(f"xk{l}", [128, NB, H], F32, u)
            yf = [sb(f"yf{l}{i}", [128, NB, H, C1], F32, u) for i in range(2)]
            xa = yf[0][:, :, :, 0:C]

        if last:
            sp("gw", bcol[:], bias.partition_broadcast(128))
        else:
            sp("gw", bcol[:], bias.rearrange("(p o) -> p o", o=1))
        sp("gw", Wt[:, 0:F], W)
        sp("gw", ab[:, 0, :], a_s.rearrange("h c -> (h c)").partition_broadcast(128))
        t = sp("gw", ab[:, 1, :], a_d.rearrange("h c -> (h c)").partition_broadcast(128))
        for s in range(2):
            t1 = dve(lambda v, s=s: v.tensor_tensor(tmp[:], Wt[:, 0:F], ab[:, s, :], ALU.mult), t)
            t = dve(lambda v, s=s: v.tensor_reduce(Wt[:, F + 4 * s:F + 4 * s + 4],
                                                   tmp.rearrange("p (h c) -> p h c", h=H), AX, ALU.add), t1)
        t_wa = t
        t_wr = dve(lambda v: v.tensor_copy(
            wrep[:], Wt[:, F + 4:F + 8].unsqueeze(2).broadcast_to([128, H, 128])), t_wa)
        e = {}
        if last:
            for k in range(NB):
                t = pe(lambda p, k=k: p.matmul(PS[:, 0, 8 * k:8 * k + 8], hin[:, 128 * k:128 * k + 128],
                                               Wt[:, F:F + 8], start=True, stop=True), t_wa)
            t_ac = act(lambda s: s.copy(acol.rearrange("p k h -> p (k h)"), PS[:, 0, 0:8 * NB]), t)
        else:
            for j in range(0, NB, 3):
                nb = min(3, NB - j)
                b = j // 3 % 4
                for i in range(nb):
                    t = pe(lambda p, i=i, j=j, b=b: p.matmul(
                        PS[:, b, 136 * i:136 * i + 136], hin[:, 128 * (i + j):128 * (i + j) + 128], Wt[:],
                        start=True, stop=True), t_wa, e.get(j - 12))
                psv = PS[:, b, 0:136 * nb].rearrange("p (k c) -> p k c", c=136)
                t_ac = act(lambda s, j=j, nb=nb, psv=psv: s.copy(acol[:, j:j + nb, :], psv[:, :, F:F + 8]), t)
                e[j] = act(lambda s, j=j, nb=nb, psv=psv: s.copy(
                    xp[:, j:j + nb].rearrange("p k h c -> p k (h c)"), psv[:, :, 0:F]))
            t_xp = e[j]
        t1 = dve(lambda v: v.tensor_reduce(red[:, 0:4], acol[:, :, 0:4].rearrange("p k h -> p h k"), AX, ALU.max),
                 t_ac)
        na = dif if last else nega
        t = dve(lambda v: v.tensor_scalar(na[:], acol[:, :, 0:4], -1.0, None, ALU.mult), t_ac)
        t = dve(lambda v: v.tensor_reduce(red[:, 4:8], na.rearrange("p k h -> p h k"), AX, ALU.max), t)
        nred = 8
        if not last:
            nred = 12
            t = act(lambda s: s.activation(xa, xp[:], ACT.Abs), t_xp)
            t = dve(lambda v: v.tensor_reduce(xk[:], xa, AX, ALU.max), t)
            t = dve(lambda v: v.tensor_reduce(red[:, 8:12], xk.rearrange("p k h -> p h k"), AX, ALU.max), t)
        t_G = pool(lambda q: q.partition_all_reduce(G[:, 0:nred], red[:, 0:nred], 128, bass.bass_isa.ReduceOp.max),
                   t, t1)
        t = dve(lambda v: v.tensor_tensor(rng[:, 0:4], G[:, 0:4], G[:, 4:8], ALU.add), t_G)
        t = dve(lambda v: v.tensor_scalar(rng[:, 0:4], rng[:, 0:4], 80.0 if last else 12.0, None, ALU.is_gt), t)
        t = dve(lambda v: v.tensor_reduce(rng[:, 4:5], rng[:, 0:4], AX, ALU.max), t)
        t = dve(lambda v: v.tensor_tensor(rng[:, 4:5], rng[:, 4:5], flag[:, 3:4], ALU.max), t)
        t_fl = dve(lambda v: v.tensor_copy(rng_i, rng[:, 4:5]), t)
        bh = lambda a: a.unsqueeze(1).broadcast_to([128, NB, 4])
        t = dve(lambda v: v.tensor_tensor(dif[:], acol[:, :, 0:4], bh(G[:, 0:4]), ALU.subtract), t_G)
        t = dve(lambda v: v.tensor_scalar(dif[:], dif[:], -80.0, None, ALU.max), t)
        t_w1 = act(lambda s: s.activation(w1[:], dif[:], ACT.Exp, scale=0.8 if last else 1.0), t)
        t_w0 = act(lambda s: s.activation(w0[:], dif[:], ACT.Exp, scale=0.2), t)
        eb = {}
        n = 0
        for h in range(H):
            for j in range(NT):
                wd = tile_w(j)
                cs = slice(512 * j, 512 * j + wd)
                b = 4 + n % 4
                t = pe(lambda p, h=h, cs=cs, b=b, wd=wd: p.matmul(
                    PS[:, b, 0:wd], wrep[:, h, :], hin[:, cs], start=True, stop=True), t_wr, eb.get(n - 4))
                if last:
                    eb[n] = dve(lambda v, h=h, cs=cs, b=b, wd=wd: v.tensor_scalar(
                        brow[:, h, cs], PS[:, b, 0:wd], G[:, h:h + 1], 0.0, ALU.add, ALU.max), t, t_G)
                elif n % 2:
                    eb[n] = dve(lambda v, h=h, cs=cs, b=b, wd=wd: v.tensor_copy(brow[:, h, cs], PS[:, b, 0:wd]), t)
                else:
                    eb[n] = act(lambda s, h=h, cs=cs, b=b, wd=wd: s.copy(brow[:, h, cs], PS[:, b, 0:wd]), t)
                n += 1
            if last:
                eb["q", h] = act(lambda s, h=h: s.activation(brow[:, h, :], brow[:, h, :], ACT.Exp, scale=-0.8),
                                 eb[n - 1])
        t_br = [eb["q", H - 1]] if last else [eb[n - 1], eb[n - 2]]
        bc = lambda a, c: a.unsqueeze(3).broadcast_to([128, NB, H, c])
        if last:
            e = {}
            for k in range(NB):
                t = pe(lambda p, k=k: p.matmul(PS[:, 1 + k % 3, :], hin[:, 128 * k:128 * k + 128], Wt[:, 0:F],
                                               start=True, stop=True), t_wa, e.get(k - 3))
                e[k] = dve(lambda v, k=k: v.tensor_tensor(
                    y[:, k, :, 0:C], PS[:, 1 + k % 3, :].rearrange("p (h c) -> p h c", h=H),
                    w0[:, k, :].unsqueeze(2).broadcast_to([128, H, C]), ALU.mult), t, t_w0)
            t_y = [e[NB - 1], act(lambda s: s.copy(y[:, :, :, C], w0[:]), t_w0)]
        else:
            t = dve(lambda v: v.tensor_tensor(qd[:], acol[:, :, 4:8], bh(G[:, 0:4]), ALU.add), t_G)
            t = dve(lambda v: v.tensor_scalar(qd[:], qd[:], 0.0, None, ALU.max), t)
            t_qd = act(lambda s: s.activation(qd[:], qd[:], ACT.Exp, scale=-0.8), t)
            t_60 = dve(lambda v: v.tensor_scalar(a60[:], acol[:, :, 0:4], STEP, None, ALU.mult))
            t = dve(lambda v: v.tensor_scalar(G[:, 8:12], G[:, 8:12], 1e-30, None, ALU.max))
            t = dve(lambda v: v.reciprocal(red[:, 8:12], G[:, 8:12]), t)
            t = dve(lambda v: v.tensor_scalar(red[:, 8:12], red[:, 8:12], SMAX, None, ALU.mult), t)
            t_y = []
            t_fx = None
            for i, (w, tw) in enumerate(((w0, t_w0), (w1, t_w1))):
                t1 = act(lambda s, w=w, i=i: s.mul(yf[i][:, :, :, C], w[:], SMAX), tw)
                t2 = dve(lambda v, w=w, i=i: v.tensor_tensor(w[:], w[:], bh(red[:, 8:12]), ALU.mult), t, t1)
                t2 = dve(lambda v, w=w, i=i: v.tensor_tensor(yf[i][:, :, :, 0:C], xp[:], bc(w[:], C), ALU.mult), t2)
                hi, lo = (Cy[:, :, 0], Cy[:, :, 1]) if i == 0 else (Y[:, :, :, 0:C1], Y[:, :, :, C1:2 * C1])
                t2 = act(lambda s, i=i, hi=hi: s.copy(hi, yf[i][:]), t1, t2)
                t3 = dve(lambda v, i=i, hi=hi, lo=lo: v.tensor_tensor(lo, yf[i][:], hi, ALU.subtract), t2)
                t_y.append(t3)
                if i == 0:
                    t_y.append(act(lambda s: s.mul(Y[:, :, :, 2 * C1:3 * C1], Cy[:, :, 0], -1.0), t2))
                    t_y.append(pool(lambda q: q.tensor_scalar(Y[:, :, :, 3 * C1:4 * C1], Cy[:, :, 1], -1.0, None,
                                                              ALU.mult), t3))
        P.barrier()
        u.close()

        ring = sb(f"cr{l}", [128, 30, 512], F16, m)
        if last:
            NM = 6
            Mb = [hout[:, 512 * i:512 * i + 512] for i in range(NM)]
            rc = sb("rc3", [128, 4], F32, m)
        else:
            NM = 8
            Mb = [sb(f"Mb{l}{i}", [128, 512], F16, m) for i in range(NM)]
            Sg = [sb(f"Sg{l}{i}", [128, 512], F16, m) for i in range(4)]
            ev = hout[:, 0:96 * C1].rearrange("p (d c) -> p d c", d=4)
            sa = sb(f"sa{l}", [128, 4, 8, C1], F32, m)
            sc = sb(f"sc{l}", [128, 4, 4, C1], F32, m)
            rc = sb(f"rc{l}", [128, 4, 4], F32, m)
        n = ns = 0
        t_c, c_free, m_free, s_free = {}, {}, {}, {}
        b_free = {}
        ev_free = None

        def drain(j, t):
            nb = tile_w(j) // 128
            if last:
                for d in range(nb):
                    for s in range(2):
                        t1 = dve(lambda v, d=d, s=s: v.reciprocal(
                            rc[:, 2 * s:2 * s + 2],
                            PS[:, 2 * d + s, 0:2 * C1].rearrange("p (h c) -> p h c", h=2)[:, :, C]), t, b_free.get("rc"))
                    for h in range(H):
                        src_ = PS[:, 2 * d + h // 2, C1 * (h % 2):C1 * (h % 2) + C]
                        o = rows[:, 4 * j + d, :]
                        if h == 0:
                            t1 = dve(lambda v, o=o, src_=src_, h=h: v.tensor_scalar(
                                o, src_, rc[:, h:h + 1], None, ALU.mult), t1)
                        else:
                            t1 = dve(lambda v, o=o, src_=src_, h=h: v.scalar_tensor_tensor(
                                out=o, in0=src_, scalar=rc[:, h:h + 1], in1=o, op0=ALU.mult, op1=ALU.add), t1)
                    b_free[2 * d] = b_free[2 * d + 1] = b_free["rc"] = t1
                return
            tv = []
            for d in range(nb):
                b_free[2 * d + 1] = act(lambda s, d=d: s.copy(ev[:, d, 12 * C1:24 * C1], PS[:, 2 * d + 1, 0:12 * C1]),
                                        t, b_free.get("ev"))
                b_free[2 * d] = dve(lambda v, d=d: v.tensor_copy(ev[:, d, 0:12 * C1], PS[:, 2 * d, 0:12 * C1]),
                                    t, b_free.get("ev"))
                tv += [b_free[2 * d], b_free[2 * d + 1]]
            mv = ev[:, 0:nb, 0:16 * C1].rearrange("p d (g s c) -> p d g s c", s=2, c=C1)
            cv = ev[:, 0:nb, 16 * C1:24 * C1].rearrange("p d (s h c) -> p d s h c", s=2, c=C1)
            mg = sa[:, 0:nb].rearrange("p d (h g) c -> p d h g c", g=2)
            scv = sc[:, 0:nb]
            qv = qd[:, 4 * j:4 * j + nb, :].unsqueeze(3).broadcast_to([128, nb, 4, C1])
            xm = G[:, 8:12].unsqueeze(1).broadcast_to([128, nb, 4])
            for d in range(nb):
                t1 = pool(lambda q, d=d: q.tensor_tensor(sa[:, d], mv[:, d, :, 0, :], mv[:, d, :, 1, :], ALU.add),
                          tv, b_free.get("hr"))
                t2 = pool(lambda q, d=d: q.tensor_tensor(scv[:, d], cv[:, d, 0], cv[:, d, 1], ALU.add))
            b_free["ev"] = t2
            for d in range(nb):
                t2 = pool(lambda q, d=d: q.tensor_tensor(scv[:, d], scv[:, d], mg[:, d, :, 1, :], ALU.add), t1, t2)
            t2 = pool(lambda q: q.tensor_tensor(scv, scv, qv, ALU.mult), t2)
            for d in range(nb):
                t3 = pool(lambda q, d=d: q.tensor_tensor(scv[:, d], scv[:, d], mg[:, d, :, 0, :], ALU.add), t2)
            t1 = dve(lambda v: v.reciprocal(rc[:, 0:nb], sc[:, 0:nb, :, C]), t3)
            t1 = dve(lambda v: v.tensor_tensor(rc[:, 0:nb], rc[:, 0:nb], xm, ALU.mult), t1)
            b_free["hr"] = pool(lambda q: q.tensor_tensor(
                rows[:, 4 * j:4 * j + nb, :].rearrange("p d (h c) -> p d h c", h=4), sc[:, 0:nb, :, 0:C],
                rc[:, 0:nb].unsqueeze(3).broadcast_to([128, nb, 4, C]), ALU.mult), t1)

        prev = None
        for j in range(NT):
            wd = tile_w(j)
            nb = wd // 128
            cs = slice(512 * j, 512 * j + wd)
            for i in range(NB):
                ci = 5 * j + i // 5
                if i % 5 == 0:
                    t_c[ci] = sp(f"cr{ci % 6}", ring[:, 5 * (ci % 6):5 * (ci % 6) + 5, 0:wd],
                                 AC[i:i + 5, :, cs].rearrange("k l d -> l k d"), c_free.get(ci - 6))
                cb = ring[:, 5 * (ci % 6) + i % 5, 0:wd]
                ms = []
                for h in range(H):
                    mb = Mb[n % NM]
                    if last:
                        tm = dve(lambda v, mb=mb, i=i, h=h, cs=cs, cb=cb, wd=wd: v.scalar_tensor_tensor(
                            out=mb[:, 0:wd], in0=brow[:, h, cs], scalar=w1[:, i, h:h + 1], in1=cb,
                            op0=ALU.max, op1=ALU.mult), t_c[ci], m_free.get(n - NM))
                    elif h < 2:
                        tm = dve(lambda v, mb=mb, i=i, h=h, cs=cs, cb=cb, wd=wd: v.scalar_tensor_tensor(
                            out=mb[:, 0:wd], in0=brow[:, h, cs], scalar=nega[:, i, h:h + 1], in1=cb,
                            op0=ALU.is_gt, op1=ALU.mult), t_c[ci], m_free.get(n - NM))
                    else:
                        sg = Sg[ns % 4]
                        ts = act(lambda s, sg=sg, i=i, h=h, cs=cs, wd=wd: s.activation(
                            sg[:, 0:wd], brow[:, h, cs], ACT.Sigmoid, bias=a60[:, i, h:h + 1], scale=STEP),
                            s_free.get(ns - 4))
                        tm = s_free[ns] = dve(lambda v, mb=mb, sg=sg, cb=cb, wd=wd: v.tensor_tensor(
                            mb[:, 0:wd], sg[:, 0:wd], cb, ALU.mult), ts, t_c[ci], m_free.get(n - NM))
                        ns += 1
                    ms.append((n, mb, tm))
                    n += 1
                if i == 0 and j:
                    drain(j - 1, prev)
                st = dict(start=False, stop=(i == NB - 1), skip_group_check=True)
                first = dict(st, start=(i == 0))
                if not last:
                    for d in range(nb):
                        pe(lambda p, d=d, cb=cb, i=i, kw=first: p.matmul(
                            PS[:, 2 * d + 1, 4 * C1:12 * C1], cb[:, 128 * d:128 * d + 128],
                            Cy[:, i].rearrange("p s h c -> p (s h c)"), **kw),
                            t_c[ci], b_free.get(2 * d + 1) if i == 0 else None)
                for h, (nn, mb, tm) in enumerate(ms):
                    for d in range(nb):
                        mblk = mb[:, 128 * d:128 * d + 128]
                        if last:
                            o, kw, mv_ = PS[:, 2 * d + h // 2, C1 * (h % 2):C1 * (h % 2) + C1], \
                                (st if h % 2 else first), y[:, i, h, :]
                        else:
                            o, kw, mv_ = PS[:, 2 * d, 4 * C1 * h:4 * C1 * h + 4 * C1] if h < 3 \
                                else PS[:, 2 * d + 1, 0:4 * C1], (st if h else first), Y[:, i, h, :]
                        t = pe(lambda p, o=o, mblk=mblk, mv_=mv_, kw=kw: p.matmul(o, mblk, mv_, **kw),
                               tm, b_free.get(2 * d) if i == 0 else None,
                               b_free.get(2 * d + 1) if i == 0 else None)
                    m_free[nn] = t
                prev = t
                if i % 5 == 4:
                    c_free[ci] = t
        drain(NT - 1, prev)
        P.barrier()
        m.close()

        def exact():
            q = ExitStack()
            xq = sb(f"xq{l}", [128, NB, F], F32, q)
            arow = sb(f"aw{l}", [128, H, NP], F32, q)
            wq = sb(f"wq{l}", [128, H, 128], F32, q)
            SG = sb(f"sg{l}", [128, NB, 128], F16, q)
            ct = sb(f"ct{l}", [128, NP], F32, q)
            T = hout
            U = sb(f"U{l}", [128, NP], F32, q)
            cur = sb(f"cu{l}", [128, 8], F32, q)
            sm = sb(f"sm{l}", [128, 4], F32, q)

            def zeros():
                zer = SG.rearrange("p a b -> p (a b)")
                t = dve(lambda v: v.memset(zer, 0.0))
                for k in range(NB):
                    sp("z", AC2[k], zer, t)

            P.general(zeros, f"z{l}_", "plain")
            t = dve(lambda v: v.tensor_copy(wq[:], Wt[:, F:F + 4].unsqueeze(2).broadcast_to([128, H, 128])))
            e = None
            for h in range(H):
                for j in range(NT):
                    cs = slice(512 * j, 512 * j + tile_w(j))
                    t1 = pe(lambda p, h=h, j=j, cs=cs: p.matmul(PS[:, 0, 0:tile_w(j)], wq[:, h, :], hin[:, cs],
                                                                start=True, stop=True), t, e)
                    e = dve(lambda v, h=h, j=j, cs=cs: v.tensor_copy(arow[:, h, cs], PS[:, 0, 0:tile_w(j)]), t1)
            for k in range(NB):
                t1 = pe(lambda p, k=k: p.matmul(PS[:, 0, 0:F], hin[:, 128 * k:128 * k + 128], Wt[:, 0:F],
                                                start=True, stop=True), e)
                e = dve(lambda v, k=k: v.tensor_copy(xq[:, k, :], PS[:, 0, 0:F]), t1)

            def block():
                at = lambda tab: lambda: tab[:, :, bass.ds(P.it * 128, 128)].rearrange("h l d -> l h d")
                e = None
                for i, tab in enumerate((AC, AC2)):
                    t = P.dma("act", f"sg{i}", SG[:], at(tab), e)
                    for c in range(NB):
                        t1 = pe(lambda p, c=c, i=i: p.transpose(
                            PST[:, c // 8, 128 * (c % 8):128 * (c % 8) + 128], SG[:, c, :], identh[:]), t, e)
                    pv = PST.rearrange("p b c -> p (b c)")[:, 0:NP]
                    if i == 0:
                        e = dve(lambda v, pv=pv: v.tensor_copy(ct[:], pv), t1)
                    else:
                        e = dve(lambda v, pv=pv: v.tensor_tensor(ct[:], ct[:], pv, ALU.add), t1, e)
                t_cu = dve(lambda v: v.tensor_copy(
                    cur[:].unsqueeze(1), acol[:, bass.ds(P.it, 1), :]))
                end = None
                for h in range(H):
                    b = cur[:, 4 + h:5 + h]
                    t_mk = dve(lambda v: v.tensor_scalar(U[:], ct[:], 0.0, BIG, ALU.is_equal, ALU.mult), e, end)
                    t = dve(lambda v, h=h: v.tensor_tensor(T[:], U[:], arow[:, h, :], ALU.add), t_mk, t_cu, end)
                    t = dve(lambda v: v.tensor_reduce(sm[:, 0:1], T[:], AX, ALU.max), t)
                    t = dve(lambda v, b=b: v.tensor_tensor(sm[:, 0:1], sm[:, 0:1], b, ALU.add), t)
                    tm = dve(lambda v: v.scalar_tensor_tensor(
                        out=sm[:, 1:2], in0=sm[:, 0:1], scalar=0.2, in1=sm[:, 0:1], op0=ALU.mult, op1=ALU.max), t)
                    t = dve(lambda v, h=h, b=b: v.tensor_scalar(T[:], arow[:, h, :], b, None, ALU.add), tm)
                    t = dve(lambda v: v.scalar_tensor_tensor(
                        out=T[:], in0=T[:], scalar=0.2, in1=T[:], op0=ALU.mult, op1=ALU.max), t)
                    t = dve(lambda v: v.tensor_scalar(T[:], T[:], sm[:, 1:2], 0.0, ALU.subtract, ALU.min), t)
                    t = act(lambda s: s.activation(T[:], T[:], ACT.Exp), t)
                    t_p = dve(lambda v: v.tensor_tensor(T[:], T[:], ct[:], ALU.mult), t)
                    t = dve(lambda v: v.tensor_reduce(sm[:, 2:3], T[:], AX, ALU.add), t_p)
                    t_r = dve(lambda v: v.reciprocal(sm[:, 3:4], sm[:, 2:3]), t)
                    ec = {}
                    for j in range(NT):
                        for d in range(tile_w(j) // 128):
                            t = pe(lambda p, j=j, d=d: p.transpose(
                                PS[:, j % 2, 128 * d:128 * d + 128], T[:, 512 * j + 128 * d:512 * j + 128 * d + 128],
                                ident[:]), t_p, ec.get(j - 2))
                        ec[j] = act(lambda s, j=j: s.copy(U[:, 512 * j:512 * j + tile_w(j)],
                                                          PS[:, j % 2, 0:tile_w(j)]), t)
                    for k in range(NB):
                        t = pe(lambda p, k=k, h=h: p.matmul(
                            PS[:, 2, 0:C], U[:, 128 * k:128 * k + 128], xq[:, k, C * h:C * h + C],
                            start=(k == 0), stop=(k == NB - 1)), ec[NT - 1], end)
                    if last and h:
                        end = dve(lambda v: v.scalar_tensor_tensor(
                            out=rows[:, bass.ds(P.it, 1), :], in0=PS[:, 2, 0:C].unsqueeze(1), scalar=sm[:, 3:4],
                            in1=rows[:, bass.ds(P.it, 1), :], op0=ALU.mult, op1=ALU.add), t, t_r)
                    else:
                        end = dve(lambda v, h=h: v.tensor_scalar(
                            rows[:, bass.ds(P.it, 1), 0 if last else C * h:C if last else C * h + C],
                            PS[:, 2, 0:C].unsqueeze(1), sm[:, 3:4], None, ALU.mult), t, t_r)

            P.loop(NB, f"b{l}_", ("pe", "dve", "act"), block)
            q.close()

        load_flag(f"range{l}", rng_i, 0, t_fl)
        P.general(exact, f"x{l}_", f"range{l}")
        if not last:
            lastj = {}
            for j in range(NT):
                for q in range(tile_w(j) // 128):
                    t = pe(lambda p, j=j, q=q: p.transpose(
                        PS[:, j % 4, 128 * q:128 * q + 128], rows[:, 4 * j + q, :], ident[:]), lastj.get(j - 4))
                lastj[j] = act(lambda s, j=j: s.activation(
                    hout[:, 512 * j:512 * j + tile_w(j)], PS[:, j % 4, 0:tile_w(j)], ACT.Relu, bias=bcol[:]), t)
        else:
            t = dve(lambda v: v.scalar_tensor_tensor(out=xr[:], in0=rows[:], scalar=0.25, in1=xr[:],
                                                     op0=ALU.mult, op1=ALU.add))
            dve(lambda v: v.tensor_tensor(xr[:], xr[:], bcol[:].unsqueeze(1).broadcast_to([128, NB, D]), ALU.add), t)
        P.barrier()
        g.close()

    gat(1, hA, hB, W1, as1, ad1, b1)
    gat(2, hB, hA, W2, as2, ad2, b2)
    gat(3, hA, hB, W3, as3, ad3, b3)
    hT = hA

    pd = ExitStack()
    ln1 = sb("ln1", [128, NB, D], F32, pd)
    ln2 = sb("ln2", [128, 2, NB], F32, pd)
    mr = sb("mr", [128, NB, D], F32, pd)

    def split(rows, hi, lo, *w):
        t = act(lambda s: s.mul(hi[:], rows[:], SC), *w)
        return dve(lambda v: v.scalar_tensor_tensor(out=lo[:], in0=rows[:], scalar=SC, in1=hi[:],
                                                    op0=ALU.mult, op1=ALU.subtract), t)

    q = ExitStack()
    hh = [sb(f"hh{i}", [128, NB, D], F16, pd) for i in range(2)]
    hl = [sb(f"hl{i}", [128, NB, D], F16, pd) for i in range(2)]
    w1t = sb("w1t", [128, 512], F32, q)
    w2t = sb("w2t", [128, 4, 128], F32, q)
    b1c = sb("b1c", [128, 4], F32, q)
    rowb = sb("rowb", [128, 3, 128], F32, q)
    uT = sb("uT", [128, NP], F32, q)
    Cf = [sb(f"Cf{i}", [128, NP], F16, q) for i in range(4)]
    hid = [sb(f"hid{i}", [128, 4, 512], F32, q) for i in range(2)]
    sp("l1w", w1t[:], mw1)
    sp("l1w", w2t[:], mw2.rearrange("(c p) d -> p c d", p=128))
    sp("l1w", b1c[:], mb1)
    for i, a in enumerate((mb2, gamma, beta)):
        t_l1 = sp("l1w", rowb[:, i, :], a.partition_broadcast(128))
    t = layernorm(xr, ln1, ln2)
    t_x1 = t
    t_sp = split(xr, hh[0], hl[0], t)
    t_xT = to_cols(xr, hT, t_x1)
    free = {}
    first = t_xT
    for k in range(NB):
        tc = sp(f"cf{k % 4}", Cf[k % 4][:], AC[k], free.get(k - 4))
        for a, part in enumerate((hh[0], hl[0])):
            for j in range(NT):
                wd = tile_w(j)
                t = pe(lambda p, k=k, j=j, wd=wd, part=part, a=a: p.matmul(
                    PS[:, j, 0:wd], part[:, k, :], Cf[k % 4][:, 512 * j:512 * j + wd],
                    start=(k == 0 and a == 0), stop=(k == NB - 1 and a == 1)), tc, t_sp, first)
        free[k] = t

    def rest1():
        t = None
        for k in range(NB):
            tc = sp("cf", Cf[0][:], AC2[k], t)
            for part in (hh[0], hl[0]):
                for j in range(NT):
                    t = pe(lambda p, k=k, j=j, part=part: p.matmul(
                        PS[:, j, 0:tile_w(j)], part[:, k, :], Cf[0][:, 512 * j:512 * j + tile_w(j)],
                        start=False, stop=True, skip_group_check=True), tc)

    P.general(rest1)
    t_u = {}
    for j in range(NT):
        wd = tile_w(j)
        t_u[j] = dve(lambda v, j=j, wd=wd: v.scalar_tensor_tensor(
            out=uT[:, 512 * j:512 * j + wd], in0=PS[:, j, 0:wd], scalar=1.0 / SC, in1=hT[:, 512 * j:512 * j + wd],
            op0=ALU.mult, op1=ALU.subtract), t)
    e = {}
    eh = {}
    eo = {}
    n = 0
    for j in range(NT):
        wd = tile_w(j)
        nb = wd // 128
        for c in range(4):
            t = pe(lambda p, j=j, c=c, wd=wd, b=n % 4: p.matmul(
                PS[:, b, 0:wd], w1t[:, 128 * c:128 * c + 128], uT[:, 512 * j:512 * j + wd],
                start=True, stop=True), t_u[NT - 1], t_l1, e.get(n - 4))
            e[n] = act(lambda s, j=j, c=c, wd=wd, b=n % 4: s.activation(
                hid[j % 2][:, c, 0:wd], PS[:, b, 0:wd], ACT.Relu, bias=b1c[:, c:c + 1]), t, eh.get(j - 2))
            n += 1
        for qq in range(nb):
            for c in range(4):
                t = pe(lambda p, j=j, qq=qq, c=c: p.matmul(
                    PS[:, 4 + j % 2, 128 * qq:128 * qq + 128], hid[j % 2][:, c, 128 * qq:128 * qq + 128],
                    w2t[:, c, :], start=(c == 0), stop=(c == 3)), e[n - 1], eo.get(j - 2))
        eh[j] = t
        t = dve(lambda v, j=j, nb=nb: v.tensor_tensor(
            mr[:, 4 * j:4 * j + nb, :], PS[:, 4 + j % 2, 0:128 * nb].rearrange("p (k c) -> p k c", c=128),
            xr[:, 4 * j:4 * j + nb, :], ALU.add), t)
        eo[j] = t
    rb3 = lambda i: rowb[:, i, :].unsqueeze(1).broadcast_to([128, NB, D])
    t = dve(lambda v: v.tensor_tensor(mr[:], mr[:], rb3(0), ALU.add), t)
    t = layernorm(mr, ln1, ln2, t)
    t = dve(lambda v: v.tensor_tensor(mr[:], mr[:], rb3(1), ALU.mult), t)
    t = dve(lambda v: v.tensor_tensor(mr[:], mr[:], rb3(2), ALU.add), t)
    t = dve(lambda v: v.tensor_tensor(xr[:], xr[:], mr[:], ALU.add), t)
    t_x2 = layernorm(xr, ln1, ln2, t)
    P.barrier()
    q.close()

    q = ExitStack()
    wkt = sb("wkt", [128, 6, 128], F32, q)
    wab = sb("wab", [128, 2, 128], F32, q)
    bkb = sb("bkb", [128, 7, 128], F32, q)
    bsum = sb("bsum", [128, 128], F32, q)
    lam = sb("lam", [128, 4], F32, q)
    scl = sb("scl", [128, NB], F32, q)
    t2x = sb("t2x", [128, NB, D], F32, q)
    sp("l2w", wkt[:], Wk.rearrange("k d o -> d k o"))
    sp("l2w", bkb[:, 0:6, :].rearrange("p k o -> p (k o)"), bk.rearrange("k o -> (k o)").partition_broadcast(128))
    t_l2 = sp("l2w", bkb[:, 6, :], cbias.partition_broadcast(128))
    t = dve(lambda v: v.tensor_reduce(bsum[:], bkb.rearrange("p k o -> p o k"), AX, ALU.add), t_l2)
    t = dve(lambda v: v.tensor_tensor(wab[:, 0, :], wkt[:, 0, :], wkt[:, 2, :], ALU.subtract), t)
    for c in (3, 4, 5):
        t = dve(lambda v, c=c: v.scalar_tensor_tensor(out=wab[:, 0, :], in0=wkt[:, c, :], scalar=-float(c - 1),
                                                      in1=wab[:, 0, :], op0=ALU.mult, op1=ALU.add), t)
    t = dve(lambda v: v.scalar_tensor_tensor(out=wab[:, 1, :], in0=wkt[:, 2, :], scalar=2.0,
                                             in1=wkt[:, 1, :], op0=ALU.mult, op1=ALU.add), t)
    for c in (3, 4, 5):
        t = dve(lambda v, c=c: v.scalar_tensor_tensor(out=wab[:, 1, :], in0=wkt[:, c, :], scalar=float(c),
                                                      in1=wab[:, 1, :], op0=ALU.mult, op1=ALU.add), t)
    t_wab = t
    dve(lambda v: v.tensor_reduce(lam[:, 0:1], net[:, 0:NB], AX, ALU.max))
    t = dve(lambda v: v.tensor_scalar(lam[:, 1:2], wmin[:, 0:1], -1.0, None, ALU.mult))
    t = dve(lambda v: v.tensor_tensor(lam[:, 2:3], lam[:, 0:1], lam[:, 1:2], ALU.max), t)
    t = pool(lambda g: g.partition_all_reduce(lam[:, 3:4], lam[:, 2:3], 128, bass.bass_isa.ReduceOp.max), t)
    t = dve(lambda v: v.reciprocal(lam[:, 0:1], lam[:, 3:4]), t)
    t1 = dve(lambda v: v.tensor_tensor(scl[:], net[:, 0:NB], net[:, NB:2 * NB], ALU.subtract))
    t_sc = dve(lambda v: v.tensor_scalar(scl[:], scl[:], lam[:, 0:1], None, ALU.mult), t, t1)
    t_xT = to_cols(xr, hT)
    e = {}
    for j in range(13):
        nb = min(2, NB - 2 * j)
        for qq in range(nb):
            k = 2 * j + qq
            t = pe(lambda p, k=k, qq=qq, j=j: p.matmul(
                PS[:, 4 + j % 4, 256 * qq:256 * qq + 256], hT[:, 128 * k:128 * k + 128],
                wab.rearrange("p a o -> p (a o)"), start=True, stop=True), t_xT, t_wab, e.get(j - 4))
        psv = PS[:, 4 + j % 4, 0:256 * nb].rearrange("p (k a o) -> p k a o", a=2, o=128)
        ks = slice(2 * j, 2 * j + nb)
        t2 = dve(lambda v, psv=psv, ks=ks, nb=nb: v.tensor_tensor(
            t2x[:, ks, :], psv[:, :, 1, :], scl[:, ks].unsqueeze(2).broadcast_to([128, nb, 128]), ALU.mult),
            t, t_sc)
        e[j] = dve(lambda v, psv=psv, ks=ks: v.tensor_tensor(t2x[:, ks, :], t2x[:, ks, :], psv[:, :, 0, :],
                                                             ALU.add), t2)
    t = dve(lambda v: v.tensor_tensor(t2x[:], t2x[:], bsum[:].unsqueeze(1).broadcast_to([128, NB, D]), ALU.add),
            e[12])
    t = dve(lambda v: v.tensor_tensor(xr[:], xr[:], t2x[:], ALU.add), t)
    t = layernorm(xr, ln1, ln2, t)
    P.barrier()
    q.close()

    q = ExitStack()
    wer = sb("wer", [128, 4, 128], F32, q)
    weT = sb("weT", [128, 4, 128], F32, q)
    wir = sb("wir", [128, 2, 3, 128], F32, q)
    wgT = sb("wgT", [128, 2, 3, 128], F32, q)
    bet = sb("bet", [4, 128], F32, q)
    bi = sb("bi", [128, 2, 3], F32, q)
    brz = sb("brz", [128, 2], F32, q)
    sel = sb("sel", [128, 4, 4], F16, q)
    cnt = sb("cnt", [4, NP], F32, q)
    hN = [hT, hB]
    Ab = [sb(f"Ab{i}", [128, NB, 512], F16, q) for i in range(3)]
    ub = [sb(f"ub{i}", [128, 512], F32, q) for i in range(2)]
    mrf = mr.rearrange("p k d -> p (k d)")
    aT, rg, zg, hnb, ng, dd = (mrf[:, 512 * i:512 * i + 512] for i in range(6))

    sp("l3w", wer[:], We.rearrange("t o d -> o t d"))
    sp("l3w", wir[:, 0], Wih.rearrange("(g o) d -> o g d", o=128))
    sp("l3w", wir[:, 1], Whh.rearrange("(g o) d -> o g d", o=128))
    sp("l3w", bet[:], be)
    sp("l3w", bi[:, 0, :], bih)
    t_l3 = sp("l3w", bi[:, 1, :], bhh)
    for i in range(4):
        t = pe(lambda p, i=i: p.transpose(PS[:, 0, 128 * i:128 * i + 128], wer[:, i, :], ident[:]), t_l3)
    act(lambda s: s.copy(weT.rearrange("p t o -> p (t o)"), PS[:, 0, :]), t)
    for a in range(2):
        for i in range(3):
            t = pe(lambda p, a=a, i=i: p.transpose(PS[:, 1 + a, 128 * i:128 * i + 128], wir[:, a, i, :], ident[:]),
                   t_l3)
        t_wg = act(lambda s, a=a: s.copy(wgT[:, a].rearrange("p g o -> p (g o)"), PS[:, 1 + a, 0:384]), t)
    t_brz = dve(lambda v: v.tensor_tensor(brz[:], bi[:, 0, 0:2], bi[:, 1, 0:2], ALU.add), t_l3)
    t = dve(lambda v: v.memset(sel[:], 0.0))
    for i in range(4):
        t_sel = dve(lambda v, i=i: v.memset(sel[:, i, i:i + 1], 1.0), t)
    P.barrier()
    split(xr, hh[0], hl[0])
    to_cols(xr, hT)
    P.barrier()

    n = 0
    a_free = {}
    u_ev = {}
    nu = 0
    t_h = None
    for step in range(4):
        cur, nxt = hN[step % 2], hN[1 - step % 2]
        sh, sl = hh[step % 2], hl[step % 2]
        nh, nl = hh[1 - step % 2], hl[1 - step % 2]
        for j in range(NT):
            wd = tile_w(j)
            cs = slice(512 * j, 512 * j + wd)
            for ty in range(4):
                ab = Ab[n % 3]
                ta = sp(f"ab{n % 3}", ab[:, :, 0:wd], AT[j][:, NB * ty:NB * ty + NB, :], a_free.get(n - 3))
                ubank = nu % 2
                for k in range(NB):
                    for a, part in enumerate((sh, sl)):
                        t = pe(lambda p, ab=ab, k=k, part=part, wd=wd, ubank=ubank, a=a: p.matmul(
                            PS[:, ubank, 0:wd], part[:, k, :], ab[:, k, 0:wd],
                            start=(k == 0 and a == 0), stop=(k == NB - 1 and a == 1)),
                            ta if k == 0 and a == 0 else None, t_h if k == 0 and a == 0 else None,
                            u_ev.get(nu - 2) if k == 0 and a == 0 else None)
                tu = t
                if step == 0:
                    for k in range(NB):
                        t = pe(lambda p, ab=ab, k=k, ty=ty, wd=wd: p.matmul(
                            PS[0:4, 7, 0:wd], sel[:, ty, :], ab[:, k, 0:wd],
                            start=(k == 0 and ty == 0), stop=(k == NB - 1 and ty == 3)),
                            t_sel, u_ev.get("cnt"))
                a_free[n] = t

                def rest3(step=step, j=j, ty=ty, wd=wd, ubank=ubank, sh=sh, sl=sl, ab=Ab[(n + 1) % 3]):
                    ta = sp("ab", ab[:, :, 0:wd], AT2[j][:, NB * ty:NB * ty + NB, :])
                    for k in range(NB):
                        for part in (sh, sl):
                            pe(lambda p, k=k, part=part: p.matmul(
                                PS[:, ubank, 0:wd], part[:, k, :], ab[:, k, 0:wd],
                                start=False, stop=True, skip_group_check=True), ta)
                        if step == 0:
                            pe(lambda p, k=k: p.matmul(
                                PS[0:4, 7, 0:wd], sel[:, ty, :], ab[:, k, 0:wd],
                                start=False, stop=True, skip_group_check=True), ta)

                P.general(rest3)
                n += 1
                u_ev[nu] = act(lambda s, nu=nu, ubank=ubank, wd=wd: s.mul(
                    ub[nu % 2][:, 0:wd], PS[:, ubank, 0:wd], 1.0 / SC), tu, u_ev.get(("w", nu - 2)))
                if step == 0 and ty == 3:
                    u_ev["cnt"] = act(lambda s, cs=cs, wd=wd: s.copy(cnt[:, cs], PS[0:4, 7, 0:wd]), t)
                u_ev[("w", nu)] = pe(lambda p, nu=nu, ty=ty, wd=wd: p.matmul(
                    PS[:, 2, 0:wd], weT[:, ty, :], ub[nu % 2][:, 0:wd], start=(ty == 0), stop=False),
                    u_ev[nu], u_ev.get("a") if ty == 0 else None)
                nu += 1
            t = pe(lambda p, cs=cs, wd=wd: p.matmul(PS[:, 2, 0:wd], bet[:], cnt[:, cs], start=False, stop=True),
                   u_ev.get("cnt"))
            t_a = act(lambda s, wd=wd: s.copy(aT[:, 0:wd], PS[:, 2, 0:wd]), t, u_ev.get("gi"))
            u_ev["a"] = t_a
            gw = u_ev.get("g")
            for i in range(2):
                pe(lambda p, i=i, wd=wd: p.matmul(PS[:, 3 + i, 0:wd], wgT[:, 0, i, :], aT[:, 0:wd],
                                                  start=True, stop=False), t_a, gw)
                t = pe(lambda p, i=i, wd=wd, cur=cur, cs=cs: p.matmul(
                    PS[:, 3 + i, 0:wd], wgT[:, 1, i, :], cur[:, cs], start=False, stop=True))
                if i == 0:
                    t_r = t
                else:
                    t_z = t
            t_in = pe(lambda p, wd=wd: p.matmul(PS[:, 5, 0:wd], wgT[:, 0, 2, :], aT[:, 0:wd],
                                                start=True, stop=True))
            t_hn = pe(lambda p, wd=wd, cur=cur, cs=cs: p.matmul(PS[:, 6, 0:wd], wgT[:, 1, 2, :], cur[:, cs],
                                                                start=True, stop=True))
            u_ev["gi"] = t_hn
            t_r = act(lambda s, wd=wd: s.activation(rg[:, 0:wd], PS[:, 3, 0:wd], ACT.Sigmoid, bias=brz[:, 0:1]), t_r)
            t_z = act(lambda s, wd=wd: s.activation(zg[:, 0:wd], PS[:, 4, 0:wd], ACT.Sigmoid, bias=brz[:, 1:2]),
                      t_z, u_ev.get("h"))
            t = dve(lambda v, wd=wd: v.scalar_tensor_tensor(
                out=hnb[:, 0:wd], in0=PS[:, 6, 0:wd], scalar=bi[:, 1, 2:3], in1=rg[:, 0:wd],
                op0=ALU.add, op1=ALU.mult), t_hn, t_r)
            t = dve(lambda v, wd=wd: v.tensor_tensor(hnb[:, 0:wd], PS[:, 5, 0:wd], hnb[:, 0:wd], ALU.add), t)
            u_ev["g"] = [t, t_z]
            t_n = act(lambda s, wd=wd: s.activation(ng[:, 0:wd], hnb[:, 0:wd], ACT.Tanh, bias=bi[:, 0, 2:3]),
                      t, u_ev.get("h"))
            t = dve(lambda v, wd=wd, cur=cur, cs=cs: v.tensor_tensor(dd[:, 0:wd], cur[:, cs], ng[:, 0:wd],
                                                                     ALU.subtract), t_n)
            t = dve(lambda v, wd=wd: v.tensor_tensor(dd[:, 0:wd], dd[:, 0:wd], zg[:, 0:wd], ALU.mult), t, t_z)
            t = dve(lambda v, wd=wd, nxt=nxt, cs=cs: v.tensor_tensor(nxt[:, cs], dd[:, 0:wd], ng[:, 0:wd],
                                                                     ALU.add), t)
            u_ev["h"] = t
            nb = wd // 128
            for qq in range(nb):
                t1 = pe(lambda p, qq=qq, nxt=nxt, j=j: p.transpose(
                    PS[:, 7, 128 * qq:128 * qq + 128],
                    nxt[:, 512 * j + 128 * qq:512 * j + 128 * qq + 128], ident[:]), t, u_ev.get("tr"),
                    u_ev.get("cnt"))
            psv = PS[:, 7, 0:wd].rearrange("p (k c) -> p k c", c=128)
            if step < 3:
                t2 = act(lambda s, nh=nh, j=j, nb=nb, psv=psv: s.mul(nh[:, 4 * j:4 * j + nb, :], psv, SC), t1)
                t3 = dve(lambda v, nh=nh, nl=nl, j=j, nb=nb, psv=psv: v.scalar_tensor_tensor(
                    out=nl[:, 4 * j:4 * j + nb, :], in0=psv, scalar=SC, in1=nh[:, 4 * j:4 * j + nb, :],
                    op0=ALU.mult, op1=ALU.subtract), t2)
            else:
                t3 = dve(lambda v, j=j, nb=nb, psv=psv: v.tensor_tensor(
                    xr[:, 4 * j:4 * j + nb, :], xr[:, 4 * j:4 * j + nb, :], psv, ALU.add), t1)
            u_ev["tr"] = t3
            u_ev["cnt"] = t3 if step == 0 else u_ev.get("cnt")
        t_h = t3
    t = layernorm(xr, ln1, ln2, t3)
    sp("out", out[0:128 * (NB - 1), :].rearrange("(b p) d -> p b d", p=128), xr[:, 0:NB - 1, :], t)
    t = sp("out", out[128 * (NB - 1):N, :], xr[0:N - 128 * (NB - 1), NB - 1, :])
    P.wait("sp", t)
    q.close()
    pd.close()

    block = ctx.enter_context(nc.Block())

    @block.sync
    def _(eng):
        P.emit("sp", eng)

    @block.gpsimd
    def _(eng):
        P.emit("pool", eng)

    @block.scalar
    def _(eng):
        P.emit("act", eng)

    @block.vector
    def _(eng):
        P.emit("dve", eng)

    @block.tensor
    def _(eng):
        P.emit("pe", eng)

    ctx.close()


_INS = ["x", "src", "dst", "bnd", "edge_attr_4", "edge_weight",
        "L0_gnn_W1", "L0_gnn_as1", "L0_gnn_ad1", "L0_gnn_b1", "L0_gnn_W2", "L0_gnn_as2", "L0_gnn_ad2", "L0_gnn_b2",
        "L0_gnn_W3", "L0_gnn_as3", "L0_gnn_ad3", "L0_gnn_b3",
        "L1_gnn_w1", "L1_gnn_b1", "L1_gnn_w2", "L1_gnn_b2", "L1_gnn_gamma", "L1_gnn_beta",
        "L2_gnn_Wk", "L2_gnn_bk", "L2_gnn_bias",
        "L3_gnn_W_edge", "L3_gnn_b_edge", "L3_gnn_W_ih", "L3_gnn_W_hh", "L3_gnn_b_ih", "L3_gnn_b_hh"]


def lay_out(inputs):
    import numpy as np

    a = {k: np.ascontiguousarray(v) for k, v in inputs.items()}

    def pad(v, fill):
        o = np.full((EP,) + v.shape[1:], fill, v.dtype)
        o[:E] = v
        return o

    a["src"] = pad(a["src"], 0)
    a["dst"] = pad(a["dst"], 4000)
    a["edge_attr_4"] = pad(a["edge_attr_4"], 0)
    a["edge_weight"] = pad(a["edge_weight"], 0)
    for name in ("L1_gnn_b1", "L3_gnn_b_ih", "L3_gnn_b_hh"):
        a[name] = np.ascontiguousarray(a[name].reshape(-1, 128).T)
    a["bnd"] = np.ascontiguousarray(a["dst"][::128])
    a["dst"] = np.concatenate([a["dst"], np.full(128, 4000, a["dst"].dtype)])
    return a


def kernel(**inputs):
    import concourse.bacc as _bacc
    from concourse.bass_utils import run_bass_kernel_spmd as _run

    nc = _bacc.Bacc("TRN2", target_bir_lowering=False, num_devices=1)
    a = lay_out(inputs)
    arrays, args = {}, []
    for name in _INS:
        arrays[f"in_{name}"] = a[name]
        args.append(nc.dram_tensor(f"in_{name}", a[name].shape, mybir.dt.from_np(a[name].dtype),
                                   kind="ExternalInput").ap())
    args.append(nc.dram_tensor("out_0", (N, D), F32, kind="ExternalOutput").ap())
    gnn_kernel(nc, *args)
    r = _run(nc, [arrays], core_ids=[0])
    return r.results[0]["out_0"]
```

```python
from contextlib import ExitStack

import concourse.bass as bass
from concourse import mybir
from concourse.alu_op_type import AluOpType as ALU

F32 = mybir.dt.float32
F16 = mybir.dt.float16
BF16 = mybir.dt.bfloat16
I32 = mybir.dt.int32
ACT = mybir.ActivationFunctionType
AX = mybir.AxisListType.X

N = 3125
NB = 25
NP = NB * 128
E = 103125
EC = 808
EP = EC * 128
SLACK = 384
D = 128
H = 4
NT = 7
BIG = -3.0e38
SC = 4096.0
GR = 2
GRG = 4
NW = 13
NXT = 49
GEN = [128, 128, 128, 128, 128, 128, 32]
LNEPS = 1e-5


def tile_w(j):
    return min(512, NP - 512 * j)


class Queues:

    def __init__(self, nc, ctx):
        self.nc, self.ctx = nc, ctx
        self.q = {e: [] for e in ("pe", "dve", "act", "pool", "sp")}
        self.n = {}
        self.sem = {}
        self.own = {}
        self.pre = ""
        self.flag = {}
        self.per = {}
        self.it = None

    def _sem(self, name):
        if name not in self.sem:
            self.sem[name] = self.ctx.enter_context(self.nc.semaphore(f"s_{name}"))
            self.n[name] = 0
            self.own[name] = self.pre
        return self.sem[name]

    def wait(self, e, *tokens):
        most = {}
        flat = list(tokens)
        while flat:
            t = flat.pop(0)
            if isinstance(t, list):
                flat = t + flat
            elif t is not None:
                most[t[0]] = max(t[1], most.get(t[0], 0))
        for name, v in most.items():
            self.q[e].append(lambda eng, name=name, v=v: eng.wait_ge(
                self.sem[name], self.it * self.per[name] + v if name in self.per else v))

    def op(self, e, fn, *tokens):
        self.wait(e, *tokens)
        name = self.pre + e
        s = self._sem(name)
        self.n[name] += 1
        self.q[e].append(lambda eng: fn(eng).then_inc(s, 1))
        return (name, self.n[name])

    def raw(self, e, fn, *tokens):
        self.wait(e, *tokens)
        self.q[e].append(fn)

    def dma(self, e, sem, out, in_, *tokens):
        sem = self.pre + sem
        s = self._sem(sem)
        self.wait(e, *tokens)
        self.n[sem] += 16
        get = lambda a: a() if callable(a) else a
        self.q[e].append(lambda eng: eng.dma_start(get(out), get(in_)).then_inc(s, 16))
        return (sem, self.n[sem])

    def token(self, name):
        return (self.pre + name, self.n[self.pre + name])

    def now(self):
        return [(k, v) for k, v in self.n.items() if v and self.own[k] == self.pre]

    def barrier(self, engines=None, but=()):
        now = [t for t in self.now() if t[0] not in but]
        for e in engines or self.q:
            self.wait(e, now)

    def general(self, build, pre="g_", flag="edges"):
        now = self.now()
        outer, self.q = self.q, {e: [] for e in self.q}
        for e in self.q:
            self.wait(e, now)
        was, self.pre = self.pre, pre
        build()
        self.barrier()
        self.pre = was
        inner, self.q = self.q, outer

        def branch(e):
            def emit(eng):
                with eng.If(self.flag[flag, e] != 0):
                    for fn in inner[e]:
                        fn(eng)
            return emit

        for e in self.q:
            self.q[e].append(branch(e))

    def loop(self, count, pre, engines, build):
        now = self.now()
        outer, self.q = self.q, {e: [] for e in self.q}
        was, self.pre = self.pre, pre
        build()
        self.barrier(engines)
        turn = {k: v for k, v in self.now()}
        self.pre = was
        inner, self.q = self.q, outer

        def run(e):
            def emit(eng):
                self.per = turn
                with eng.Fori(0, count) as it:
                    self.it = it
                    for fn in inner[e]:
                        fn(eng)
                self.per = {}
            return emit

        def after(name, v):
            return lambda eng: eng.wait_ge(self.sem[name], v)

        for e in self.q:
            if e in engines:
                self.wait(e, now)
                self.q[e].append(run(e))
            else:
                for k, v in turn.items():
                    self.q[e].append(after(k, v * count))

    def emit(self, e, eng):
        for fn in self.q[e]:
            fn(eng)


def gnn_kernel(nc, x, src, dst, bnd, attr, ew,
               W1, as1, ad1, b1, W2, as2, ad2, b2, W3, as3, ad3, b3,
               mw1, mb1, mw2, mb2, gamma, beta, Wk, bk, cbias,
               We, be, Wih, Whh, bih, bhh, out):
    ctx = ExitStack()
    P = Queues(nc, ctx)
    pe = lambda fn, *w: P.op("pe", fn, *w)
    dve = lambda fn, *w: P.op("dve", fn, *w)
    act = lambda fn, *w: P.op("act", fn, *w)
    pool = lambda fn, *w: P.op("pool", fn, *w)
    sp = lambda sem, o, i, *w: P.dma("sp", sem, o, i, *w)

    def sb(name, shape, dt=F32, c=ctx):
        return c.enter_context(nc.sbuf_tensor(name, shape, dt))

    def dram(name, shape, dt):
        return nc.dram_tensor(name, shape, dt).ap()

    AT = [dram(f"AT{j}", (128, 4 * NB, tile_w(j)), F16) for j in range(NT)]
    AC = dram("AC", (NB, 128, NP), F16)
    AT2 = [dram(f"ATL{j}", (128, 4 * NB, tile_w(j)), F16) for j in range(NT)]
    AC2 = dram("ACL", (NB, 128, NP), F16)
    KT_D = dram("KTAB", (EP + SLACK, 4), F32)
    WS_D = dram("WSUM", (NW * 256,), F32)
    CNT_D = dram("TCNT", (4, NP), F32)

    PS = ctx.enter_context(nc.psum_tensor("PS", [128, 8, 512], F32))
    PST = PS[:, 4:8, :].bitcast(F16)

    ident = sb("ident", [128, 128])
    identh = sb("identh", [128, 128], F16)
    io_i = sb("io_i", [128, 400], I32)
    ioh = sb("ioh", [128, 400], F16)
    iof = sb("iof", [128, 128])
    thr_i = sb("thr_i", [128, NW], I32)
    thr = sb("thr", [128, NW])
    thr25 = sb("thr25", [128, NW])
    thr100 = sb("thr100", [128, NW])
    epst = sb("epst", [128, 1])
    one = sb("one", [128, 1])
    sel = sb("sel", [128, 4, 4], F16)
    xr = sb("xr", [128, NB, D])
    net = sb("net", [128, 2 * NB])
    wmin = sb("wmin", [128, 4])
    flag = sb("flag", [128, 5])
    flag_i = sb("flag_i", [128, 2], I32)
    range_i = sb("range_i", [128, 3], I32)

    c0 = pool(lambda g: g.memset(ident[:], 1.0))
    t_id = pool(lambda g: g.affine_select(out=ident[:], in_=ident[:], compare_op=ALU.is_equal, fill=0.0,
                                          base=0, pattern=[[-1, 128]], channel_multiplier=1), c0)
    t_io = pool(lambda g: g.iota(io_i[:], pattern=[[1, 400]], base=0, channel_multiplier=0))
    t_th = pool(lambda g: g.iota(thr_i[:], pattern=[[256, NW]], base=0, channel_multiplier=GR))
    t_ep = dve(lambda v: v.memset(epst[:], LNEPS))
    dve(lambda v: v.memset(one[:], 1.0))
    t_idh = dve(lambda v: v.tensor_copy(identh[:], ident[:]), t_id)
    t_ioh = dve(lambda v: v.tensor_copy(ioh[:], io_i[:]), t_io)
    t_iof = dve(lambda v: v.tensor_copy(iof[:], io_i[:, 0:128]), t_io)
    t_thr = dve(lambda v: v.tensor_copy(thr[:], thr_i[:]), t_th)
    t_25 = dve(lambda v: v.tensor_scalar(thr25[:], thr[:], 25.0, None, ALU.mult), t_thr)
    t_100 = dve(lambda v: v.tensor_scalar(thr100[:], thr[:], 100.0, None, ALU.mult), t_thr)
    t = dve(lambda v: v.memset(sel[:], 0.0))
    for i in range(4):
        dve(lambda v, i=i: v.memset(sel[:, i, i:i + 1], 1.0), t)
    t_xz = dve(lambda v: v.memset(xr[:, NB - 1, :], 0.0))

    pa = ExitStack()
    KW = sb("KW", [128, NW, 3, 128], F32, pa)
    KH = sb("KH", [128, NW, 128], F32, pa)
    w3 = sb("w3", [128, NW, 128, 3], BF16, pa)
    pb = ExitStack()
    lo_f = sb("lo_f", [128, EC], F32, pb)
    hi_f = sb("hi_f", [128, EC], F32, pb)
    ewt = sb("ewt", [128, EC], F32, pb)
    dst_i = sb("dst_i", [128, EC], I32, pb)
    src_i = sb("src_i", [128, EC], I32, pb)
    dsn_i = sb("dsn_i", [128, EC], I32, pb)
    att = sb("att", [128, EC, 4], F32, pb)
    mx = sb("mx", [128, EC], F32, pb)
    ne = sb("ne", [128, EC, 3], F32, pb)
    tt = sb("tt", [128, EC], F32, pb)
    di = sb("di", [128, EC], I32, pb)
    df = sb("df", [128, EC], F32, pb)
    k4 = sb("k4", [128, EC, 4], F32, pb)
    tail = sb("tail", [128, 3, 4], F32, pb)
    bb_i = sb("bb_i", [128, EC], I32, pb)
    bb = sb("bb", [128, EC], F32, pb)
    scr = sb("scr", [128, EC], F32, pb)
    nbt = sb("nbt", [128, NW], F32, pb)
    c0f = sb("c0f", [128, NW], F32, pb)
    c0i = sb("c0i", [128, NW], I32, pb)
    drow = sb("drow", [128, NW, 128], I32, pb)
    drf = sb("drf", [128, NW, 128], F32, pb)
    sf = sb("sf", [128, NW], F32, pb)
    si = sb("si", [128, NW], I32, pb)
    win = sb("win", [128, NW, 128, 4], F32, pb)
    win2 = sb("win2", [128, NW, 2, 128], F32, pb)
    wrm = sb("wrm", [128, NW, 128], F32, pb)
    wcl = sb("wcl", [128, NW, 128], F32, pb)
    wmk = sb("wmk", [128, NW, 128], F32, pb)
    wsx = sb("wsx", [128, NW, GR], F32, pb)

    t_bb = sp("bb", bb_i[:], bnd.partition_broadcast(128))
    t_s = sp("src", src_i[:], src.rearrange("(p i) -> p i", p=128))
    t_d = sp("dst", dst_i[:], dst[0:EP].rearrange("(p i) -> p i", p=128))
    t_a = sp("att", att[:], attr.rearrange("(p i) t -> p i t", p=128))
    t_w = sp("ew", ewt[:], ew.rearrange("(p i) -> p i", p=128))
    t_dn = sp("dsn", dsn_i[:], dst[1:EP + 1].rearrange("(p i) -> p i", p=128))
    sp("x", xr[:, 0:NB - 1, :], x[0:128 * (NB - 1), :].rearrange("(b p) d -> p b d", p=128))
    t_x = sp("x", xr[0:N - 128 * (NB - 1), NB - 1, :], x[128 * (NB - 1):N, :], t_xz)

    t = dve(lambda v: v.tensor_copy(bb[:], bb_i[:]), t_bb)
    for k in range(NW):
        t = dve(lambda v, k=k: v.tensor_scalar(scr[:], bb[:], thr[:, k:k + 1], 0.0, ALU.is_lt, ALU.add,
                                               accum_out=nbt[:, k:k + 1]), t, t_thr)
    t = dve(lambda v: v.tensor_scalar(c0f[:], nbt[:], 1.0, 0.0, ALU.subtract, ALU.max), t)
    t_c0 = dve(lambda v: v.tensor_copy(c0i[:], c0f[:]), t)
    dst_r = dst[0:EP].rearrange("(c e) -> c e", e=128)

    def gather(sem, o, tab, ix, *w):
        s = P._sem(sem)
        P.wait("pool", *w)
        P.n[sem] += 16
        P.q["pool"].append(lambda g: g.indirect_dma_start(
            out=o, out_offset=None, in_=tab,
            in_offset=bass.IndirectOffsetOnAxis(ap=ix, axis=0)).then_inc(s, 16))
        return (sem, P.n[sem])

    for k in range(NW):
        t_g = gather("g0", drow[:, k, :], dst_r, c0i[:, k:k + 1], t_c0)

    t = dve(lambda v: v.tensor_scalar(di[:], src_i[:], 7, None, ALU.logical_shift_right), t_s)
    t_hi = dve(lambda v: v.tensor_copy(hi_f[:], di[:]), t)
    t = dve(lambda v: v.tensor_scalar(di[:], src_i[:], 127, None, ALU.bitwise_and), t_hi)
    t_lo = dve(lambda v: v.tensor_copy(lo_f[:], di[:]), t)
    t_df = dve(lambda v: v.tensor_copy(df[:], dst_i[:]), t_d)
    t = dve(lambda v: v.tensor_reduce(mx[:], att[:], AX, ALU.max), t_a)
    for c in range(3):
        t_ne = dve(lambda v, c=c: v.tensor_tensor(ne[:, :, c], att[:, :, c], mx[:], ALU.not_equal), t)
    t = dve(lambda v: v.scalar_tensor_tensor(out=tt[:], in0=ne[:, :, 2], scalar=1.0, in1=ne[:, :, 1],
                                             op0=ALU.add, op1=ALU.mult), t_ne)
    t = dve(lambda v: v.scalar_tensor_tensor(out=tt[:], in0=tt[:], scalar=1.0, in1=ne[:, :, 0],
                                             op0=ALU.add, op1=ALU.mult), t)
    t = dve(lambda v: v.scalar_tensor_tensor(out=tt[:], in0=tt[:], scalar=25.0, in1=hi_f[:],
                                             op0=ALU.mult, op1=ALU.add), t, t_hi)
    t_k0 = dve(lambda v: v.scalar_tensor_tensor(out=k4[:, :, 0], in0=df[:], scalar=100.0, in1=tt[:],
                                                op0=ALU.mult, op1=ALU.add), t, t_df)
    t_k1 = dve(lambda v: v.scalar_tensor_tensor(out=k4[:, :, 1], in0=df[:], scalar=25.0, in1=hi_f[:],
                                                op0=ALU.mult, op1=ALU.add), t_df)
    t_k2 = act(lambda s: s.copy(k4[:, :, 2], lo_f[:]), t_lo)
    t_k3 = act(lambda s: s.copy(k4[:, :, 3], ewt[:]), t_w)
    t_tl = dve(lambda v: v.memset(tail[:], 1.0e6))
    sp("ktab", KT_D[0:EP, :].rearrange("(p i) c -> p (i c)", p=128), k4.rearrange("p i c -> p (i c)"),
       t_k1, t_k3)
    t_kt = sp("ktab", KT_D[EP:EP + SLACK, :].rearrange("(p i) c -> p (i c)", p=128),
              tail.rearrange("p i c -> p (i c)"), t_tl)
    t = dve(lambda v: v.tensor_copy(drf[:], drow[:]), t_g)
    for k in range(NW):
        t = dve(lambda v, k=k: v.tensor_scalar(scr[:, 0:128], drf[:, k, :], thr[:, k:k + 1], 0.0, ALU.is_lt,
                                               ALU.add, accum_out=nbt[:, k:k + 1]), t)
    t = dve(lambda v: v.scalar_tensor_tensor(out=sf[:], in0=c0f[:], scalar=128.0, in1=nbt[:],
                                             op0=ALU.mult, op1=ALU.add), t)
    t_si = dve(lambda v: v.tensor_copy(si[:], sf[:]), t)
    part = ((0, 7), (7, NW))
    t_win = []
    for i, (k0, k1) in enumerate(part):
        for k in range(k0, k1):
            t = gather(f"g1{i}", win[:, k].rearrange("p e c -> p (e c)"), KT_D, si[:, k:k + 1], t_si, t_kt)
        t_win.append(t)
    dve(lambda v: v.tensor_reduce(wmin[:, 0:1], ewt[:], AX, ALU.min), t_w)
    t = dve(lambda v: v.tensor_tensor(scr[:], dst_i[:], dsn_i[:], ALU.is_gt), t_dn, t_si)
    t_ord = dve(lambda v: v.tensor_reduce(flag[:, 0:1], scr[:], AX, ALU.max), t)
    t2 = []
    t_wsx = None
    for (k0, k1), tw in zip(part, t_win):
        ks = slice(k0, k1)
        bcw = lambda a, ks=ks: a[:, ks].unsqueeze(2).broadcast_to([128, ks.stop - ks.start, 128])
        t2.append(dve(lambda v, ks=ks, bcw=bcw: v.tensor_tensor(
            win2[:, ks, 0, :], win[:, ks, :, 0], bcw(thr100), ALU.subtract), tw, t_100))
        t_w1 = dve(lambda v, ks=ks, bcw=bcw: v.tensor_tensor(
            win2[:, ks, 1, :], win[:, ks, :, 1], bcw(thr25), ALU.subtract), t_25)
        t2.append(t_w1)
        for d in range(GR if k0 == 0 else 0):
            t = dve(lambda v, d=d, ks=ks: v.scalar_tensor_tensor(
                out=wmk[:, ks], in0=win2[:, ks, 1, :], scalar=25.0 * d, in1=win[:, ks, :, 3],
                op0=ALU.is_ge, op1=ALU.mult), t_w1, t_wsx)
            t = dve(lambda v, d=d, ks=ks: v.scalar_tensor_tensor(
                out=wmk[:, ks], in0=win2[:, ks, 1, :], scalar=25.0 * d + 25.0, in1=wmk[:, ks],
                op0=ALU.is_lt, op1=ALU.mult), t)
            t_wsx = dve(lambda v, d=d, ks=ks: v.tensor_reduce(wsx[:, ks, d], wmk[:, ks], AX, ALU.add), t)
    ks = slice(*part[1])
    t1 = dve(lambda v: v.tensor_scalar(nbt[:], win2[:, :, 0, 127], 100.0 * GR, None, ALU.is_lt), t2)
    t1 = dve(lambda v: v.tensor_reduce(flag[:, 1:2], nbt[:], AX, ALU.max), t1)
    t = dve(lambda v: v.tensor_tensor(flag[:, 2:3], flag[:, 0:1], flag[:, 1:2], ALU.max), t_ord, t1)
    t = pool(lambda g: g.partition_all_reduce(flag[:, 3:4], flag[:, 2:3], 128, bass.bass_isa.ReduceOp.max), t)
    t = dve(lambda v: v.tensor_scalar(flag[:, 4:5], flag[:, 3:4], -1.0, 1.0, ALU.mult, ALU.add), t)
    t = dve(lambda v: v.tensor_copy(flag_i[:], flag[:, 3:5]), t)

    def load_flag(name, tile, col, *w):
        def emit_on(e):
            def emit(eng):
                P.flag[name, e] = eng.value_load(tile[0:1, col:col + 1], min_val=0, max_val=1)
            return emit

        for e in P.q:
            P.raw(e, emit_on(e), *w)

    load_flag("edges", flag_i, 0, t)
    load_flag("plain", flag_i, 1)
    nev = {}
    for k in range(NW):
        b = k % 4
        for a in range(4):
            tp = pe(lambda p, k=k, a=a, b=b: p.transpose(
                PS[:, b, 128 * a:128 * a + 128], win2[:, k, a, :] if a < 2 else win[:, k, :, a], ident[:]),
                t2, t_id, nev.get(k - 4) if a == 0 else None)
        act(lambda s, k=k, b=b: s.copy(KW[:, k].rearrange("p a g -> p (a g)"), PS[:, b, 0:384]), tp)
        nev[k] = act(lambda s, k=k, b=b: s.copy(wcl[:, k, :], PS[:, b, 384:512]))
    for d in range(GR):
        t = dve(lambda v, d=d: v.scalar_tensor_tensor(
            out=wmk[:, ks], in0=win2[:, ks, 1, :], scalar=25.0 * d, in1=win[:, ks, :, 3],
            op0=ALU.is_ge, op1=ALU.mult), t_w1, t_wsx)
        t = dve(lambda v, d=d: v.scalar_tensor_tensor(
            out=wmk[:, ks], in0=win2[:, ks, 1, :], scalar=25.0 * d + 25.0, in1=wmk[:, ks],
            op0=ALU.is_lt, op1=ALU.mult), t)
        t_wsx = dve(lambda v, d=d: v.tensor_reduce(wsx[:, ks, d], wmk[:, ks], AX, ALU.add), t)
    t_wst = sp("wsum", WS_D.rearrange("(k p d) -> p k d", p=128, d=GR), wsx[:], t_wsx)
    t_kw = nev[NW - 1]
    t = dve(lambda v: v.tensor_scalar(KH[:], KW[:, :, 1, :], 25.0, -25.0, ALU.is_ge, ALU.mult), t_kw)
    dve(lambda v: v.tensor_tensor(KH[:], KH[:], KW[:, :, 1, :], ALU.add), t)
    t = act(lambda s: s.copy(w3[:, :, :, 0], wcl[:]), t_kw)
    t = pool(lambda q: q.tensor_tensor(wrm[:], wcl[:], w3[:, :, :, 0], ALU.subtract), t)
    t = act(lambda s: s.copy(w3[:, :, :, 1], wrm[:]), t)
    pool(lambda q: q.tensor_tensor(w3[:, :, :, 2], wrm[:], w3[:, :, :, 1], ALU.subtract), t)
    P.barrier()
    pb.close()

    pc = ExitStack()
    OM = [sb(f"OM{i}", [128, 8, GR, 5 * NB], BF16, pc) for i in range(3)]
    OL = [sb(f"OL{i}", [128, 8, 128], BF16, pc) for i in range(3)]
    OA = [sb(f"OA{i}", [128, 128], F32, pc) for i in range(2)]
    n_oa = 0
    t_oa = {}
    HT = [sb(f"HT{i}", [128, 8, NB], BF16, pc) for i in range(2)]
    WH = [sb(f"WH{i}", [128, 8, 3, NB], BF16, pc) for i in range(3)]
    CS = [sb(f"CS{i}", [4, 256], F32, pc) for i in range(2)]
    NG = NP // GR
    t_cs = {}

    def type_sum(k, c, wd):
        t = t_cs[k, "p"] = pe(lambda p: p.matmul(
            PS[0:4, 4 + k % 2, 0:wd], sel[:, c // NB, :],
            ST[k % 2][:, c, 0:wd] if k < NW - 1 else ST[k % 2].rearrange("p c d -> p (c d)")[:, 128 * c:128 * c + 128],
            start=(c == 0), stop=(c == 4 * NB - 1)), ev_k[k] if c == 0 else None, t_cs.get(k - 2) if c == 0 else None)
        if c == 4 * NB - 1:
            t = act(lambda s: s.copy(CS[k % 2][:, 0:wd], PS[0:4, 4 + k % 2, 0:wd]), t, t_cs.get((k - 2, "d")))
            t_cs[k] = t
            t_cs[k, "d"] = sp(f"cs{k % 2}", CNT_D[:, 256 * k:256 * k + wd], CS[k % 2][:, 0:wd], t)

    wst = sb("wst", [NB, 128], F32, pc)
    ST = [sb(f"ST{i}", [128, 5 * NB, 256], F16, pc) for i in range(2)]
    t_wst = sp("wsum", wst[:], WS_D[0:NP].rearrange("(b p) -> b p", p=128))
    t_wh = {}
    t_we = {}

    def weigh_src(b8):
        for i in range(8):
            t_we[b8] = pe(lambda p, i=i: p.matmul(
                PS[:, 3, 0:3 * NB], OL[b8 % 3][:, i], WH[b8 % 3][:, i].rearrange("p a h -> p (a h)"),
                start=(b8 == 0 and i == 0), stop=(b8 == NG // 8 - 1 and i == 7)), t_wh[b8], t_ol.get(8 * b8 + i))

    t_pc = {}
    t_ol = {}
    ev = {}
    ev_k = {}
    st_dma = {}
    pair = lambda a, w: a[:, 0:GR * w].rearrange("p (d c) -> p d c", d=GR)
    for g in range(NG):
        k, gl = divmod(g, 128)
        s2 = k % 2
        b = (g // 2) % 3
        sl = g // 8 % 3
        if g % 8 == 0:
            g8 = slice(gl, gl + 8)
            b8 = g // 8
            dve(lambda v, sl=sl, k=k, g8=g8: v.tensor_tensor(
                OM[sl][:, :, :, 4 * NB:5 * NB], pair(iof, NB).unsqueeze(1).broadcast_to([128, 8, GR, NB]),
                KW[:, k, 1, g8].unsqueeze(2).unsqueeze(3).broadcast_to([128, 8, GR, NB]), ALU.is_equal),
                t_pc.get(g - 17), t_we.get(b8 - 3))
            nv, na = (4, 2) if b8 % 2 else (4, 1)
            dve(lambda v, sl=sl, k=k, gl=gl, nv=nv: v.tensor_tensor(
                OL[sl][:, 0:nv], iof[:].unsqueeze(1).broadcast_to([128, nv, 128]),
                KW[:, k, 2, gl:gl + nv].unsqueeze(2).broadcast_to([128, nv, 128]), ALU.is_equal))
            t = dve(lambda v, b8=b8, k=k, g8=g8: v.tensor_tensor(
                HT[b8 % 2][:], iof[:, 0:NB].unsqueeze(1).broadcast_to([128, 8, NB]),
                KH[:, k, g8].unsqueeze(2).broadcast_to([128, 8, NB]), ALU.is_equal), t_wh.get(b8 - 2))
            for i in range(nv, nv + na):
                t1 = act(lambda s, k=k, c=gl + i, o=OA[n_oa % 2]: s.activation(
                    o[:], iof[:], ACT.Abs, bias=KW[:, k, 2, c:c + 1], scale=-1.0), t_oa.get(n_oa - 2))
                t_ol[g + i] = t_oa[n_oa] = act(lambda s, sl=sl, i=i, o=OA[n_oa % 2]: s.activation(
                    OL[sl][:, i], o[:], ACT.Relu, bias=one[:], scale=-1.0), t1, t_pc.get(g - 17), t_we.get(b8 - 3))
                n_oa += 1
            for i in range(nv + na, 8):
                t_ol[g + i] = pool(lambda q, sl=sl, i=i, k=k, c=gl + i: q.tensor_scalar(
                    OL[sl][:, i], iof[:], KW[:, k, 2, c:c + 1], None, ALU.is_equal), t_pc.get(g - 17), t_we.get(b8 - 3))
            for a in range(3):
                t_wh[b8] = pool(lambda q, a=a, b8=b8, k=k, g8=g8: q.tensor_tensor(
                    WH[b8 % 3][:, :, a, :], HT[b8 % 2][:], w3[:, k, g8, a].unsqueeze(2).broadcast_to([128, 8, NB]),
                    ALU.mult), t, t_we.get(b8 - 3))
            if b8:
                weigh_src(b8 - 1)
        t = dve(lambda v, sl=sl, k=k, gl=gl: v.tensor_scalar(
            OM[sl][:, gl % 8, :, 0:4 * NB], pair(ioh, 4 * NB), KW[:, k, 0, gl:gl + 1], None, ALU.is_equal))
        t_pc[g] = pe(lambda p, sl=sl, b=b, g=g: p.matmul(
            PS[:, b, 250 * (g % 2):250 * (g % 2) + 250], OL[sl][:, g % 8, :],
            OM[sl][:, g % 8].rearrange("p d c -> p (d c)"),
            start=True, stop=True), t, t_ol.get(g), ev.get(g // 2 - 3) if g % 2 == 0 else None)
        if k and gl < (50 if k == NW - 1 else 100):
            for c in [gl] if k < NW - 1 else [2 * gl, 2 * gl + 1]:
                type_sum(k - 1, c, 256)
        if g % 2:
            col = GR * (gl - 1)
            st = ST[s2] if k < NW - 1 else ST[s2].rearrange("p c d -> p (c d)")[:, 0:5 * NB * 128].rearrange(
                "p (c d) -> p c d", d=128)
            ev[g // 2] = act(lambda s, st=st, b=b, col=col: s.copy(
                st[:, :, col:col + 2 * GR], PS[:, b, 0:500].rearrange("p (d c) -> p c d", d=2 * GR)),
                t_pc[g], [st_dma.get(k - 2), t_cs.get(k - 2)] if col == 0 else None)
        if k == NW - 2 and gl == 63:
            n0 = 256 * k
            sp(f"st{s2}", AT[n0 // 512][:, :, n0 % 512:n0 % 512 + 128], st[:, 0:4 * NB, 0:128], ev[g // 2])
        if gl == 127 or g == NG - 1:
            wd = GR * (gl + 1)
            n0 = 256 * k
            ev_k[k] = ev[g // 2]
            o = 128 if k == NW - 2 else 0
            tA = sp(f"st{s2}", AT[n0 // 512][:, :, n0 % 512 + o:n0 % 512 + wd], st[:, 0:4 * NB, o:wd], ev[g // 2])
            for db in range(wd // 128):
                c = slice(128 * db, 128 * db + 128)
                td = pool(lambda q, st=st, r=4 * NB + 2 * k + db, c=c: q.tensor_tensor(
                    st[:, r, c], st[:, r, c], identh[:], ALU.add), ev[g // 2])
            tC = sp(f"sc{s2}", AC[:, :, n0:n0 + wd].rearrange("h l d -> l h d"), st[:, 4 * NB:5 * NB, 0:wd], td)
            st_dma[k] = [tA, tC]
    weigh_src(NG // 8 - 1)
    for c in range(4 * NB):
        type_sum(NW - 1, c, GR * 64)
    t = pe(lambda p: p.transpose(PS[:, 6, 0:NB], wst[:], ident[0:NB, 0:NB]), t_wst)
    dve(lambda v: v.tensor_copy(net[:, NB:2 * NB], PS[:, 6, 0:NB]), t)
    t = dve(lambda v: v.tensor_reduce(net[:, 0:NB], PS[:, 3, 0:3 * NB].rearrange("p (a h) -> p h a", a=3), AX,
                                      ALU.add), t_we[NG // 8 - 1])
    P.barrier(but=("st0", "st1", "sc0", "sc1"))
    pc.close()
    pa.close()

    def general_build():
        q = ExitStack()
        nx = EC + NB
        kall = sb("kall", [128, nx, 4], F32, q)
        kxi = sb("kxi", [128, 2, NB], I32, q)
        gbk = sb("gbk", [128, 3], F32, q)
        gst = sb("gst", [128, 3], F32, q)
        KD = sb("KD", [128, NXT, 3], F32, q)
        OG = sb("OG", [128, NXT, 628], F16, q)
        tot = sb("tot", [128, 500], F32, q)
        part = sb("part", [128, 2, 500], F16, q)
        wsd = sb("wsd", [128, 8, 2, 128], F32, q)
        wsh = sb("wsh", [128, 8, 2, NB], F32, q)
        dpl = sb("dpl", [128, 2, 2, EC], F32, q)
        dpi = sb("dpi", [128, 2, EC], I32, q)
        t = sp("kall", kall[:, 0:EC, :].rearrange("p i c -> p (i c)"), KT_D[0:EP, :].rearrange("(p i) c -> p (i c)", p=128))
        pool(lambda g: g.iota(kxi[:, 0, :], pattern=[[128 * 25 + 1, NB]], base=0, channel_multiplier=25))
        t1 = pool(lambda g: g.iota(kxi[:, 1, :], pattern=[[0, NB]], base=0, channel_multiplier=1))
        dve(lambda v: v.memset(kall[:, EC:nx, 0], 1.0e6))
        dve(lambda v: v.tensor_copy(kall[:, EC:nx, 1], kxi[:, 0, :]), t1)
        dve(lambda v: v.tensor_copy(kall[:, EC:nx, 2], kxi[:, 1, :]))
        dve(lambda v: v.memset(gst[:], 0.0))
        dve(lambda v: v.memset(gbk[:], 0.0))
        P.barrier()
        dve(lambda v: v.memset(gst[:, 0:1], 400.0))
        dve(lambda v: v.memset(gst[:, 1:2], 100.0))
        P.barrier()
        dc = lambda a: a.rearrange("p (c d) -> p d c", d=GRG)
        for j in range(NT):
            if not GEN[j]:
                continue
            s_ohm, s_mm, s_cut, s_st = (P._sem(f"g_{n}{j}") for n in ("ohm", "mm", "cut", "st"))
            dve(lambda v, j=j: v.memset(gbk[:, 0:1], 400.0 * 128 * j))
            dve(lambda v, j=j: v.memset(gbk[:, 1:2], 100.0 * 128 * j))

            def hot(v, j=j, s_ohm=s_ohm, s_mm=s_mm, s_cut=s_cut, s_st=s_st):
                with v.Fori(0, GEN[j]) as g:
                    v.memset(tot[:], 0.0)
                    with v.Fori(0, nx // NXT) as b:
                        v.drain()
                        v.tensor_tensor(KD[:], kall[:, bass.ds(b * NXT, NXT), 0:3],
                                        gbk[:].unsqueeze(1).broadcast_to([128, NXT, 3]), ALU.subtract)
                        v.drain()
                        for c in range(NXT):
                            v.tensor_scalar(OG[:, c, 0:400], ioh[:, 0:400], KD[:, c, 0:1], None, ALU.is_equal)
                            v.tensor_scalar(OG[:, c, 400:500], ioh[:, 0:100], KD[:, c, 1:2], None, ALU.is_equal)
                            v.tensor_scalar(OG[:, c, 500:628], ioh[:, 0:128], KD[:, c, 2:3], None, ALU.is_equal)
                        v.drain()
                        v.sem_inc(s_ohm, 1)
                        v.wait_ge(s_mm, g * (nx // NXT) + b + 1)
                        v.tensor_tensor(tot[:], tot[:], PS[:, 0, 0:500], ALU.add)
                    v.drain()
                    v.wait_ge(s_st, g * 64 + 1)
                    v.tensor_copy(dc(part[:, 0, 0:400]), tot[:, 0:400].rearrange("p (d c) -> p d c", d=GRG))
                    v.tensor_copy(dc(part[:, 0, 400:500]), tot[:, 400:500].rearrange("p (d c) -> p d c", d=GRG))
                    v.drain()
                    for a, b in ((0, 400), (400, 500)):
                        v.tensor_tensor(dc(part[:, 1, a:b]), tot[:, a:b].rearrange("p (d c) -> p d c", d=GRG),
                                        dc(part[:, 0, a:b]), ALU.subtract)
                    v.tensor_tensor(gbk[:], gbk[:], gst[:], ALU.add)
                    v.drain()
                    v.sem_inc(s_cut, 1)

            def count(p, j=j, s_ohm=s_ohm, s_mm=s_mm):
                with p.Fori(0, GEN[j]) as g:
                    with p.Fori(0, nx // NXT) as b:
                        p.wait_ge(s_ohm, g * (nx // NXT) + b + 1)
                        for c in range(NXT):
                            mm = p.matmul(PS[:, 0, 0:500], OG[:, c, 500:628], OG[:, c, 0:500],
                                          start=(c == 0), stop=(c == NXT - 1))
                        mm.then_inc(s_mm, 1)

            def store(a, j=j, s_cut=s_cut, s_st=s_st):
                a.sem_inc(s_st, 1)
                with a.Fori(0, GEN[j]) as g:
                    a.wait_ge(s_cut, g + 1)
                    for i, (ta, tc) in enumerate(((AT[j], AC), (AT2[j], AC2))):
                        a.dma_start(ta[:, :, bass.ds(g * GRG, GRG)],
                                    part[:, i, 0:400].rearrange("p (c d) -> p c d", d=GRG)).then_inc(s_st, 16)
                        a.dma_start(tc[:, :, bass.ds(g * GRG + 512 * j, GRG)].rearrange("h l d -> l h d"),
                                    part[:, i, 400:500].rearrange("p (c d) -> p c d", d=GRG)).then_inc(s_st, 16)
                    a.wait_ge(s_st, g * 64 + 65)

            P.barrier()
            P.raw("dve", hot)
            P.raw("pe", count)
            P.raw("act", store)
            s_j = P._sem(f"g_end{j}")
            P.n[f"g_end{j}"] += 1
            P.raw("act", lambda a, s_j=s_j: a.sem_inc(s_j, 1))
            P.barrier()
        t1 = None
        for i, ends in enumerate((src, dst[0:EP])):
            t = sp("kall", dpi[:, 0, :], ends.rearrange("(p i) -> p i", p=128), t1)
            t1 = dve(lambda v: v.tensor_scalar(dpi[:, 1, :], dpi[:, 0, :], 7, None, ALU.logical_shift_right), t)
            t1 = dve(lambda v, i=i: v.tensor_copy(dpl[:, i, 1, :], dpi[:, 1, :]), t1)
            t1 = dve(lambda v: v.tensor_scalar(dpi[:, 1, :], dpi[:, 0, :], 127, None, ALU.bitwise_and), t1)
            t1 = dve(lambda v, i=i: v.tensor_copy(dpl[:, i, 0, :], dpi[:, 1, :]), t1)
        dve(lambda v: v.memset(net[:], 0.0))

        def into():
            for c in range(8):
                col = lambda a, c=c: a[:, bass.ds(P.it * 8 + c, 1)]
                for i in range(2):
                    dve(lambda v, c=c, i=i, col=col: v.tensor_tensor(
                        wsd[:, c, i, :], iof[:], col(dpl[:, i, 0, :]).broadcast_to([128, 128]), ALU.is_equal))
                    t = dve(lambda v, c=c, i=i, col=col: v.tensor_tensor(
                        wsh[:, c, i, :], iof[:, 0:NB], col(dpl[:, i, 1, :]).broadcast_to([128, NB]), ALU.is_equal))
                    t = dve(lambda v, c=c, i=i, col=col: v.tensor_tensor(
                        wsh[:, c, i, :], wsh[:, c, i, :], col(kall[:, 0:EC, 3]).broadcast_to([128, NB]), ALU.mult), t)
                    tm = pe(lambda p, c=c, i=i: p.matmul(PS[:, i, 0:NB], wsd[:, c, i, :], wsh[:, c, i, :],
                                                         start=(c == 0), stop=(c == 7)), t)
            for i in range(2):
                dve(lambda v, i=i: v.tensor_tensor(net[:, NB * i:NB * i + NB], net[:, NB * i:NB * i + NB],
                                                   PS[:, i, 0:NB], ALU.add), tm)

        P.loop(EC // 8, "gw_", ("pe", "dve"), into)
        q.close()


    rows = sb("rows", [128, NB, D])

    P.general(general_build)
    hA = sb("hA", [128, NP])
    hB = sb("hB", [128, NP])

    def to_cols(rows, dst_T, *w):
        last = {}
        for j in range(NT):
            for q in range(tile_w(j) // 128):
                t = pe(lambda p, j=j, q=q: p.transpose(PS[:, j % 4, 128 * q:128 * q + 128],
                                                       rows[:, 4 * j + q, :], ident[:]),
                       *w, last.get(j - 4))
            last[j] = act(lambda s, j=j: s.copy(dst_T[:, 512 * j:512 * j + tile_w(j)],
                                                PS[:, j % 4, 0:tile_w(j)]), t)
        return last[NT - 1]

    to_cols(xr, hA)
    SMAX = 16384.0
    STEP = 2.0 ** 60

    gw = ExitStack()
    Wts, wreps, bcols, t_was = {}, {}, {}, {}
    gu = ExitStack()
    for l, W, bias in ((1, W1, b1), (2, W2, b2), (3, W3, b3)):
        F = 512 if l == 3 else 128
        Wts[l] = sb(f"W{l}", [128, F + 8], F32, gw)
        wreps[l] = sb(f"wr{l}", [128, H, 128], F32, gw)
        bcols[l] = sb(f"bc{l}", [128, 128 if l == 3 else 1], F32, gw)
    for l, W, a_s, a_d, bias in ((1, W1, as1, ad1, b1), (2, W2, as2, ad2, b2), (3, W3, as3, ad3, b3)):
        F = 512 if l == 3 else 128
        Wt = Wts[l]
        ab = sb(f"ab{l}", [128, 2, F], F32, gu)
        tmp = sb(f"tmp{l}", [128, F], F32, gu)
        sp(f"gw{l}", Wt[:, 0:F], W)
        sp(f"gw{l}", ab[:, 0, :], a_s.rearrange("h c -> (h c)").partition_broadcast(128))
        sp(f"gw{l}", ab[:, 1, :], a_d.rearrange("h c -> (h c)").partition_broadcast(128))
        t = sp(f"gw{l}", bcols[l][:], bias.partition_broadcast(128) if l == 3 else bias.rearrange("(p o) -> p o", o=1))
        for s in range(2):
            t1 = dve(lambda v, s=s, Wt=Wt, tmp=tmp, ab=ab, F=F: v.tensor_tensor(
                tmp[:], Wt[:, 0:F], ab[:, s, :], ALU.mult), t)
            t = dve(lambda v, s=s, Wt=Wt, tmp=tmp, F=F: v.tensor_reduce(
                Wt[:, F + 4 * s:F + 4 * s + 4], tmp.rearrange("p (h c) -> p h c", h=H), AX, ALU.add), t1)
        t_was[l] = [t, dve(lambda v, l=l, Wt=Wt, F=F: v.tensor_copy(
            wreps[l][:], Wt[:, F + 4:F + 8].unsqueeze(2).broadcast_to([128, H, 128])), t)]
    P.barrier()
    gu.close()

    def gat(l, hin, hout):
        last = l == 3
        C = 128 if last else 32
        C1 = C + 1
        F = H * C
        g = ExitStack()
        Wt, wrep, bcol = Wts[l], wreps[l], bcols[l]
        t_wa, t_wr = t_was[l]
        acol = sb(f"ac{l}", [128, NB, 8], F32, g)
        red = sb(f"re{l}", [128, 16], F32, g)
        G = sb(f"G{l}", [128, 16], F32, g)
        rng = sb(f"rn{l}", [128, 8], F32, g)
        rng_i = range_i[:, l - 1:l]
        m = ExitStack()
        if last:
            y = sb("y3", [128, NB, H, C1], F32, m)
        else:
            Y = sb(f"Y{l}", [128, NB, 2, H, 2 * C1], F16, m)
            nega = sb(f"na{l}", [128, NB, 4], F32, m)
            a60 = sb(f"a6{l}", [128, NB, 4], F32, m)
            qd = sb(f"qd{l}", [128, NB, 4], F32, m)
        brow = sb(f"br{l}", [128, H, NP], F32, m)
        w1 = sb(f"w1{l}", [128, NB, 4], F32, m)
        w0 = sb(f"w0{l}", [128, NB, 4], F32, m)
        u = ExitStack()
        dif = sb(f"df{l}", [128, NB, 4], F32, u)
        if not last:
            xp = sb(f"xp{l}", [128, NB, H, C], F32, u)
            xk = sb(f"xk{l}", [128, NB, H], F32, u)
            yf = [sb(f"yf{l}{i}", [128, NB, H, C1], F32, u) for i in range(2)]
            xa = yf[0][:, :, :, 0:C]

        if last:
            pool(lambda q: q.tensor_tensor(xr[:], xr[:], bcol[:].unsqueeze(1).broadcast_to([128, NB, D]), ALU.add))
        e = {}
        if last:
            for k in range(NB):
                t = pe(lambda p, k=k: p.matmul(PS[:, 0, 8 * k:8 * k + 8], hin[:, 128 * k:128 * k + 128],
                                               Wt[:, F:F + 8], start=True, stop=True), t_wa)
            t_ac = act(lambda s: s.copy(acol.rearrange("p k h -> p (k h)"), PS[:, 0, 0:8 * NB]), t)
        else:
            for j in range(0, NB, 3):
                nb = min(3, NB - j)
                b = j // 3 % 4
                for i in range(nb):
                    t = pe(lambda p, i=i, j=j, b=b: p.matmul(
                        PS[:, b, 136 * i:136 * i + 136], hin[:, 128 * (i + j):128 * (i + j) + 128], Wt[:],
                        start=True, stop=True), t_wa, e.get(j - 12))
                psv = PS[:, b, 0:136 * nb].rearrange("p (k c) -> p k c", c=136)
                t_ac = act(lambda s, j=j, nb=nb, psv=psv: s.copy(acol[:, j:j + nb, :], psv[:, :, F:F + 8]), t)
                e[j] = act(lambda s, j=j, nb=nb, psv=psv: s.copy(
                    xp[:, j:j + nb].rearrange("p k h c -> p k (h c)"), psv[:, :, 0:F]))
            t_xp = e[j]
        eb = {}
        spans = [(h, j) for h in range(H) for j in range(NT)]

        def project_dst(n, eng):
            h, j = spans[n]
            wd = tile_w(j)
            cs = slice(512 * j, 512 * j + wd)
            b = 4 + n % 4 if last else (4 + n) % 8
            t = pe(lambda p: p.matmul(PS[:, b, 0:wd], wrep[:, h, :], hin[:, cs], start=True, stop=True),
                   t_wr, eb.get(n - (4 if last else 8)), None if last or n < 4 else t_xp)
            if last:
                eb[n] = dve(lambda v: v.tensor_scalar(brow[:, h, cs], PS[:, b, 0:wd], G[:, h:h + 1], 0.0,
                                                      ALU.add, ALU.max), t, t_G)
                if j == NT - 1:
                    act(lambda s: s.activation(brow[:, h, :], brow[:, h, :], ACT.Exp, scale=-0.8), eb[n])
            elif eng == "A":
                eb[n] = act(lambda s: s.copy(brow[:, h, cs], PS[:, b, 0:wd]), t)
            else:
                eb[n] = dve(lambda v: v.tensor_copy(brow[:, h, cs], PS[:, b, 0:wd]), t)

        def project_on(n, engines):
            for i, c in enumerate(engines):
                project_dst(n + i, c)

        t1 = dve(lambda v: v.tensor_reduce(red[:, 0:4], acol[:, :, 0:4].rearrange("p k h -> p h k"), AX, ALU.max),
                 t_ac)
        na = dif if last else nega
        t = dve(lambda v: v.tensor_scalar(na[:], acol[:, :, 0:4], -1.0, None, ALU.mult), t_ac)
        t = dve(lambda v: v.tensor_reduce(red[:, 4:8], na.rearrange("p k h -> p h k"), AX, ALU.max), t)
        nred = 8
        if not last:
            nred = 12
            t = act(lambda s: s.activation(xa, xp[:], ACT.Abs), t_xp)
            t = dve(lambda v: v.tensor_reduce(xk[:], xa, AX, ALU.max), t)
            t = dve(lambda v: v.tensor_reduce(red[:, 8:12], xk.rearrange("p k h -> p h k"), AX, ALU.max), t)
        t_G = pool(lambda q: q.partition_all_reduce(G[:, 0:nred], red[:, 0:nred], 128, bass.bass_isa.ReduceOp.max),
                   t, t1)
        t = dve(lambda v: v.tensor_tensor(rng[:, 0:4], G[:, 0:4], G[:, 4:8], ALU.add), t_G)
        t = dve(lambda v: v.tensor_scalar(rng[:, 0:4], rng[:, 0:4], 80.0 if last else 12.0, None, ALU.is_gt), t)
        t = dve(lambda v: v.tensor_reduce(rng[:, 4:5], rng[:, 0:4], AX, ALU.max), t)
        t = dve(lambda v: v.tensor_tensor(rng[:, 4:5], rng[:, 4:5], flag[:, 3:4], ALU.max), t)
        t_fl = dve(lambda v: v.tensor_copy(rng_i, rng[:, 4:5]), t)
        bh = lambda a: a.unsqueeze(1).broadcast_to([128, NB, 4])
        t = dve(lambda v: v.tensor_tensor(dif[:], acol[:, :, 0:4], bh(G[:, 0:4]), ALU.subtract), t_G)
        t = dve(lambda v: v.tensor_scalar(dif[:], dif[:], -80.0, None, ALU.max), t)
        if not last:
            project_on(0, "AAAAAA")
        t_w1 = act(lambda s: s.activation(w1[:], dif[:], ACT.Exp, scale=0.8 if last else 1.0), t)
        t_w0 = act(lambda s: s.activation(w0[:], dif[:], ACT.Exp, scale=0.2), t)
        bc = lambda a, c: a.unsqueeze(3).broadcast_to([128, NB, H, c])
        if last:
            project_on(0, "D" * len(spans))
            e = {}
            for k in range(NB):
                t = pe(lambda p, k=k: p.matmul(PS[:, 1 + k % 3, :], hin[:, 128 * k:128 * k + 128], Wt[:, 0:F],
                                               start=True, stop=True), t_wa, e.get(k - 3))
                e[k] = dve(lambda v, k=k: v.tensor_tensor(
                    y[:, k, :, 0:C], PS[:, 1 + k % 3, :].rearrange("p (h c) -> p h c", h=H),
                    w0[:, k, :].unsqueeze(2).broadcast_to([128, H, C]), ALU.mult), t, t_w0)
            t_y = [e[NB - 1], act(lambda s: s.copy(y[:, :, :, C], w0[:]), t_w0)]
        else:
            t = dve(lambda v: v.tensor_tensor(qd[:], acol[:, :, 4:8], bh(G[:, 0:4]), ALU.add), t_G)
            t = dve(lambda v: v.tensor_scalar(qd[:], qd[:], 0.0, None, ALU.max), t)
            t_qd = act(lambda s: s.activation(qd[:], qd[:], ACT.Exp, scale=-0.8), t)
            t_60 = dve(lambda v: v.tensor_scalar(a60[:], acol[:, :, 0:4], STEP, None, ALU.mult))
            t = dve(lambda v: v.tensor_scalar(G[:, 8:12], G[:, 8:12], 1e-30, None, ALU.max))
            t = dve(lambda v: v.reciprocal(red[:, 8:12], G[:, 8:12]), t)
            t = dve(lambda v: v.tensor_scalar(red[:, 8:12], red[:, 8:12], SMAX, None, ALU.mult), t)
            t_y = []
            t_fx = None
            t_hi = []
            for i, (w, tw, on) in enumerate(((w1, t_w1, (6, "DDDD", "AAAAAA")), (w0, t_w0, (16, "DDDD", "AADAADAA")))):
                t1 = act(lambda s, w=w, i=i: s.mul(yf[i][:, :, :, C], w[:], SMAX), tw)
                t2 = dve(lambda v, w=w, i=i: v.tensor_tensor(w[:], w[:], bh(red[:, 8:12]), ALU.mult), t, t1)
                t2 = dve(lambda v, w=w, i=i: v.tensor_tensor(yf[i][:, :, :, 0:C], xp[:], bc(w[:], C), ALU.mult), t2)
                project_on(on[0], on[1])
                t_hi.append(act(lambda s, i=i: s.copy(Y[:, :, i, :, 0:C1], yf[i][:]), t1, t2))
                project_on(on[0] + len(on[1]), on[2])
            for i in range(2):
                t_y.append(dve(lambda v, i=i: v.tensor_tensor(Y[:, :, i, :, C1:2 * C1], yf[i][:],
                                                              Y[:, :, i, :, 0:C1], ALU.subtract), t_hi[i]))
        P.barrier()
        u.close()

        NR = 5 if last else 6
        ring = sb(f"cr{l}", [128, 5 * NR, 512], F16, m)
        if last:
            NM = 6
            Mb = [hout[:, 512 * i:512 * i + 512] for i in range(NM)]
            rc = sb("rc3", [128, 4], F32, m)
            ev = sb("ev3", [128, 4, H, C1], F32, m)
        else:
            NM = 16
            Mb = [sb(f"Mb{l}{i}", [128, 512], F16, m) for i in range(NM)]
            Sg = [sb(f"Sg{l}{i}", [128, 512], F16, m) for i in range(6)]
            ev = hout[:, 0:96 * C1].rearrange("p (d c) -> p d c", d=4)
            sa = sb(f"sa{l}", [128, 4, 8, C1], F32, m)
            sc = sb(f"sc{l}", [128, 4, 4, C1], F32, m)
            rc = sb(f"rc{l}", [128, 4, 4], F32, m)
        n = ns = 0
        t_c, c_free, m_free, s_free = {}, {}, {}, {}
        b_free = {}
        ev_free = None

        def drain(j, t):
            nb = tile_w(j) // 128
            if last:
                for d in range(nb):
                    for i in range(2):
                        b_free[2 * d + i] = act(lambda s, d=d, i=i: s.copy(
                            ev[:, d, 2 * i:2 * i + 2, :].rearrange("p h c -> p (h c)"), PS[:, 2 * d + i, 0:2 * C1]),
                            t, b_free.get("ev"))
                return
            tv = []
            for d in range(nb):
                b_free[2 * d + 1] = act(lambda s, d=d: s.copy(ev[:, d, 12 * C1:24 * C1], PS[:, 2 * d + 1, 0:12 * C1]),
                                        t, b_free.get("ev"))
                b_free[2 * d] = dve(lambda v, d=d: v.tensor_copy(ev[:, d, 0:12 * C1], PS[:, 2 * d, 0:12 * C1]),
                                    t, b_free.get("ev"))
                tv += [b_free[2 * d], b_free[2 * d + 1]]
            mv = ev[:, 0:nb, 0:16 * C1].rearrange("p d (g s c) -> p d g s c", s=2, c=C1)
            cv = ev[:, 0:nb, 16 * C1:24 * C1].rearrange("p d (h s c) -> p d h s c", s=2, c=C1)
            mg = sa[:, 0:nb].rearrange("p d (h g) c -> p d h g c", g=2)
            scv = sc[:, 0:nb]
            qv = qd[:, 4 * j:4 * j + nb, :].unsqueeze(3).broadcast_to([128, nb, 4, C1])
            for d in range(nb):
                t1 = pool(lambda q, d=d: q.tensor_tensor(sa[:, d], mv[:, d, :, 0, :], mv[:, d, :, 1, :], ALU.add),
                          tv, b_free.get("hr"))
                t2 = pool(lambda q, d=d: q.tensor_tensor(scv[:, d], cv[:, d, :, 0], cv[:, d, :, 1], ALU.add))
            b_free["ev"] = t2
            for d in range(nb):
                t2 = pool(lambda q, d=d: q.tensor_tensor(scv[:, d], scv[:, d], mg[:, d, :, 1, :], ALU.subtract), t1, t2)
            t2 = pool(lambda q: q.tensor_tensor(scv, scv, qv, ALU.mult), t2)
            for d in range(nb):
                t3 = pool(lambda q, d=d: q.tensor_tensor(scv[:, d], scv[:, d], mg[:, d, :, 0, :], ALU.add), t2)
            b_free["s"] = t3

        def divide(j):
            nb = tile_w(j) // 128
            if last:
                for d in range(nb):
                    o = rows[:, 4 * j + d, :]
                    t1 = dve(lambda v, d=d: v.reciprocal(rc[:], ev[:, d, :, C]), b_free[2 * d], b_free[2 * d + 1],
                             b_free.get("rc"))
                    t1 = dve(lambda v, o=o, d=d: v.tensor_scalar(
                        o, ev[:, d, 0, 0:C], rc[:, 0:1], None, ALU.mult), t1)
                    for h in range(1, H):
                        t1 = dve(lambda v, o=o, d=d, h=h: v.scalar_tensor_tensor(
                            out=o, in0=ev[:, d, h, 0:C], scalar=rc[:, h:h + 1], in1=o, op0=ALU.mult, op1=ALU.add), t1)
                    b_free["rc"] = t1
                b_free["ev"] = t1
                return
            xm = G[:, 8:12].unsqueeze(1).broadcast_to([128, nb, 4])
            t1 = dve(lambda v: v.reciprocal(rc[:, 0:nb], sc[:, 0:nb, :, C]), b_free["s"], b_free.get("hr"))
            t1 = dve(lambda v: v.tensor_tensor(rc[:, 0:nb], rc[:, 0:nb], xm, ALU.mult), t1)
            b_free["hr"] = pool(lambda q: q.tensor_tensor(
                rows[:, 4 * j:4 * j + nb, :].rearrange("p d (h c) -> p d h c", h=4), sc[:, 0:nb, :, 0:C],
                rc[:, 0:nb].unsqueeze(3).broadcast_to([128, nb, 4, C]), ALU.mult), t1)

        prev = None
        for j in range(NT):
            wd = tile_w(j)
            nb = wd // 128
            cs = slice(512 * j, 512 * j + wd)
            for i in range(NB):
                ci = 5 * j + i // 5
                if i % 5 == 0:
                    t_c[ci] = sp(f"cr{ci % NR}", ring[:, 5 * (ci % NR):5 * (ci % NR) + 5, 0:wd],
                                 AC[i:i + 5, :, cs].rearrange("k l d -> l k d"), c_free.get(ci - NR))
                cb = ring[:, 5 * (ci % NR) + i % 5, 0:wd]
                ms = []
                for h in range(H):
                    mb = Mb[n % NM]
                    if last:
                        tm = dve(lambda v, mb=mb, i=i, h=h, cs=cs, cb=cb, wd=wd: v.scalar_tensor_tensor(
                            out=mb[:, 0:wd], in0=brow[:, h, cs], scalar=w1[:, i, h:h + 1], in1=cb,
                            op0=ALU.max, op1=ALU.mult), t_c[ci], m_free.get(n - NM))
                    elif h < (1 if i < 8 or i % 2 else 2):
                        tm = dve(lambda v, mb=mb, i=i, h=h, cs=cs, cb=cb, wd=wd: v.scalar_tensor_tensor(
                            out=mb[:, 0:wd], in0=brow[:, h, cs], scalar=nega[:, i, h:h + 1], in1=cb,
                            op0=ALU.is_gt, op1=ALU.mult), t_c[ci], m_free.get(n - NM))
                    else:
                        sg = Sg[ns % 6]
                        ts = act(lambda s, sg=sg, i=i, h=h, cs=cs, wd=wd: s.activation(
                            sg[:, 0:wd], brow[:, h, cs], ACT.Sigmoid, bias=a60[:, i, h:h + 1], scale=STEP),
                            s_free.get(ns - 6))
                        mul = pool if h == 3 and i >= 8 else dve
                        tm = s_free[ns] = mul(lambda v, mb=mb, sg=sg, cb=cb, wd=wd: v.tensor_tensor(
                            mb[:, 0:wd], sg[:, 0:wd], cb, ALU.mult), ts, t_c[ci], m_free.get(n - NM))
                        ns += 1
                    ms.append((n, mb, tm))
                    n += 1
                if i == 0 and j:
                    drain(j - 1, prev)
                if i == 9 and j:
                    divide(j - 1)
                st = dict(start=False, stop=(i == NB - 1), skip_group_check=True)
                first = dict(st, start=(i == 0))
                if not last:
                    for d in range(nb):
                        pe(lambda p, d=d, cb=cb, i=i, kw=first: p.matmul(
                            PS[:, 2 * d + 1, 4 * C1:12 * C1], cb[:, 128 * d:128 * d + 128],
                            Y[:, i, 1].rearrange("p h c -> p (h c)"), **kw),
                            t_c[ci], b_free.get(2 * d + 1) if i == 0 else None)
                for h, (nn, mb, tm) in enumerate(ms):
                    for d in range(nb):
                        mblk = mb[:, 128 * d:128 * d + 128]
                        if last:
                            o, kw, mv_ = PS[:, 2 * d + h // 2, C1 * (h % 2):C1 * (h % 2) + C1], \
                                (st if h % 2 else first), y[:, i, h, :]
                        else:
                            o, kw, mv_ = PS[:, 2 * d, 4 * C1 * h:4 * C1 * h + 4 * C1] if h < 3 \
                                else PS[:, 2 * d + 1, 0:4 * C1], (st if h else first), Y[:, i, :, h, :]
                        t = pe(lambda p, o=o, mblk=mblk, mv_=mv_, kw=kw: p.matmul(o, mblk, mv_, **kw),
                               tm, b_free.get(2 * d) if i == 0 else None,
                               b_free.get(2 * d + 1) if i == 0 else None)
                    m_free[nn] = t
                prev = t
                if i % 5 == 4:
                    c_free[ci] = t
        drain(NT - 1, prev)
        divide(NT - 1)
        P.barrier()
        m.close()

        def exact():
            q = ExitStack()
            xq = sb(f"xq{l}", [128, NB, F], F32, q)
            arow = sb(f"aw{l}", [128, H, NP], F32, q)
            wq = sb(f"wq{l}", [128, H, 128], F32, q)
            SG = sb(f"sg{l}", [128, NB, 128], F16, q)
            ct = sb(f"ct{l}", [128, NP], F32, q)
            T = hout
            U = sb(f"U{l}", [128, NP], F32, q)
            cur = sb(f"cu{l}", [128, 8], F32, q)
            sm = sb(f"sm{l}", [128, 4], F32, q)

            def zeros():
                zer = SG.rearrange("p a b -> p (a b)")
                t = dve(lambda v: v.memset(zer, 0.0))
                for k in range(NB):
                    sp("z", AC2[k], zer, t)

            P.general(zeros, f"z{l}_", "plain")
            t = dve(lambda v: v.tensor_copy(wq[:], Wt[:, F:F + 4].unsqueeze(2).broadcast_to([128, H, 128])))
            e = None
            for h in range(H):
                for j in range(NT):
                    cs = slice(512 * j, 512 * j + tile_w(j))
                    t1 = pe(lambda p, h=h, j=j, cs=cs: p.matmul(PS[:, 0, 0:tile_w(j)], wq[:, h, :], hin[:, cs],
                                                                start=True, stop=True), t, e)
                    e = dve(lambda v, h=h, j=j, cs=cs: v.tensor_copy(arow[:, h, cs], PS[:, 0, 0:tile_w(j)]), t1)
            for k in range(NB):
                t1 = pe(lambda p, k=k: p.matmul(PS[:, 0, 0:F], hin[:, 128 * k:128 * k + 128], Wt[:, 0:F],
                                                start=True, stop=True), e)
                e = dve(lambda v, k=k: v.tensor_copy(xq[:, k, :], PS[:, 0, 0:F]), t1)

            def block():
                at = lambda tab: lambda: tab[:, :, bass.ds(P.it * 128, 128)].rearrange("h l d -> l h d")
                e = None
                for i, tab in enumerate((AC, AC2)):
                    t = P.dma("act", f"sg{i}", SG[:], at(tab), e)
                    for c in range(NB):
                        t1 = pe(lambda p, c=c, i=i: p.transpose(
                            PST[:, c // 8, 128 * (c % 8):128 * (c % 8) + 128], SG[:, c, :], identh[:]), t, e)
                    pv = PST.rearrange("p b c -> p (b c)")[:, 0:NP]
                    if i == 0:
                        e = dve(lambda v, pv=pv: v.tensor_copy(ct[:], pv), t1)
                    else:
                        e = dve(lambda v, pv=pv: v.tensor_tensor(ct[:], ct[:], pv, ALU.add), t1, e)
                t_cu = dve(lambda v: v.tensor_copy(
                    cur[:].unsqueeze(1), acol[:, bass.ds(P.it, 1), :]))
                end = None
                for h in range(H):
                    b = cur[:, 4 + h:5 + h]
                    t_mk = dve(lambda v: v.tensor_scalar(U[:], ct[:], 0.0, BIG, ALU.is_equal, ALU.mult), e, end)
                    t = dve(lambda v, h=h: v.tensor_tensor(T[:], U[:], arow[:, h, :], ALU.add), t_mk, t_cu, end)
                    t = dve(lambda v: v.tensor_reduce(sm[:, 0:1], T[:], AX, ALU.max), t)
                    t = dve(lambda v, b=b: v.tensor_tensor(sm[:, 0:1], sm[:, 0:1], b, ALU.add), t)
                    tm = dve(lambda v: v.scalar_tensor_tensor(
                        out=sm[:, 1:2], in0=sm[:, 0:1], scalar=0.2, in1=sm[:, 0:1], op0=ALU.mult, op1=ALU.max), t)
                    t = dve(lambda v, h=h, b=b: v.tensor_scalar(T[:], arow[:, h, :], b, None, ALU.add), tm)
                    t = dve(lambda v: v.scalar_tensor_tensor(
                        out=T[:], in0=T[:], scalar=0.2, in1=T[:], op0=ALU.mult, op1=ALU.max), t)
                    t = dve(lambda v: v.tensor_scalar(T[:], T[:], sm[:, 1:2], 0.0, ALU.subtract, ALU.min), t)
                    t = act(lambda s: s.activation(T[:], T[:], ACT.Exp), t)
                    t_p = dve(lambda v: v.tensor_tensor(T[:], T[:], ct[:], ALU.mult), t)
                    t = dve(lambda v: v.tensor_reduce(sm[:, 2:3], T[:], AX, ALU.add), t_p)
                    t_r = dve(lambda v: v.reciprocal(sm[:, 3:4], sm[:, 2:3]), t)
                    ec = {}
                    for j in range(NT):
                        for d in range(tile_w(j) // 128):
                            t = pe(lambda p, j=j, d=d: p.transpose(
                                PS[:, j % 2, 128 * d:128 * d + 128], T[:, 512 * j + 128 * d:512 * j + 128 * d + 128],
                                ident[:]), t_p, ec.get(j - 2))
                        ec[j] = act(lambda s, j=j: s.copy(U[:, 512 * j:512 * j + tile_w(j)],
                                                          PS[:, j % 2, 0:tile_w(j)]), t)
                    for k in range(NB):
                        t = pe(lambda p, k=k, h=h: p.matmul(
                            PS[:, 2, 0:C], U[:, 128 * k:128 * k + 128], xq[:, k, C * h:C * h + C],
                            start=(k == 0), stop=(k == NB - 1)), ec[NT - 1], end)
                    if last and h:
                        end = dve(lambda v: v.scalar_tensor_tensor(
                            out=rows[:, bass.ds(P.it, 1), :], in0=PS[:, 2, 0:C].unsqueeze(1), scalar=sm[:, 3:4],
                            in1=rows[:, bass.ds(P.it, 1), :], op0=ALU.mult, op1=ALU.add), t, t_r)
                    else:
                        end = dve(lambda v, h=h: v.tensor_scalar(
                            rows[:, bass.ds(P.it, 1), 0 if last else C * h:C if last else C * h + C],
                            PS[:, 2, 0:C].unsqueeze(1), sm[:, 3:4], None, ALU.mult), t, t_r)

            P.loop(NB, f"b{l}_", ("pe", "dve", "act"), block)
            q.close()

        load_flag(f"range{l}", rng_i, 0, t_fl)
        P.general(exact, f"x{l}_", f"range{l}")
        if not last:
            lastj = {}
            for j in range(NT):
                for q in range(tile_w(j) // 128):
                    t = pe(lambda p, j=j, q=q: p.transpose(
                        PS[:, j % 4, 128 * q:128 * q + 128], rows[:, 4 * j + q, :], ident[:]), lastj.get(j - 4))
                lastj[j] = act(lambda s, j=j: s.activation(
                    hout[:, 512 * j:512 * j + tile_w(j)], PS[:, j % 4, 0:tile_w(j)], ACT.Relu, bias=bcol[:]), t)
        P.barrier()
        g.close()

    gat(1, hA, hB)
    gat(2, hB, hA)
    gat(3, hA, hB)
    gw.close()
    hT = hA

    pd = ExitStack()
    mr = sb("mr", [128, NB, D], F32, pd)
    hh = [sb(f"hh{i}", [128, NB, D], F16, pd) for i in range(2)]
    hl = [sb(f"hl{i}", [128, NB, D], F16, pd) for i in range(2)]
    Ab = [sb(f"Ab{i}", [128, NB, 512], F16, pd) for i in range(3)]
    ub = [sb(f"ub{i}", [128, 512], F32, pd) for i in range(2)]
    junk = sb("junk", [128, 8, D], F32, pd)
    lns = sb("lns", [128, 4, 4, NB], F32, pd)
    w1t = sb("w1t", [128, 512], F32, pd)
    w2t = sb("w2t", [128, 4, 128], F32, pd)
    b1c = sb("b1c", [128, 4], F32, pd)
    rowb = sb("rowb", [128, 4, 128], F32, pd)
    wkt = sb("wkt", [128, 6, 128], F32, pd)
    wab = sb("wab", [128, 2, 128], F32, pd)
    bk7 = sb("bk7", [128, 7, 128], F32, pd)
    lam = sb("lam", [128, 4], F32, pd)
    scl = sb("scl", [128, NB], F32, pd)
    wer = sb("wer", [128, 4, 128], F32, pd)
    weT = sb("weT", [128, 4, 128], F32, pd)
    wir = sb("wir", [128, 2, 3, 128], F32, pd)
    wgT = sb("wgT", [128, 2, 3, 128], F32, pd)
    bet = sb("bet", [4, 128], F32, pd)
    bi = sb("bi", [128, 2, 3], F32, pd)
    brz = sb("brz", [128, 2], F32, pd)
    Cf = [Ab[1].rearrange("p k d -> p (k d)")[:, NP * i:NP * i + NP] for i in range(4)]
    flat = Ab[2].rearrange("p k d -> p (k d)").bitcast(F32)
    uT = flat[:, 0:NP]
    hid = flat[:, NP:NP + 2048].rearrange("p (c d) -> p c d", c=4)

    for i, a in enumerate((gamma, beta, mb2)):
        sp("l1r", rowb[:, i, :], a.partition_broadcast(128))
    t_row = P.token("l1r")
    free = {}
    t_cf = {}
    for k in range(4):
        t_cf[k] = sp(f"cf{k}", Cf[k], AC[k])
    sp("l1w", w1t[:], mw1)
    sp("l1w", w2t[:], mw2.rearrange("(c p) d -> p c d", p=128))
    t_l1 = sp("l1w", b1c[:], mb1)
    sp("l2w", wkt[:], Wk.rearrange("k d o -> d k o"))
    sp("l2w", bk7[:, 0:6, :].rearrange("p k o -> p (k o)"), bk.rearrange("k o -> (k o)").partition_broadcast(128))
    t_l2 = sp("l2w", bk7[:, 6, :], cbias.partition_broadcast(128))
    sp("l3w", wer[:], We.rearrange("t o d -> o t d"))
    sp("l3w", wir[:, 0], Wih.rearrange("(g o) d -> o g d", o=128))
    sp("l3w", wir[:, 1], Whh.rearrange("(g o) d -> o g d", o=128))
    sp("l3w", bet[:], be)
    sp("l3w", bi[:, 0, :], bih)
    t_l3 = sp("l3w", bi[:, 1, :], bhh)

    junk_n = 0
    t_junk = {}

    def blocks(j):
        return range(4 * j, 4 * j + tile_w(j) // 128)

    def stats(i, X, j, t):
        nonlocal junk_n
        ks = slice(4 * j, 4 * j + tile_w(j) // 128)
        t = dve(lambda v: v.tensor_reduce(lns[:, i, 0, ks], X[:, ks, :], AX, ALU.add), t)
        t = dve(lambda v: v.tensor_scalar(lns[:, i, 0, ks], lns[:, i, 0, ks], -1.0 / D, None, ALU.mult), t)
        for k in blocks(j):
            n = junk_n
            t1 = t_junk[n] = act(lambda s, k=k, n=n: s.activation(
                junk[:, n % 8, :], X[:, k, :], ACT.Square, bias=lns[:, i, 0, k:k + 1],
                accum_out=lns[:, i, 1, k:k + 1]), t, t_junk.get(n - 8))
            junk_n += 1
        return act(lambda s: s.activation(lns[:, i, 2, ks], lns[:, i, 1, ks], ACT.Sqrt, bias=epst[:],
                                          scale=1.0 / D), t1)

    def scale_of(i, j, t):
        ks = slice(4 * j, 4 * j + tile_w(j) // 128)
        return dve(lambda v: v.reciprocal(lns[:, i, 3, ks], lns[:, i, 2, ks]), t)

    def apply(i, X, j, t):
        t = scale_of(i, j, t)
        for k in blocks(j):
            t1 = dve(lambda v, k=k: v.tensor_scalar(X[:, k, :], X[:, k, :], lns[:, i, 0, k:k + 1],
                                                    lns[:, i, 3, k:k + 1], ALU.add, ALU.mult), t)
        return t1

    def halves(X, j, hi, lo, t, free_=None):
        ks = slice(4 * j, 4 * j + tile_w(j) // 128)
        t = act(lambda s: s.mul(hi[:, ks, :], X[:, ks, :], SC), t, free_)
        return dve(lambda v: v.scalar_tensor_tensor(out=lo[:, ks, :], in0=X[:, ks, :], scalar=SC,
                                                    in1=hi[:, ks, :], op0=ALU.mult, op1=ALU.subtract), t)

    t_tc = {}

    def cols(X, j, b, t, free_=None):
        wd = tile_w(j)
        for d, k in enumerate(blocks(j)):
            t1 = pe(lambda p, d=d, k=k: p.transpose(PS[:, b, 128 * d:128 * d + 128], X[:, k, :], ident[:]),
                    t, t_tc.get(b))
        t_tc[b] = act(lambda s: s.copy(hT[:, 512 * j:512 * j + wd], PS[:, b, 0:wd]), t1, free_)
        return t_tc[b]

    def pipeline(stages):
        for slot in range(NT + len(stages) - 1):
            for i in reversed(range(len(stages))):
                if 0 <= slot - i < NT:
                    stages[i](slot - i)

    xb2 = hB.rearrange("p (k d) -> p k d", d=D)

    t_s, t_x1, t_hs, t_x1T, t_xb = {}, {}, {}, {}, {}

    def sum_in(j):
        ks = slice(4 * j, 4 * j + tile_w(j) // 128)
        t = dve(lambda v: v.scalar_tensor_tensor(out=xr[:, ks, :], in0=rows[:, ks, :], scalar=0.25, in1=xr[:, ks, :],
                                                 op0=ALU.mult, op1=ALU.add))
        t_s[j] = stats(0, xr, j, t)

    def norm_in(j):
        ks = slice(4 * j, 4 * j + tile_w(j) // 128)
        t = t_x1[j] = apply(0, xr, j, t_s[j])
        t_hs[j] = halves(xr, j, hh[0], hl[0], t)
        t_xb[j] = pool(lambda q: q.tensor_tensor(
            rows[:, ks, :], xr[:, ks, :],
            rowb[:, 1, :].unsqueeze(1).broadcast_to([128, tile_w(j) // 128, D]), ALU.add), t, t_row)
        t_xb[j] = [t_xb[j], pool(lambda q: q.tensor_tensor(
            xb2[:, ks, :], xr[:, ks, :],
            rowb[:, 2, :].unsqueeze(1).broadcast_to([128, tile_w(j) // 128, D]), ALU.add), t, t_row)]
        t_x1T[j] = cols(xr, j, 7, t)

    def spread(j):
        for k in blocks(j):
            if k not in t_cf:
                t_cf[k] = sp(f"cf{k % 4}", Cf[k % 4], AC[k], free[k - 4])
            for a, part in enumerate((hh[0], hl[0])):
                for i in range(NT):
                    wd = tile_w(i)
                    free[k] = pe(lambda p, k=k, i=i, wd=wd, part=part, a=a: p.matmul(
                        PS[:, i, 0:wd], part[:, k, :], Cf[k % 4][:, 512 * i:512 * i + wd],
                        start=(k == 0 and a == 0), stop=(k == NB - 1 and a == 1)), t_cf[k], t_hs[j])

    pipeline([sum_in, norm_in, spread])
    t_u1 = free[NB - 1]

    def rest1():
        t = None
        for k in range(NB):
            tc = sp("cf", Cf[0], AC2[k], t)
            for part in (hh[0], hl[0]):
                for j in range(NT):
                    t = pe(lambda p, k=k, j=j, part=part: p.matmul(
                        PS[:, j, 0:tile_w(j)], part[:, k, :], Cf[0][:, 512 * j:512 * j + tile_w(j)],
                        start=False, stop=True, skip_group_check=True), tc)

    P.general(rest1)
    t_bs = dve(lambda v: v.tensor_reduce(rowb[:, 3, :], bk7.rearrange("p k o -> p o k"), AX, ALU.add), t_l2)
    t = dve(lambda v: v.tensor_tensor(wab[:, 0, :], wkt[:, 0, :], wkt[:, 2, :], ALU.subtract))
    for c in (3, 4, 5):
        t = dve(lambda v, c=c: v.scalar_tensor_tensor(out=wab[:, 0, :], in0=wkt[:, c, :], scalar=-float(c - 1),
                                                      in1=wab[:, 0, :], op0=ALU.mult, op1=ALU.add), t)
    t = dve(lambda v: v.scalar_tensor_tensor(out=wab[:, 1, :], in0=wkt[:, 2, :], scalar=2.0,
                                             in1=wkt[:, 1, :], op0=ALU.mult, op1=ALU.add), t)
    for c in (3, 4, 5):
        t = dve(lambda v, c=c: v.scalar_tensor_tensor(out=wab[:, 1, :], in0=wkt[:, c, :], scalar=float(c),
                                                      in1=wab[:, 1, :], op0=ALU.mult, op1=ALU.add), t)
    t_wab = t
    dve(lambda v: v.tensor_reduce(lam[:, 0:1], net[:, 0:NB], AX, ALU.max))
    t = dve(lambda v: v.tensor_scalar(lam[:, 1:2], wmin[:, 0:1], -1.0, None, ALU.mult))
    t = dve(lambda v: v.tensor_tensor(lam[:, 2:3], lam[:, 0:1], lam[:, 1:2], ALU.max), t)
    t = pool(lambda g: g.partition_all_reduce(lam[:, 3:4], lam[:, 2:3], 128, bass.bass_isa.ReduceOp.max), t)
    t_u = {}
    for j in range(NT):
        wd = tile_w(j)
        t_u[j] = dve(lambda v, j=j, wd=wd: v.scalar_tensor_tensor(
            out=uT[:, 512 * j:512 * j + wd], in0=PS[:, j, 0:wd], scalar=1.0 / SC, in1=hT[:, 512 * j:512 * j + wd],
            op0=ALU.mult, op1=ALU.subtract), t_u1, t_x1T[j])
    t = dve(lambda v: v.reciprocal(lam[:, 0:1], lam[:, 3:4]), t)
    t1 = dve(lambda v: v.tensor_tensor(scl[:], net[:, 0:NB], net[:, NB:2 * NB], ALU.subtract))
    t_sc = dve(lambda v: v.tensor_scalar(scl[:], scl[:], lam[:, 0:1], None, ALU.mult), t, t1)
    t_brz = dve(lambda v: v.tensor_tensor(brz[:], bi[:, 0, 0:2], bi[:, 1, 0:2], ALU.add), t_l3)

    for i in range(4):
        t = pe(lambda p, i=i: p.transpose(PS[:, 7, 128 * i:128 * i + 128], wer[:, i, :], ident[:]), t_l3, t_tc[7])
    t = t_we3 = act(lambda s: s.copy(weT.rearrange("p t o -> p (t o)"), PS[:, 7, :]), t)
    for a in range(2):
        for i in range(3):
            t1 = pe(lambda p, a=a, i=i: p.transpose(PS[:, 7, 128 * i:128 * i + 128], wir[:, a, i, :], ident[:]), t)
        t = act(lambda s, a=a: s.copy(wgT[:, a].rearrange("p g o -> p (g o)"), PS[:, 7, 0:384]), t1)
    t_tc[7] = t

    e_h, e_a, e_m, e_2, t_m, t_m2, t_x2, t_x2T, t_y2, t_x3, t_x3h = ({} for _ in range(11))
    t_blk = {}
    n_h = 0

    def hidden(j):
        nonlocal n_h
        wd = tile_w(j)
        for c in range(4):
            t = pe(lambda p, c=c, b=n_h % 2: p.matmul(
                PS[:, b, 0:wd], w1t[:, 128 * c:128 * c + 128], uT[:, 512 * j:512 * j + wd],
                start=True, stop=True), t_u[max(j, n_h % 2)], t_l1, e_a.get(n_h - 2))
            e_h[j] = e_a[n_h] = act(lambda s, c=c, b=n_h % 2: s.activation(
                hid[:, c, 0:wd], PS[:, b, 0:wd], ACT.Relu, bias=b1c[:, c:c + 1]), t, e_m.get(j - 1))
            n_h += 1

    def out1(j):
        b = 4 + j % 2
        for d in range(tile_w(j) // 128):
            for c in range(4):
                e_m[j] = pe(lambda p, d=d, c=c: p.matmul(
                    PS[:, b, 128 * d:128 * d + 128], hid[:, c, 128 * d:128 * d + 128], w2t[:, c, :],
                    start=(c == 0), stop=(c == 3)), e_h[j], e_2.get(b, t_u[b]))

    def sum1(j):
        b = 4 + j % 2
        nb = tile_w(j) // 128
        ks = slice(4 * j, 4 * j + nb)
        t = e_2[b] = dve(lambda v: v.tensor_tensor(
            mr[:, ks, :], xb2[:, ks, :], PS[:, b, 0:128 * nb].rearrange("p (k c) -> p k c", c=128), ALU.add), e_m[j], t_xb[j])
        t_m[j] = stats(1, mr, j, t)

    def norm1(j):
        t = scale_of(1, j, t_m[j])
        for k in blocks(j):
            t1 = dve(lambda v, k=k: v.scalar_tensor_tensor(
                out=mr[:, k, :], in0=mr[:, k, :], scalar=lns[:, 1, 0, k:k + 1], in1=rowb[:, 0, :],
                op0=ALU.add, op1=ALU.mult), t)
        for k in blocks(j):
            t2 = dve(lambda v, k=k: v.scalar_tensor_tensor(
                out=xr[:, k, :], in0=mr[:, k, :], scalar=lns[:, 1, 3, k:k + 1], in1=rows[:, k, :],
                op0=ALU.mult, op1=ALU.add), t1, t_xb[j])
        t_m2[j] = stats(2, xr, j, t2)

    def norm2(j):
        ks = slice(4 * j, 4 * j + tile_w(j) // 128)
        t_x2[j] = apply(2, xr, j, t_m2[j])
        t_xb[j] = pool(lambda q: q.tensor_tensor(
            rows[:, ks, :], xr[:, ks, :],
            rowb[:, 3, :].unsqueeze(1).broadcast_to([128, tile_w(j) // 128, D]), ALU.add), t_x2[j], t_bs)

    def turn2(j):
        t_x2T[j] = cols(xr, j, 6, [t_x2[j], t_u[6]])

    t_ch = {}

    def cheb(j):
        for k in blocks(j):
            d = k % 4
            b = 2 + d // 2
            o = 256 * (d % 2)
            t_ch[j, d] = pe(lambda p, k=k, b=b, o=o: p.matmul(
                PS[:, b, o:o + 256], hT[:, 128 * k:128 * k + 128], wab.rearrange("p a o -> p (a o)"),
                start=True, stop=True), t_x2T[j], t_wab, e_2.get(b, t_u[b]))

    def sum2(j):
        nb = tile_w(j) // 128
        for i in range(0, nb, 2):
            b = 2 + i // 2
            n2 = min(2, nb - i)
            psv = PS[:, b, 0:256 * n2].rearrange("p (k a o) -> p k a o", a=2, o=128)
            ks = slice(4 * j + i, 4 * j + i + n2)
            for d in range(n2):
                t = dve(lambda v, d=d, k=4 * j + i + d, psv=psv: v.scalar_tensor_tensor(
                    out=mr[:, k, :], in0=psv[:, d, 1, :], scalar=scl[:, k:k + 1], in1=rows[:, k, :],
                    op0=ALU.mult, op1=ALU.add), t_ch[j, i + n2 - 1], t_sc, t_xb[j])
            t = e_2[b] = dve(lambda v, ks=ks, psv=psv: v.tensor_tensor(
                xr[:, ks, :], mr[:, ks, :], psv[:, :, 0, :], ALU.add), t)
        t_y2[j] = stats(3, xr, j, t)

    def norm3(j):
        t_x3[j] = apply(3, xr, j, t_y2[j])
        t_x3h[j] = halves(xr, j, hh[0], hl[0], t_x3[j], t_u1)

    def turn3(j):
        t_blk[0, j] = [t_x3h[j], cols(xr, j, 7, t_x3[j])]

    pipeline([hidden, out1, sum1, norm1, norm2, turn2, cheb, sum2, norm3, turn3])

    hN = [hT, hB]
    cnt = hB[0:4, :]
    t_cnt = sp("l3c", cnt, CNT_D, t_m[NT - 1])
    fb = rows.rearrange("p k d -> p (k d)")
    mrf = mr.rearrange("p k d -> p (k d)")
    aT, rg, zg, hnb, ng, dd = (mrf[:, 512 * i:512 * i + 512] for i in range(6))


    def count_types():
        e = None
        for j in range(NT):
            wd = tile_w(j)
            first = True
            for tab in (AT, AT2):
                for ty in range(4):
                    ta = sp("ab", Ab[0][:, :, 0:wd], tab[j][:, NB * ty:NB * ty + NB, :], e)
                    for k in range(NB):
                        e = pe(lambda p, k=k, ty=ty, wd=wd, first=first: p.matmul(
                            PS[0:4, 7, 0:wd], sel[:, ty, :], Ab[0][:, k, 0:wd], start=first, stop=True,
                            skip_group_check=True), ta, e if first else None)
                        first = False
            e = act(lambda s, j=j, wd=wd: s.copy(cnt[:, 512 * j:512 * j + wd], PS[0:4, 7, 0:wd]), e)

    P.general(count_types)
    t_fin = [t_blk[0, NT - 1], t_tc[6], e_2[4], e_2[5]]
    a_free, u_ev, w_ev, t_ab = {-2: t_u1, -1: e_m[NT - 1]}, {}, {}, {}
    gru = {}

    def accum(step, j, ty, ks):
        n = 4 * (NT * step + j) + ty
        wd = tile_w(j)
        ab = Ab[n % 3]
        if n not in t_ab:
            t_ab[n] = sp(f"ab{n % 3}", ab[:, :, 0:wd], AT[j][:, NB * ty:NB * ty + NB, :], a_free.get(n - 3))
        for k in ks:
            for a, part in enumerate((hh[step % 2], hl[step % 2])):
                a_free[n] = pe(lambda p, k=k, part=part, a=a: p.matmul(
                    PS[:, n % 2, 0:wd], part[:, k, :], ab[:, k, 0:wd],
                    start=(k == 0 and a == 0), stop=(k == NB - 1 and a == 1), skip_group_check=True),
                    t_ab[n] if k == ks[0] else None, u_ev.get(n - 2, e_a[n_h - 1]) if k == 0 else None,
                    t_blk.get((step, k // 4)) if a == 0 and (k % 4 == 0 or k == ks[0]) else None)

    def close(step, j, ty):
        n = 4 * (NT * step + j) + ty
        wd = tile_w(j)

        def rest3():
            ab = Ab[(n + 2) % 3]
            ta = sp("ab", ab[:, :, 0:wd], AT2[j][:, NB * ty:NB * ty + NB, :])
            for k in range(NB):
                for part in (hh[step % 2], hl[step % 2]):
                    pe(lambda p, k=k, part=part: p.matmul(
                        PS[:, n % 2, 0:wd], part[:, k, :], ab[:, k, 0:wd],
                        start=False, stop=True, skip_group_check=True), ta)

        P.general(rest3)
        u_ev[n] = act(lambda s: s.mul(ub[n % 2][:, 0:wd], PS[:, n % 2, 0:wd], 1.0 / SC),
                      a_free[n], w_ev.get(n - 2))

    def weigh(step, j, ty):
        n = 4 * (NT * step + j) + ty
        wd = tile_w(j)
        w_ev[n] = pe(lambda p: p.matmul(PS[:, 2, 0:wd], weT[:, ty, :], ub[n % 2][:, 0:wd],
                                        start=(ty == 0), stop=(ty == 3)),
                     u_ev[n], gru.get("a", t_fin) if ty == 0 else None)

    def fold_bias():
        e = {}
        for j in range(NT):
            wd = tile_w(j)
            cs = slice(512 * j, 512 * j + wd)
            t = pe(lambda p, j=j, cs=cs, wd=wd: p.matmul(PS[:, 4 + j % 3, 0:wd], bet[:], cnt[:, cs],
                                                         start=True, stop=True), t_cnt, t_fin, e.get(j - 3))
            e[j] = gru["b"] = act(lambda s, j=j, cs=cs, wd=wd: s.copy(fb[:, cs], PS[:, 4 + j % 3, 0:wd]),
                                  t, e_2[2], e_2[3])

    def gates_in(step, j):
        wd = tile_w(j)
        cs = slice(512 * j, 512 * j + wd)
        n = 4 * (NT * step + j) + 3
        gru["a"] = dve(lambda v: v.tensor_tensor(aT[:, 0:wd], PS[:, 2, 0:wd], fb[:, cs], ALU.add),
                       w_ev[n], gru["b"], gru.get("gi"))

    def gates(step, j):
        wd = tile_w(j)
        cs = slice(512 * j, 512 * j + wd)
        cur, nxt = hN[step % 2], hN[1 - step % 2]
        t_rz = []
        for i in range(2):
            pe(lambda p, i=i: p.matmul(PS[:, 3 + i, 0:wd], wgT[:, 1, i, :], cur[:, cs], start=True, stop=False),
               gru.get("g", t_fin), t_blk[0, j] if step == 0 else None)
            t_rz.append(pe(lambda p, i=i: p.matmul(PS[:, 3 + i, 0:wd], wgT[:, 0, i, :], aT[:, 0:wd],
                                                   start=False, stop=True), gru["a"]))
        t_hn = pe(lambda p: p.matmul(PS[:, 6, 0:wd], wgT[:, 1, 2, :], cur[:, cs], start=True, stop=True))
        t_in = pe(lambda p: p.matmul(PS[:, 5, 0:wd], wgT[:, 0, 2, :], aT[:, 0:wd], start=True, stop=True))
        gru["gi"] = t_in
        t_r = act(lambda s: s.activation(rg[:, 0:wd], PS[:, 3, 0:wd], ACT.Sigmoid, bias=brz[:, 0:1]), t_rz[0])
        t_z = act(lambda s: s.activation(zg[:, 0:wd], PS[:, 4, 0:wd], ACT.Sigmoid, bias=brz[:, 1:2]),
                  t_rz[1], gru.get("h"))
        t = dve(lambda v: v.scalar_tensor_tensor(out=hnb[:, 0:wd], in0=PS[:, 6, 0:wd], scalar=bi[:, 1, 2:3],
                                                 in1=rg[:, 0:wd], op0=ALU.add, op1=ALU.mult), t_hn, t_r)
        t = dve(lambda v: v.tensor_tensor(hnb[:, 0:wd], PS[:, 5, 0:wd], hnb[:, 0:wd], ALU.add), t, t_in)
        gru["g"] = [t, t_z]
        t_n = act(lambda s: s.activation(ng[:, 0:wd], hnb[:, 0:wd], ACT.Tanh, bias=bi[:, 0, 2:3]), t, gru.get("h"))
        t = dve(lambda v: v.tensor_tensor(dd[:, 0:wd], cur[:, cs], ng[:, 0:wd], ALU.subtract), t_n)
        t = dve(lambda v: v.tensor_tensor(dd[:, 0:wd], dd[:, 0:wd], zg[:, 0:wd], ALU.mult), t, t_z)
        gru["h"] = dve(lambda v: v.tensor_tensor(nxt[:, cs], dd[:, 0:wd], ng[:, 0:wd], ALU.add), t)

    def turn(step, j):
        nxt = hN[1 - step % 2]
        nh, nl = hh[1 - step % 2], hl[1 - step % 2]
        wd = tile_w(j)
        nb = wd // 128
        for d in range(nb):
            t1 = pe(lambda p, d=d: p.transpose(PS[:, 7, 128 * d:128 * d + 128],
                                               nxt[:, 512 * j + 128 * d:512 * j + 128 * d + 128], ident[:]),
                    gru["h"], gru.get("tr"))
        psv = PS[:, 7, 0:wd].rearrange("p (k c) -> p k c", c=128)
        ks = slice(4 * j, 4 * j + nb)
        if step < 3:
            t2 = act(lambda s: s.mul(nh[:, ks, :], psv, SC), t1)
            t3 = dve(lambda v: v.scalar_tensor_tensor(out=nl[:, ks, :], in0=psv, scalar=SC, in1=nh[:, ks, :],
                                                      op0=ALU.mult, op1=ALU.subtract), t2)
        else:
            t3 = dve(lambda v: v.tensor_tensor(xr[:, ks, :], xr[:, ks, :], psv, ALU.add), t1)
            t = apply(0, xr, j, stats(0, xr, j, t3))
            n0 = 512 * j
            if j < NT - 1:
                P.dma("pool", "out", out[n0:n0 + wd, :].rearrange("(b p) d -> p b d", p=128), xr[:, ks, :], t)
            else:
                P.dma("pool", "out", out[n0:N, :], xr[0:N - n0, NB - 1, :], t)
        gru["tr"] = t_blk[step + 1, j] = t3

    every = list(range(NB))
    before = None
    for step in range(4):
        for j in range(NT):
            if before and j == 0:
                accum(step, 0, 0, every[0:6])
                weigh(*before, 3)
                gates_in(*before)
                accum(step, 0, 0, every[6:12])
                gates(*before)
                accum(step, 0, 0, every[12:24])
                turn(*before)
                accum(step, 0, 1, every[0:24])
                accum(step, 0, 0, every[24:])
                close(step, 0, 0)
                accum(step, 0, 1, every[24:])
                close(step, 0, 1)
                weigh(step, 0, 0)
            else:
                accum(step, j, 0, every)
                close(step, j, 0)
                if not before:
                    fold_bias()
                if before:
                    weigh(*before, 3)
                    gates_in(*before)
                accum(step, j, 1, every)
                close(step, j, 1)
                weigh(step, j, 0)
                if before:
                    gates(*before)
            accum(step, j, 2, every)
            close(step, j, 2)
            weigh(step, j, 1)
            if before and j:
                turn(*before)
            accum(step, j, 3, every)
            close(step, j, 3)
            weigh(step, j, 2)
            before = (step, j)
    weigh(*before, 3)
    gates_in(*before)
    gates(*before)
    turn(*before)
    P.wait("sp", P.token("out"))
    pd.close()

    block = ctx.enter_context(nc.Block())

    @block.sync
    def _(eng):
        P.emit("sp", eng)

    @block.gpsimd
    def _(eng):
        P.emit("pool", eng)

    @block.scalar
    def _(eng):
        P.emit("act", eng)

    @block.vector
    def _(eng):
        P.emit("dve", eng)

    @block.tensor
    def _(eng):
        P.emit("pe", eng)

    ctx.close()


_INS = ["x", "src", "dst", "bnd", "edge_attr_4", "edge_weight",
        "L0_gnn_W1", "L0_gnn_as1", "L0_gnn_ad1", "L0_gnn_b1", "L0_gnn_W2", "L0_gnn_as2", "L0_gnn_ad2", "L0_gnn_b2",
        "L0_gnn_W3", "L0_gnn_as3", "L0_gnn_ad3", "L0_gnn_b3",
        "L1_gnn_w1", "L1_gnn_b1", "L1_gnn_w2", "L1_gnn_b2", "L1_gnn_gamma", "L1_gnn_beta",
        "L2_gnn_Wk", "L2_gnn_bk", "L2_gnn_bias",
        "L3_gnn_W_edge", "L3_gnn_b_edge", "L3_gnn_W_ih", "L3_gnn_W_hh", "L3_gnn_b_ih", "L3_gnn_b_hh"]


def lay_out(inputs):
    import numpy as np

    a = {k: np.ascontiguousarray(v) for k, v in inputs.items()}

    def pad(v, fill):
        o = np.full((EP,) + v.shape[1:], fill, v.dtype)
        o[:E] = v
        return o

    a["src"] = pad(a["src"], 0)
    a["dst"] = pad(a["dst"], 4000)
    a["edge_attr_4"] = pad(a["edge_attr_4"], 0)
    a["edge_weight"] = pad(a["edge_weight"], 0)
    for name in ("L1_gnn_b1", "L3_gnn_b_ih", "L3_gnn_b_hh"):
        a[name] = np.ascontiguousarray(a[name].reshape(-1, 128).T)
    a["bnd"] = np.ascontiguousarray(a["dst"][::128])
    a["dst"] = np.concatenate([a["dst"], np.full(128, 4000, a["dst"].dtype)])
    return a


def kernel(**inputs):
    import concourse.bacc as _bacc
    from concourse.bass_utils import run_bass_kernel_spmd as _run

    nc = _bacc.Bacc("TRN2", target_bir_lowering=False, num_devices=1)
    a = lay_out(inputs)
    arrays, args = {}, []
    for name in _INS:
        arrays[f"in_{name}"] = a[name]
        args.append(nc.dram_tensor(f"in_{name}", a[name].shape, mybir.dt.from_np(a[name].dtype),
                                   kind="ExternalInput").ap())
    args.append(nc.dram_tensor("out_0", (N, D), F32, kind="ExternalOutput").ap())
    gnn_kernel(nc, *args)
    r = _run(nc, [arrays], core_ids=[0])
    return r.results[0]["out_0"]
```
